# Optimizing a Trainium2 kernel written in Bass

```python
import numpy as np
import jax
import jax.numpy as jnp

def _softmax(x, axis=-1):
    return jax.nn.softmax(x, axis=axis)
def _gelu(x):
    return jax.nn.gelu(x, approximate=True)
def _silu(x):
    return jax.nn.silu(x)
def _sigmoid(x):
    return jax.nn.sigmoid(x)
def _layernorm(x, axis=-1, eps=1e-5):
    m = jnp.mean(x, axis=axis, keepdims=True)
    v = jnp.var(x, axis=axis, keepdims=True)
    return (x - m) / jnp.sqrt(v + eps)
def _scatter_add(tgt, idx, src, axis=0):
    return tgt.at[idx].add(src)
def _segment_sum(src, seg, n):
    return jax.ops.segment_sum(src, seg, n)

kernel_name = 'mk_conv_preact_d4_conv_nchw48_1a3fe1'

def setup_inputs(seed: int = 0):
    np.random.seed(seed)
    _w = jnp.asarray
    def _rec_inputs():
        import jax
        import jax.numpy as jnp
        _gk = jax.random.key(seed)
        x = -0.0004039 + 1 * jax.random.normal(jax.random.fold_in(_gk, 1), (4, 48, 256, 256), jnp.float32)
        return x
    x = _rec_inputs()
    def _L0_conv_setup():
        import jax, jax.numpy as jnp
        import numpy as np
        from jax import lax
        NUM_HEADS = 1
        DN = ('NCHW', 'OIHW', 'NCHW')
        EPS = 1e-12

        def _l2_normalize(t):
            n = jnp.sqrt(jnp.sum(t * t, axis=-1, keepdims=True))
            return t / jnp.maximum(n, EPS)
        key = jax.random.key(seed)
        k0, k1, k2, k3 = jax.random.split(key, 4)
        b, c, h, w = (4, 48, 256, 256)
        x = jax.random.normal(k0, (b, c, h, w), dtype=jnp.float32)
        qkv_w = jax.random.normal(k1, (3 * c, c, 1, 1), dtype=jnp.float32) * 0.05
        dw_w = jax.random.normal(k2, (3 * c, 1, 3, 3), dtype=jnp.float32) * 0.05
        proj_w = jax.random.normal(k3, (c, c, 1, 1), dtype=jnp.float32) * 0.05
        temperature = jnp.ones((NUM_HEADS, 1, 1), dtype=jnp.float32)
        return {'x': x, 'qkv_w': qkv_w, 'dw_w': dw_w, 'proj_w': proj_w, 'temperature': temperature}
    _L0_conv_all = _L0_conv_setup()
    _L0_conv_in = {k: v for k, v in _L0_conv_all.items() if k in ('qkv_w', 'dw_w', 'proj_w', 'temperature', )}
    del _L0_conv_all

    def _L1_conv_setup():
        import jax, jax.numpy as jnp
        import numpy as np
        B, C, H, W = (32, 48, 64, 128)
        K = 5

        def _conv1d(x, w, b):
            y = jax.lax.conv_general_dilated(x, w, window_strides=(1,), padding=[(2, 2)], dimension_numbers=('NCH', 'OIH', 'NCH'))
            return y + b[None, :, None]
        key = jax.random.key(seed)
        ks = jax.random.split(key, 7)
        s = 0.02
        return {'x': jax.random.normal(ks[0], (B, C, H, W), dtype=jnp.float32), 'down_w': jax.random.normal(ks[1], (C, C, K), dtype=jnp.float32) * s, 'down_b': jax.random.normal(ks[2], (C,), dtype=jnp.float32) * s, 'right_w': jax.random.normal(ks[3], (C, C, K), dtype=jnp.float32) * s, 'right_b': jax.random.normal(ks[4], (C,), dtype=jnp.float32) * s, 'left_w': jax.random.normal(ks[5], (C, C, K), dtype=jnp.float32) * s, 'left_b': jax.random.normal(ks[6], (C,), dtype=jnp.float32) * s}
    _L1_conv_all = _L1_conv_setup()
    _L1_conv_in = {k: v for k, v in _L1_conv_all.items() if k in ('down_w', 'down_b', 'right_w', 'right_b', 'left_w', 'left_b', )}
    del _L1_conv_all

    def _L2_conv_setup():
        import jax, jax.numpy as jnp
        import numpy as np
        B, C, H, W = (32, 48, 64, 128)
        K = 5

        def _conv1d(x, w, b):
            y = jax.lax.conv_general_dilated(x, w, window_strides=(1,), padding=[(2, 2)], dimension_numbers=('NCH', 'OIH', 'NCH'))
            return y + b[None, :, None]
        key = jax.random.key(seed)
        ks = jax.random.split(key, 7)
        s = 0.02
        return {'x': jax.random.normal(ks[0], (B, C, H, W), dtype=jnp.float32), 'down_w': jax.random.normal(ks[1], (C, C, K), dtype=jnp.float32) * s, 'down_b': jax.random.normal(ks[2], (C,), dtype=jnp.float32) * s, 'right_w': jax.random.normal(ks[3], (C, C, K), dtype=jnp.float32) * s, 'right_b': jax.random.normal(ks[4], (C,), dtype=jnp.float32) * s, 'left_w': jax.random.normal(ks[5], (C, C, K), dtype=jnp.float32) * s, 'left_b': jax.random.normal(ks[6], (C,), dtype=jnp.float32) * s}
    _L2_conv_all = _L2_conv_setup()
    _L2_conv_in = {k: v for k, v in _L2_conv_all.items() if k in ('down_w', 'down_b', 'right_w', 'right_b', 'left_w', 'left_b', )}
    del _L2_conv_all

    def _L3_conv_setup():
        import jax, jax.numpy as jnp
        import numpy as np
        B, C, H, W = (4, 48, 256, 256)
        HID = 96
        P = 8

        def _edffn(x, w_in, w_dw, fft_w, w_out):
            h = jnp.einsum('bchw,oc->bohw', x, w_in)
            h = jax.lax.conv_general_dilated(h, w_dw, window_strides=(1, 1), padding='SAME', feature_group_count=2 * HID, dimension_numbers=('NCHW', 'OIHW', 'NCHW'))
            x1, x2 = jnp.split(h, 2, axis=1)
            h = jax.nn.gelu(x1, approximate=False) * x2
            y = jnp.einsum('bchw,oc->bohw', h, w_out)
            b, c, hh, ww = y.shape
            hn, wn = (-hh % P, -ww % P)
            if hn or wn:
                y = jnp.pad(y, ((0, 0), (0, 0), (0, hn), (0, wn)), mode='reflect')
            Hp, Wp = (hh + hn, ww + wn)
            yp = y.reshape(b, c, Hp // P, P, Wp // P, P).transpose(0, 1, 2, 4, 3, 5)
            f = jnp.fft.rfft2(yp.astype(jnp.float32)) * fft_w
            yp = jnp.fft.irfft2(f, s=(P, P))
            y = yp.transpose(0, 1, 2, 4, 3, 5).reshape(b, c, Hp, Wp)
            return y[:, :, :hh, :ww]
        key = jax.random.key(seed)
        k0, k1, k2, k3, k4 = jax.random.split(key, 5)
        x = jax.random.normal(k0, (B, C, H, W), jnp.float32)
        w_in = jax.random.normal(k1, (2 * HID, C), jnp.float32) * 0.05
        w_dw = jax.random.normal(k2, (2 * HID, 1, 3, 3), jnp.float32) * 0.1
        fft_w = 1.0 + 0.1 * jax.random.normal(k3, (C, 1, 1, P, P // 2 + 1), jnp.float32)
        w_out = jax.random.normal(k4, (C, HID), jnp.float32) * 0.05
        return {'x': x, 'w_in': w_in, 'w_dw': w_dw, 'fft_w': fft_w, 'w_out': w_out}
    _L3_conv_all = _L3_conv_setup()
    _L3_conv_in = {k: v for k, v in _L3_conv_all.items() if k in ('w_in', 'w_dw', 'fft_w', 'w_out', )}
    del _L3_conv_all

    return {
        "x": x,
        "L0_conv_qkv_w": _L0_conv_in["qkv_w"],
        "L0_conv_dw_w": _L0_conv_in["dw_w"],
        "L0_conv_proj_w": _L0_conv_in["proj_w"],
        "L0_conv_temperature": _L0_conv_in["temperature"],
        "L1_conv_down_w": _L1_conv_in["down_w"],
        "L1_conv_down_b": _L1_conv_in["down_b"],
        "L1_conv_right_w": _L1_conv_in["right_w"],
        "L1_conv_right_b": _L1_conv_in["right_b"],
        "L1_conv_left_w": _L1_conv_in["left_w"],
        "L1_conv_left_b": _L1_conv_in["left_b"],
        "L2_conv_down_w": _L2_conv_in["down_w"],
        "L2_conv_down_b": _L2_conv_in["down_b"],
        "L2_conv_right_w": _L2_conv_in["right_w"],
        "L2_conv_right_b": _L2_conv_in["right_b"],
        "L2_conv_left_w": _L2_conv_in["left_w"],
        "L2_conv_left_b": _L2_conv_in["left_b"],
        "L3_conv_w_in": _L3_conv_in["w_in"],
        "L3_conv_w_dw": _L3_conv_in["w_dw"],
        "L3_conv_fft_w": _L3_conv_in["fft_w"],
        "L3_conv_w_out": _L3_conv_in["w_out"],
    }

def reference(x, L0_conv_qkv_w, L0_conv_dw_w, L0_conv_proj_w, L0_conv_temperature, L1_conv_down_w, L1_conv_down_b, L1_conv_right_w, L1_conv_right_b, L1_conv_left_w, L1_conv_left_b, L2_conv_down_w, L2_conv_down_b, L2_conv_right_w, L2_conv_right_b, L2_conv_left_w, L2_conv_left_b, L3_conv_w_in, L3_conv_w_dw, L3_conv_fft_w, L3_conv_w_out):
    import jax
    import jax.numpy as jnp
    def _L0_conv_ref(x, qkv_w, dw_w, proj_w, temperature):
        import jax, jax.numpy as jnp
        import numpy as np
        from jax import lax
        NUM_HEADS = 1
        DN = ('NCHW', 'OIHW', 'NCHW')
        EPS = 1e-12

        def _l2_normalize(t):
            n = jnp.sqrt(jnp.sum(t * t, axis=-1, keepdims=True))
            return t / jnp.maximum(n, EPS)
        b, c, h, w = x.shape
        heads = NUM_HEADS
        qkv = lax.conv_general_dilated(x, qkv_w, (1, 1), 'VALID', dimension_numbers=DN)
        qkv = lax.conv_general_dilated(qkv, dw_w, (1, 1), ((1, 1), (1, 1)), feature_group_count=3 * c, dimension_numbers=DN)
        q, k, v = jnp.split(qkv, 3, axis=1)
        q = q.reshape(b, heads, c // heads, h * w)
        k = k.reshape(b, heads, c // heads, h * w)
        v = v.reshape(b, heads, c // heads, h * w)
        q = _l2_normalize(q)
        k = _l2_normalize(k)
        attn = jax.nn.softmax(jnp.einsum('bhcn,bhdn->bhcd', q, k) * temperature, axis=-1)
        out = jnp.einsum('bhcd,bhdn->bhcn', attn, v).reshape(b, c, h, w)
        return lax.conv_general_dilated(out, proj_w, (1, 1), 'VALID', dimension_numbers=DN)

    def _L1_conv_ref(x, down_w, down_b, right_w, right_b, left_w, left_b):
        import jax, jax.numpy as jnp
        import numpy as np
        B, C, H, W = (32, 48, 64, 128)
        K = 5

        def _conv1d(x, w, b):
            y = jax.lax.conv_general_dilated(x, w, window_strides=(1,), padding=[(2, 2)], dimension_numbers=('NCH', 'OIH', 'NCH'))
            return y + b[None, :, None]
        Bb, Cc, Hh, Ww = x.shape

        def step(w, b):

            def f(carry, inp):
                nxt = inp + _conv1d(carry, w, b)
                return (nxt, nxt)
            return f
        xs = jnp.moveaxis(x, 2, 0)
        d0 = xs[0]
        _, d_rest = jax.lax.scan(step(down_w, down_b), d0, xs[1:])
        D = jnp.concatenate([d0[None], d_rest], 0)
        seq = jnp.concatenate([D[Hh - 3::-1], D[Hh - 1:Hh]], 0)
        u0 = D[Hh - 1]
        _, u_rest = jax.lax.scan(step(down_w, down_b), u0, seq)
        U = jnp.concatenate([u0[None], u_rest], 0)[::-1]
        ws = jnp.moveaxis(jnp.moveaxis(U, 0, 2), 3, 0)
        r0 = ws[0]
        _, r_rest = jax.lax.scan(step(right_w, right_b), r0, ws[1:])
        R = jnp.concatenate([r0[None], r_rest], 0)
        l0 = R[Ww - 1]
        _, l_rest = jax.lax.scan(step(left_w, left_b), l0, R[Ww - 2::-1])
        L = jnp.concatenate([l0[None], l_rest], 0)[::-1]
        return jnp.moveaxis(L, 0, 3)

    def _L2_conv_ref(x, down_w, down_b, right_w, right_b, left_w, left_b):
        import jax, jax.numpy as jnp
        import numpy as np
        B, C, H, W = (32, 48, 64, 128)
        K = 5

        def _conv1d(x, w, b):
            y = jax.lax.conv_general_dilated(x, w, window_strides=(1,), padding=[(2, 2)], dimension_numbers=('NCH', 'OIH', 'NCH'))
            return y + b[None, :, None]
        Bb, Cc, Hh, Ww = x.shape

        def step(w, b):

            def f(carry, inp):
                nxt = inp + _conv1d(carry, w, b)
                return (nxt, nxt)
            return f
        xs = jnp.moveaxis(x, 2, 0)
        d0 = xs[0]
        _, d_rest = jax.lax.scan(step(down_w, down_b), d0, xs[1:])
        D = jnp.concatenate([d0[None], d_rest], 0)
        seq = jnp.concatenate([D[Hh - 3::-1], D[Hh - 1:Hh]], 0)
        u0 = D[Hh - 1]
        _, u_rest = jax.lax.scan(step(down_w, down_b), u0, seq)
        U = jnp.concatenate([u0[None], u_rest], 0)[::-1]
        ws = jnp.moveaxis(jnp.moveaxis(U, 0, 2), 3, 0)
        r0 = ws[0]
        _, r_rest = jax.lax.scan(step(right_w, right_b), r0, ws[1:])
        R = jnp.concatenate([r0[None], r_rest], 0)
        l0 = R[Ww - 1]
        _, l_rest = jax.lax.scan(step(left_w, left_b), l0, R[Ww - 2::-1])
        L = jnp.concatenate([l0[None], l_rest], 0)[::-1]
        return jnp.moveaxis(L, 0, 3)

    def _L3_conv_ref(x, w_in, w_dw, fft_w, w_out):
        import jax, jax.numpy as jnp
        import numpy as np
        B, C, H, W = (4, 48, 256, 256)
        HID = 96
        P = 8

        def _edffn(x, w_in, w_dw, fft_w, w_out):
            h = jnp.einsum('bchw,oc->bohw', x, w_in)
            h = jax.lax.conv_general_dilated(h, w_dw, window_strides=(1, 1), padding='SAME', feature_group_count=2 * HID, dimension_numbers=('NCHW', 'OIHW', 'NCHW'))
            x1, x2 = jnp.split(h, 2, axis=1)
            h = jax.nn.gelu(x1, approximate=False) * x2
            y = jnp.einsum('bchw,oc->bohw', h, w_out)
            b, c, hh, ww = y.shape
            hn, wn = (-hh % P, -ww % P)
            if hn or wn:
                y = jnp.pad(y, ((0, 0), (0, 0), (0, hn), (0, wn)), mode='reflect')
            Hp, Wp = (hh + hn, ww + wn)
            yp = y.reshape(b, c, Hp // P, P, Wp // P, P).transpose(0, 1, 2, 4, 3, 5)
            f = jnp.fft.rfft2(yp.astype(jnp.float32)) * fft_w
            yp = jnp.fft.irfft2(f, s=(P, P))
            y = yp.transpose(0, 1, 2, 4, 3, 5).reshape(b, c, Hp, Wp)
            return y[:, :, :hh, :ww]
        return _edffn(x, w_in, w_dw, fft_w, w_out)

    def _gn(v, G=16, eps=1e-5):
        B_, C_, H_, W_ = v.shape
        g = v.reshape(B_, G, C_ // G, H_, W_)
        m = jnp.mean(g, axis=(2, 3, 4), keepdims=True)
        s = jnp.var(g, axis=(2, 3, 4), keepdims=True)
        return ((g - m) / jnp.sqrt(s + eps)).reshape(v.shape)

    def _ln_c(v, eps=1e-6):
        m = jnp.mean(v, axis=1, keepdims=True)
        s = jnp.var(v, axis=1, keepdims=True)
        return (v - m) / jnp.sqrt(s + eps)

    def _ln_t(v, eps=1e-5):
        m = jnp.mean(v, axis=-1, keepdims=True)
        s = jnp.var(v, axis=-1, keepdims=True)
        return (v - m) / jnp.sqrt(s + eps)

    def _to_tokens(v):
        B_, C_, H_, W_ = v.shape
        return v.reshape(B_, C_, H_ * W_).transpose(0, 2, 1)
    def _from_tokens(t, like):
        B_, C_, H_, W_ = like.shape
        return t.transpose(0, 2, 1).reshape(B_, C_, H_, W_)

    x = x + _L0_conv_ref(_gn(x), L0_conv_qkv_w, L0_conv_dw_w, L0_conv_proj_w, L0_conv_temperature)
    x = x + _L1_conv_ref(_gn(x), L1_conv_down_w, L1_conv_down_b, L1_conv_right_w, L1_conv_right_b, L1_conv_left_w, L1_conv_left_b)
    x = x + _L2_conv_ref(_gn(x), L2_conv_down_w, L2_conv_down_b, L2_conv_right_w, L2_conv_right_b, L2_conv_left_w, L2_conv_left_b)
    x = x + _L3_conv_ref(_gn(x), L3_conv_w_in, L3_conv_w_dw, L3_conv_fft_w, L3_conv_w_out)
    return x


_drawn_inputs = setup_inputs


def setup_inputs(seed=0):
    import zlib

    import numpy as np

    out = dict(_drawn_inputs(seed))
    spreads = {}
    factors = {'L0_conv_qkv_w': 8.0,
     'L0_conv_dw_w': 8.0,
     'L0_conv_proj_w': 8.0,
     'L1_conv_right_b': 4.586,
     'L1_conv_left_b': 4.056,
     'L2_conv_down_b': 3.943,
     'L2_conv_right_b': 7.209,
     'L2_conv_left_b': 5.983,
     'L3_conv_w_in': 8.0,
     'L3_conv_w_dw': 8.0,
     'L3_conv_fft_w': 8.0,
     'L3_conv_w_out': 8.0}
    for name, (base, spread) in spreads.items():
        noise = np.random.default_rng([zlib.crc32(name.encode()), seed]).standard_normal(out[name].shape)
        drawn = base * np.exp(spread * noise) if base else spread * noise
        out[name] = jnp.asarray(drawn.astype(out[name].dtype))
    for name, factor in factors.items():
        out[name] = (out[name] * factor).astype(out[name].dtype)
    return out
```

```python
from contextlib import ExitStack

import numpy as np

import concourse.bass as bass
from concourse import mybir

F32 = mybir.dt.float32
ACT = mybir.ActivationFunctionType
ALU = mybir.AluOpType
AX_X = mybir.AxisListType.X

B, C, H, W = 4, 48, 256, 256
C2 = 2 * C
BLK = 16
NB = H // BLK
HALF = BLK // 2
SUB = HALF * HALF
TILE = NB * 4 * B * SUB // 2
PAIRS = W // 2
PITCH = PAIRS + 2
GROUPS = 16
GN_EPS = 1e-5
L2_EPS = 1e-12
HID = 96
NSTAT = 4 * NB


class Phase:

    def __init__(self, nc, name):
        self.nc, self.name, self.ctx = nc, f"{name}{nc.next_id()}", ExitStack()
        self.sems = []

    def __enter__(self):
        self.ctx.__enter__()
        return self

    def __exit__(self, *a):
        self.ctx.__exit__(*a)
        if self.sems and a[0] is None:
            self.nc.clear_and_free_semaphores(self.sems)
            self.nc.all_engine_barrier()

    def sb(self, name, shape):
        return self.ctx.enter_context(self.nc.sbuf_tensor(f"{self.name}_{name}", shape, F32))

    def ps(self, name, shape=(128, 512)):
        return self.ctx.enter_context(self.nc.psum_tensor(f"{self.name}_{name}", list(shape), F32))

    def sem(self, name):
        self.sems.append(self.nc.alloc_semaphore(f"{self.name}_{name}"))
        return self.sems[-1]

    def block(self):
        self.passed = self.sem("passed")
        return self.ctx.enter_context(self.nc.Block())

    def hold(self, eng, sem, value):
        eng.wait_ge(sem, value)
        eng.sem_inc(self.passed, 1)


def row_block(t, hb):
    return t[hb].rearrange("wb hp wp c b s -> (wp c) (wb hp) (b s)")


def col_block(t, wb, hp, wp):
    return t[:, wb, hp, wp].rearrange("hb c b s -> c hb (b s)")


def step_view(tile, axis, r, b0, nb):
    v = tile.rearrange("p (k q b i j) -> p k q b i j", k=NB, q=2, b=B, i=HALF)
    v = v[:, :, r % 2, b0:b0 + nb]
    v = v[:, :, :, r // 2, :] if axis == "h" else v[:, :, :, :, r // 2]
    return v.rearrange("p k b j -> p b k j")




def stats_phase(nc, src, stats):
    with Phase(nc, "st") as ph:
        tiles = [ph.sb(f"tile{k}", [C2, TILE]) for k in range(2)]
        loaded = [ph.sem(f"loaded{k}") for k in range(2)]
        used = ph.sem("used")
        block = ph.block()

        @block.sync
        def _(sp):
            for k in range(2):
                sp.dma_start(tiles[k][:, :].rearrange("p (k s) -> p k s", s=B * SUB),
                             row_block(src, k)).then_inc(loaded[k], 16)
            with sp.Fori(1, NB // 2) as i:
                for k in range(2):
                    ph.hold(sp, used, 2 * i + k - 1)
                    sp.dma_start(tiles[k][:, :].rearrange("p (k s) -> p k s", s=B * SUB),
                                 row_block(src, 2 * i + k)).then_inc(loaded[k], 16)

        @block.vector
        def _(dve):
            with dve.Fori(0, NB // 2) as i:
                for k in range(2):
                    dve.wait_ge(loaded[k], 16 * i + 16)
                    for n in range(4 * B):
                        b, part = n // 4, n % 4
                        ins = stats_of(nc, tiles[k], stats, b, part, 2 * i + k)
                    ins.then_inc(used, 1)


def stats_of(nc, tile, stats, b, part, n):
    v = tile[:, :].rearrange("p (k b s) -> p k b s", b=B, s=SUB)
    per = 2 * NB // 4
    return nc.vector.bn_stats(stats[:, b, bass.ds(n * 4 + part, 1), :].rearrange("p a s -> p (a s)"),
                              v[:, part * per:(part + 1) * per, b, :])


def norm_phase(nc, stats, group_avg, scale, shift):
    with Phase(nc, "gn") as ph:
        mv = ph.sb("mv", [C2, B, 2])
        dev = ph.sb("dev", [C2, B])
        dev2 = ph.sb("dev2", [C2, B])
        spread = ph.sb("spread", [C2, B])
        eps = ph.sb("eps", [C2, 1])
        std = ph.sb("std", [C2, B])
        mean = ph.sb("mean", [C2, B])
        pm, pv = ph.ps("pm"), ph.ps("pv")
        vec = ph.sem("vec")
        summed = ph.sem("summed")
        rooted = ph.sem("rooted")
        block = ph.block()

        @block.vector
        def _(dve):
            nc.vector.memset(eps[:, :], GN_EPS).then_inc(vec, 1)
            for b in range(B):
                nc.vector.bn_aggr(mv[:, b, :], stats[:, b, :, :].rearrange("p n s -> p (n s)")).then_inc(vec, 1)
            dve.wait_ge(summed, 1)
            nc.vector.tensor_copy(mean[:, :], pm[0:C2, 0:B]).then_inc(vec, 1)
            dve.wait_ge(vec, 6)
            nc.vector.tensor_tensor(dev[:, :], mv[:, :, 0], mean[:, :], ALU.subtract).then_inc(vec, 1)
            dve.wait_ge(vec, 7)
            nc.vector.tensor_tensor(dev2[:, :], dev[:, :], dev[:, :], ALU.mult).then_inc(vec, 1)
            dve.wait_ge(vec, 8)
            nc.vector.tensor_tensor(spread[:, :], dev2[:, :], mv[:, :, 1], ALU.add).then_inc(vec, 1)
            dve.wait_ge(rooted, 1)
            nc.vector.reciprocal(scale[:, :], std[:, :]).then_inc(vec, 1)
            dve.wait_ge(vec, 10)
            nc.vector.scalar_tensor_tensor(out=shift[:, :], in0=mean[:, :], scalar=-1.0, in1=scale[:, :],
                                           op0=ALU.mult, op1=ALU.mult).then_inc(vec, 1)

        @block.tensor
        def _(pe):
            pe.wait_ge(vec, 5)
            nc.tensor.matmul(pm[0:C2, 0:B], group_avg[:, :], mv[:, :, 0], start=True, stop=True).then_inc(summed, 1)
            pe.wait_ge(vec, 9)
            nc.tensor.matmul(pv[0:C2, 0:B], group_avg[:, :], spread[:, :], start=True, stop=True).then_inc(summed, 1)

        @block.scalar
        def _(act):
            act.wait_ge(summed, 2)
            nc.scalar.activation(std[:, :], pv[0:C2, 0:B], ACT.Sqrt, bias=eps[:, :]).then_inc(rooted, 1)




def forward_sweep(nc, name, src, axis, taps_dram, dst, norm=None):
    shifted = 1 if norm is not None else 0
    with Phase(nc, name) as ph:
        ins = [ph.sb(f"in{k}", [C2, TILE]) for k in range(2)]
        outs = [ph.sb(f"out{k}", [C2 + 1, BLK, B, PITCH]) for k in range(2)]
        taps = ph.sb("taps", [C2 + 1, 3, C2])
        sums = [[ph.ps(f"sum{c}{k}") for k in range(2)] for c in range(2)]
        cleared = ph.sem("cleared")
        taps_in = ph.sem("taps_in")
        loaded = [ph.sem(f"loaded{k}") for k in range(2)]
        normed = ph.sem("normed")
        conved = [ph.sem(f"conved{c}") for c in range(2)]
        stepped = [ph.sem(f"stepped{c}") for c in range(2)]
        ones_set = ph.sem("ones_set")
        stored = [ph.sem(f"stored{k}") for k in range(2)]
        turned = ph.sem("turned")
        block = ph.block()

        @block.sync
        def _(sp):
            def load(n, k):
                view = ins[k][:, :].rearrange("p (k s) -> p k s", s=B * SUB)
                if axis == "h":
                    sp.dma_start(view, row_block(src, n)).then_inc(loaded[k], 64)
                else:
                    v4 = ins[k][:, :].rearrange("p (k q s) -> p k q s", q=2, s=B * SUB)
                    for hp in range(2):
                        for wp in range(2):
                            sp.dma_start(v4[hp * C:(hp + 1) * C, :, wp], col_block(src, n, hp, wp))\
                              .then_inc(loaded[k], 16)

            def store(n, k):
                for c in range(2):
                    ph.hold(sp, stepped[c], BLK * n + BLK)
                for b in range(B):
                    sp.dma_start(dst[:, bass.ds(BLK * n + shifted, BLK), b], outs[k][0:C2, :, b, 1:1 + PAIRS])\
                      .then_inc(stored[k], 16)

            sp.dma_start(taps[:, :, :], taps_dram).then_inc(taps_in, 16)
            load(0, 0)
            load(1, 1)
            with sp.Fori(0, NB // 2 - 1) as i:
                for k in range(2):
                    store(2 * i + k, k)
                    load(2 * i + k + 2, k)
            store(NB - 2, 0)
            store(NB - 1, 1)
            if shifted:
                sp.wait_ge(stored[0], 64 * (NB // 2))
                sp.wait_ge(stored[1], 64 * (NB // 2))
                for pos in (H - 1, 0):
                    sp.dma_start(dst[:, pos], outs[1][0:C2, BLK - 1, :, 1:1 + PAIRS]).then_inc(turned, 16)
                sp.wait_ge(turned, 32)
            else:
                for k in range(2):
                    sp.wait_ge(stored[k], 64 * (NB // 2))

        if norm is not None:
            scale, shift = norm

            @block.scalar
            def _(act):
                with act.Fori(0, NB // 2) as i:
                    for k in range(2):
                        act.wait_ge(loaded[k], 64 * i + 64)
                        v = ins[k][:, :].rearrange("p (k b s) -> p k b s", b=B, s=SUB)
                        for b in range(B):
                            ins_ = nc.scalar.activation(v[:, :, b], v[:, :, b], ACT.Identity, bias=shift[:, b:b + 1],
                                                        scale=scale[:, b:b + 1])
                        ins_.then_inc(normed, 1)

        @block.gpsimd
        def _(pool):
            for k in range(2):
                nc.gpsimd.memset(outs[k][0:C2, :, :, :], 0.0).then_inc(cleared, 1)
                nc.gpsimd.memset(outs[k][C2:C2 + 1, :, :, :], 1.0).then_inc(cleared, 1)
            pool.wait_ge(cleared, 4)
            nc.gpsimd.memset(outs[1][C2:C2 + 1, BLK - 1, :, :], 0.0).then_inc(cleared, 1)
            for c in range(2):
                pool.wait_ge(conved[c], 1)
            nc.gpsimd.memset(outs[1][C2:C2 + 1, BLK - 1, :, :], 1.0).then_inc(ones_set, 1)

        def conv_step(c, k, r):
            prev = outs[k][:, r - 1] if r else outs[1 - k][:, BLK - 1]
            for s in (0, 2, 1):
                kk = C2 + 1 if s == 1 else C2
                mm = nc.tensor.matmul(sums[c][r % 2][0:C2, 0:2 * PAIRS], taps[0:kk, s, :],
                                      prev[0:kk, 2 * c:2 * c + 2, s:s + PAIRS], start=(s == 0), stop=(s == 1))
            mm.then_inc(conved[c], 1)

        @block.tensor
        def _(pe):
            def body(n, first=False):
                for k in range(2):
                    for r in range(BLK):
                        for c in range(2):
                            if not (first and k == 0 and r == 0):
                                pe.wait_ge(stepped[c], BLK * (n + k) + r)
                            if first and k == 1 and r == 1 and c == 0:
                                pe.wait_ge(ones_set, 1)
                            conv_step(c, k, r)

            pe.wait_ge(cleared, 5)
            pe.wait_ge(taps_in, 16)
            body(0, first=True)
            with pe.Fori(1, NB // 2) as i:
                body(2 * i)

        @block.vector
        def _(dve):
            def body(i, first=False):
                for k in range(2):
                    n = 2 * i + k
                    if norm is not None:
                        dve.wait_ge(normed, n + 1)
                    else:
                        dve.wait_ge(loaded[k], 64 * i + 64)
                    if not first:
                        dve.wait_ge(stored[k], 64 * i)
                    for r in range(BLK):
                        for c in range(2):
                            dve.wait_ge(conved[c], BLK * n + r + 1)
                            nc.vector.tensor_tensor(
                                outs[k][0:C2, r, 2 * c:2 * c + 2, 1:1 + PAIRS].rearrange("p b (k j) -> p b k j", j=HALF),
                                sums[c][r % 2][0:C2, 0:2 * PAIRS].rearrange("p (b k j) -> p b k j", b=2, j=HALF),
                                step_view(ins[k][:, :], axis, r, 2 * c, 2), ALU.add).then_inc(stepped[c], 1)

            dve.wait_ge(cleared, 5)
            body(0, first=True)
            with dve.Fori(1, NB // 2) as i:
                body(i)


RING = 4


def backward_sweep(nc, name, src, axis, taps_dram, dst, residual=None, stats=None, patches=None):
    with Phase(nc, name) as ph:
        ins = [ph.sb(f"in{k}", [C2, BLK, B, PAIRS]) for k in range(2)]
        ring = ph.sb("ring", [C2 + 1, RING, B, PITCH])
        outs = [ph.sb(f"out{k}", [C2, TILE]) for k in range(2)]
        px = ph.sb("px", [C2, 64, 128]) if patches is not None else None
        taps = ph.sb("taps", [C2 + 1, 3, C2])
        sums = [[ph.ps(f"sum{c}{k}") for k in range(2)] for c in range(2)]
        cleared = ph.sem("cleared")
        taps_in = ph.sem("taps_in")
        loaded = [ph.sem(f"loaded{k}") for k in range(2)]
        res_in = [ph.sem(f"res_in{k}") for k in range(2)]
        conved = [ph.sem(f"conved{c}") for c in range(2)]
        stepped = [ph.sem(f"stepped{c}") for c in range(2)]
        placed = ph.sem("placed")
        measured = ph.sem("measured")
        ones_set = ph.sem("ones_set")
        stored = [ph.sem(f"stored{k}") for k in range(2)]
        px_made = ph.sem("px_made")
        px_stored = ph.sem("px_stored")
        block = ph.block()

        def out_blocks(n, k):
            if axis == "h":
                return [(row_block(dst, n), outs[k][:, :].rearrange("p (k s) -> p k s", s=B * SUB))]
            v4 = outs[k][:, :].rearrange("p (k q s) -> p k q s", q=2, s=B * SUB)
            return [(col_block(dst, n, hp, wp), v4[hp * C:(hp + 1) * C, :, wp]) for hp in range(2) for wp in range(2)]

        @block.sync
        def _(sp):
            def load_in(m, k):
                sp.dma_start(ins[k][:, :, :, :], src[:, bass.ds(BLK * (NB - 1) - BLK * m, BLK)]).then_inc(loaded[k], 16)

            def load_residual(m, k):
                v4 = outs[k][:, :].rearrange("p (k q s) -> p k q s", q=2, s=B * SUB)
                for hp in range(2):
                    for wp in range(2):
                        sp.dma_start(v4[hp * C:(hp + 1) * C, :, wp], col_block(residual, NB - 1 - m, hp, wp))\
                          .then_inc(res_in[k], 16)

            def store(i, k):
                m = 2 * i + k
                ph.hold(sp, placed, BLK * m + BLK)
                pairs = out_blocks(NB - 1 - m, k)
                for d, s in pairs:
                    sp.dma_start(d, s).then_inc(stored[k], 64 // len(pairs))
                if patches is not None:
                    ph.hold(sp, px_made, m + 1)
                    for hp in range(2):
                        sp.dma_start(patches[:, 1 - k, hp, :, :, NB // 2 - 1 - i].rearrange("c x q n -> c (x q) n"),
                                     px[hp * C:(hp + 1) * C, :, :]).then_inc(px_stored, 16)

            sp.dma_start(taps[:, :, :], taps_dram).then_inc(taps_in, 16)
            for k in range(2):
                load_in(k, k)
                if residual is not None:
                    load_residual(k, k)
            with sp.Fori(0, NB // 2 - 1) as i:
                for k in range(2):
                    store(i, k)
                    load_in(2 * i + k + 2, k)
                    if residual is not None:
                        ph.hold(sp, stored[k], 64 * i + 64)
                        ph.hold(sp, measured, 2 * i + k + 1)
                        load_residual(2 * i + k + 2, k)
            for k in range(2):
                store(NB // 2 - 1, k)
            for k in range(2):
                sp.wait_ge(stored[k], 64 * (NB // 2))
            if patches is not None:
                sp.wait_ge(px_stored, 32 * NB)

        def conv_step(c, r):
            prev = ring[:, (r - 1) % RING]
            for s in (0, 2, 1):
                kk = C2 + 1 if s == 1 else C2
                mm = nc.tensor.matmul(sums[c][r % 2][0:C2, 0:2 * PAIRS], taps[0:kk, s, :],
                                      prev[0:kk, 2 * c:2 * c + 2, s:s + PAIRS], start=(s == 0), stop=(s == 1))
            mm.then_inc(conved[c], 1)

        @block.tensor
        def _(pe):
            def body(m, first=False):
                for k in range(2):
                    for r in range(BLK):
                        for c in range(2):
                            if not (first and k == 0 and r == 0):
                                pe.wait_ge(stepped[c], BLK * (m + k) + r)
                            if first and k == 0 and r == RING and c == 0:
                                pe.wait_ge(ones_set, 1)
                            conv_step(c, r)

            pe.wait_ge(cleared, 3)
            pe.wait_ge(taps_in, 16)
            body(0, first=True)
            with pe.Fori(1, NB // 2) as i:
                body(2 * i)

        @block.vector
        def _(dve):
            def measure(k, m, n):
                ins_ = stats_of(nc, outs[k], stats, n // 4, n % 4, m)
                if n == 4 * B - 1:
                    ins_.then_inc(measured, 1)

            def body(i, first=False):
                for k in range(2):
                    m = 2 * i + k
                    dve.wait_ge(loaded[k], 16 * i + 16)
                    todo = list(range(4 * B)) if stats is not None and not (first and k == 0) else []
                    for r in range(BLK):
                        for c in range(2):
                            dve.wait_ge(conved[c], BLK * m + r + 1)
                            if c == 0 and not (first and k == 0 and r < RING):
                                dve.wait_ge(placed, BLK * m + r - RING + 1)
                            nc.vector.tensor_tensor(
                                ring[0:C2, r % RING, 2 * c:2 * c + 2, 1:1 + PAIRS],
                                sums[c][r % 2][0:C2, 0:2 * PAIRS].rearrange("p (b j) -> p b j", b=2),
                                ins[k][:, BLK - 1 - r, 2 * c:2 * c + 2, :], ALU.add).then_inc(stepped[c], 1)
                            if todo and r >= 2:
                                if len(todo) == 4 * B:
                                    dve.wait_ge(placed, BLK * m)
                                measure(1 - k, m - 1, todo.pop(0))
                    assert not todo

            dve.wait_ge(cleared, 3)
            body(0, first=True)
            with dve.Fori(1, NB // 2) as i:
                body(i)
            if stats is not None:
                dve.wait_ge(placed, BLK * NB)
                for n in range(4 * B):
                    measure(1, NB - 1, n)

        def place_body(eng, emit, i, first):
            for k in range(2):
                m = 2 * i + k
                if residual is not None:
                    eng.wait_ge(res_in[k], 64 * i + 64)
                elif not first:
                    eng.wait_ge(stored[k], 64 * i)
                for r in range(BLK):
                    for c in range(2):
                        eng.wait_ge(stepped[c], BLK * m + r + 1)
                    row = ring[0:C2, r % RING, :, 1:1 + PAIRS].rearrange("p b (k j) -> p b k j", j=HALF)
                    emit(step_view(outs[k][:, :], axis, BLK - 1 - r, 0, B), row).then_inc(placed, 1)

        @block.gpsimd
        def _(pool):
            nc.gpsimd.memset(ring[0:C2, :, :, :], 0.0).then_inc(cleared, 1)
            nc.gpsimd.memset(ring[C2:C2 + 1, :, :, :], 1.0).then_inc(cleared, 1)
            pool.wait_ge(cleared, 2)
            nc.gpsimd.memset(ring[C2:C2 + 1, RING - 1, :, :], 0.0).then_inc(cleared, 1)
            for c in range(2):
                pool.wait_ge(conved[c], 1)
            nc.gpsimd.memset(ring[C2:C2 + 1, RING - 1, :, :], 1.0).then_inc(ones_set, 1)
            if residual is not None:
                def add(o, row):
                    return nc.gpsimd.tensor_tensor(o, o, row, ALU.add)

                place_body(pool, add, 0, True)
                with pool.Fori(1, NB // 2) as i:
                    place_body(pool, add, i, False)

        @block.scalar
        def _(act):
            if residual is None:
                def copy(o, row):
                    return nc.scalar.copy(o, row)

                place_body(act, copy, 0, True)
                with act.Fori(1, NB // 2) as i:
                    place_body(act, copy, i, False)
            if patches is not None:
                def body(i, first):
                    for k in range(2):
                        m = 2 * i + k
                        act.wait_ge(placed, BLK * m + BLK)
                        if not (first and k == 0):
                            act.wait_ge(px_stored, 32 * m)
                        v = outs[k][:, :].rearrange("p (k q b e i j) -> p k q b e i j", k=NB, q=2, b=B, e=2, i=HALF // 2)
                        o = px[:, :, :].rearrange("p (i j q) (b k e) -> p q b e k i j", i=HALF // 2, q=2, b=B, e=2)
                        for q in range(2):
                            for b in range(B):
                                for e in range(2):
                                    ins_ = nc.scalar.copy(o[:, q, b, e], v[:, :, q, b, e])
                        ins_.then_inc(px_made, 1)

                body(0, True)
                with act.Fori(1, NB // 2) as i:
                    body(i, False)



SLOTS = 4
A_ROWS = BLK + 2


class RowStream:

    def __init__(self, nc, ph, src, scale, shift, per):
        self.per, self.lead = per, SLOTS * per
        self.nc, self.ph, self.src, self.scale, self.shift = nc, ph, src, scale, shift
        self.now = ph.sb("now", [C2, 2])
        self.now_set = ph.sem("now_set")
        self.raw = [ph.sb(f"raw{k}", [C2, 2 * NB * SUB]) for k in range(SLOTS)]
        self.own = [ph.sb(f"own{k}", [C2, A_ROWS, PITCH]) for k in range(SLOTS)]
        self.next_ = [ph.sb(f"next{k}", [C2, A_ROWS, PITCH]) for k in range(SLOTS)]
        self.raw_in = [ph.sem(f"raw_in{k}") for k in range(SLOTS)]
        self.cleared = ph.sem("cleared")
        self.normed = ph.sem("normed")
        self.whole = ph.sem("whole")
        self.next_in = [ph.sem(f"next_in{k}") for k in range(SLOTS)]
        self.conved = ph.sem("conved")

    def sync_batch(self, sp, b, raw_free, after_copy=None):
        def load(hb):
            k = hb % SLOTS
            d = self.raw[k][:, :].rearrange("p (k s) -> p k s", s=SUB)
            s = self.src[hb][:, :, :, :, bass.ds(b, 1)].rearrange("wb hp wp c b s -> (wp c) (wb hp) (b s)")
            sp.dma_start(d, s).then_inc(self.raw_in[k], 16)

        for hb in range(SLOTS - 1):
            load(hb)
        for hb in range(NB):
            k = hb % SLOTS
            n = A_ROWS * PITCH - 1
            self.ph.hold(sp, self.whole, NB * b + hb + 2)
            self.wait_free(sp, b, hb)
            own = self.own[k][:, :, :].rearrange("p r j -> p (r j)")
            nxt = self.next_[k][:, :, :].rearrange("p r j -> p (r j)")
            sp.dma_start(nxt[0:C, 0:n], own[0:C, 1:n + 1]).then_inc(self.next_in[k], 16)
            sp.dma_start(nxt[C:C2, 1:n + 1], own[C:C2, 0:n]).then_inc(self.next_in[k], 16)
            if after_copy is not None:
                after_copy(hb)
            if hb + SLOTS - 1 < NB:
                raw_free(hb - 1)
                load(hb + SLOTS - 1)

    def pool_clear(self, pool):
        for k in range(SLOTS):
            ins = self.nc.gpsimd.memset(self.own[k][:, :, :], 0.0)
        ins.then_inc(self.cleared, 1)
        pool.sem_inc(self.conved, self.lead)
        pool.sem_inc(self.whole, 1)
        pool.wait_ge(self.cleared, 1)

    def pool_batch(self, pool, b):
        nc = self.nc
        self.ph.hold(pool, self.whole, NB * b + 1)
        nc.gpsimd.tensor_copy(self.now[:, 0:1], self.scale[:, bass.ds(b, 1)])
        nc.gpsimd.tensor_copy(self.now[:, 1:2], self.shift[:, bass.ds(b, 1)]).then_inc(self.now_set, 1)
        self.ph.hold(pool, self.now_set, b + 1)

        def norm(out, in_):
            return nc.gpsimd.tensor_scalar(out, in_, self.now[:, 0:1], self.now[:, 1:2], ALU.mult, ALU.add)

        for hb in range(NB):
            k, before = hb % SLOTS, (hb - 1) % SLOTS
            raw = self.raw[k][:, :].rearrange("p (k q i j) -> p k q i j", k=NB, q=2, i=HALF)
            self.ph.hold(pool, self.raw_in[k], 16 * (NB // SLOTS) * b + 16 * (hb // SLOTS) + 16)
            if hb:
                norm(self.own[before][:, A_ROWS - 1, 1:1 + PAIRS].rearrange("p (k j) -> p k j", j=HALF),
                     raw[:, :, 0, 0, :]).then_inc(self.whole, 1)
            self.wait_free(pool, b, hb)
            for hp in range(2):
                rows = self.own[k][:, 1 + hp:1 + hp + BLK - 1:2, 1:1 + PAIRS]
                norm(rows.rearrange("p i (k j) -> p i k j", j=HALF), raw[:, :, hp].rearrange("p k i j -> p i k j"))
            if hb:
                self.ph.hold(pool, self.normed, NB * b + hb)
                ins = nc.gpsimd.tensor_copy(self.own[k][:, 0, :], self.own[before][:, BLK, :])
            else:
                ins = nc.gpsimd.memset(self.own[k][:, 0, :], 0.0)
            ins.then_inc(self.normed, 1)
            if hb == NB - 1:
                nc.gpsimd.memset(self.own[k][:, A_ROWS - 1, :], 0.0).then_inc(self.whole, 1)

    def wait_free(self, eng, b, hb):
        self.ph.hold(eng, self.conved, self.per * (NB * b + hb + 1))

    def wait_conved(self, eng, b, g):
        eng.wait_ge(self.conved, self.lead + self.per * NB * b + g + 1)

    def wait_block(self, pe, b, hb):
        pe.wait_ge(self.next_in[hb % SLOTS], 32 * (NB // SLOTS) * b + 32 * (hb // SLOTS) + 32)

    def operands(self, k, dh, first, rows, step=1):
        r0 = first + dh
        for ab, t in enumerate((self.own, self.next_)):
            if rows == 1:
                yield ab, t[k][:, r0, 1:1 + PAIRS]
            else:
                yield ab, t[k][:, r0:r0 + step * (rows - 1) + 1:step, 1:1 + PAIRS]


def tap_of(ab, dh, pi, po):
    if ab == 0:
        return 3 * dh + 1 + pi - po
    return {(0, 1): 3 * dh + 2, (1, 0): 3 * dh}.get((pi, po))


TILES6 = [(ab, dh, po) for ab in range(2) for dh in range(3) for po in range(2)]


def kernels_phase(nc, p, names):
    rows = {"qk": ("qkv_w", "dw_w", 0), "v": ("qkv_w", "dw_w", 2 * C), "x1": ("w_in", "w_dw", 0), "x2": ("w_in", "w_dw", HID)}
    with_v = names == ("qk",)
    with Phase(nc, "kn") as ph:
        every = names + ("v",) * with_v
        size = {n: C if n == "v" else HID for n in every}
        w1 = {n: ph.sb(f"w1_{n}", [size[n], C2]) for n in every}
        dw = {n: ph.sb(f"dw_{n}", [size[n], 9]) for n in every}
        scaled = {n: p["v_taps"] if n == "v" else ph.sb(f"scaled_{n}", [HID, len(TILES6), C2]) for n in every}
        sums = [ph.ps(f"sum{k}") for k in range(4)]
        loaded, made, multiplied, copied = ph.sem("loaded"), ph.sem("made"), ph.sem("multiplied"), ph.sem("copied")
        block = ph.block()

        @block.sync
        def _(sp):
            for n in every:
                w, d, at = rows[n]
                for pi in range(2):
                    sp.dma_start(w1[n][:, pi * C:(pi + 1) * C], p[w][at:at + size[n]]).then_inc(loaded, 16)
                sp.dma_start(dw[n][:, :], p[d][at:at + size[n]]).then_inc(loaded, 16)

        @block.vector
        def _(dve):
            dve.wait_ge(loaded, 3 * len(every) * 16)
            for n in every:
                for j, (ab, dh, po) in enumerate(TILES6):
                    for pi in range(2):
                        t = tap_of(ab, dh, pi, po)
                        o = scaled[n][:, j, pi * C:(pi + 1) * C]
                        if t is None:
                            ins = nc.vector.memset(o, 0.0)
                        else:
                            ins = nc.vector.tensor_scalar(o, w1[n][:, pi * C:(pi + 1) * C], dw[n][:, t:t + 1], None, ALU.mult)
                ins.then_inc(made, 1)
            i = 0
            for n in names:
                for ab, dh, po in TILES6:
                    dve.wait_ge(multiplied, i + 1)
                    s = sums[i % 4][0:C2, 0:HID]
                    if n == "qk":
                        ins = nc.vector.tensor_copy(p["w_qk"][:, ab, dh, po * HID:(po + 1) * HID], s)
                    else:
                        w3, x = p["w_hid"][:, ab, dh], int(n == "x2")
                        if po == 0:
                            ins = nc.vector.tensor_copy(w3[:, 128 * x:128 * x + HID], s)
                        else:
                            nc.vector.tensor_copy(w3[:, 128 * x + HID:128 * x + 128], s[:, 0:32])
                            ins = nc.vector.tensor_copy(w3[:, 256 + 64 * x:256 + 64 * x + 64], s[:, 32:HID])
                    ins.then_inc(copied, 1)
                    i += 1

        @block.tensor
        def _(pe):
            i = 0
            for j, n in enumerate(names):
                pe.wait_ge(made, j + 1)
                for t in range(len(TILES6)):
                    if i >= 4:
                        pe.wait_ge(copied, i - 3)
                    nc.tensor.matmul(sums[i % 4][0:C2, 0:HID], scaled[n][:, t, :], p["ident"][:, :],
                                     start=True, stop=True).then_inc(multiplied, 1)
                    i += 1


def gram_phase(nc, src, scale, shift, w_qk, gram):
    with Phase(nc, "qk") as ph:
        rs = RowStream(nc, ph, src, scale, shift, BLK)
        qk = [ph.ps(f"qk{k}") for k in range(4)]
        gsum = ph.ps("gsum")
        rows = [ph.sb(f"rows{k}", [128, 2 * HID]) for k in range(4)]
        evacuated, used, folded = (ph.sem(n) for n in ("evacuated", "used", "folded"))
        block = ph.block()
        BODY = SLOTS * BLK

        @block.sync
        def _(sp):
            with sp.Fori(0, B) as b:
                def raw_free(hb):
                    if hb >= 0:
                        ph.hold(sp, rs.normed, NB * b + hb + 1)

                rs.sync_batch(sp, b, raw_free)

        @block.gpsimd
        def _(pool):
            rs.pool_clear(pool)
            with pool.Fori(0, B) as b:
                rs.pool_batch(pool, b)

        @block.tensor
        def _(pe):
            def grams(b, row):
                pe.wait_ge(evacuated, H * b + row + 1 + 4)
                r = row % BODY
                if r == 0:
                    pe.wait_ge(folded, (H // BODY) * b + row // BODY + 1)
                for par in range(2):
                    q = rows[row % 4][:, par * HID:(par + 1) * HID]
                    mm = nc.tensor.matmul(gsum[0:HID, 0:HID], q, q, start=(r == 0 and par == 0),
                                          stop=(r == BODY - 1 and par == 1))
                mm.then_inc(used, 1)

            with pe.Fori(0, B) as b:
                for row in range(H):
                    hb, r = row // BLK, row % BLK
                    k = hb % SLOTS
                    if r == 0:
                        rs.wait_block(pe, b, hb)
                    pe.wait_ge(evacuated, H * b + row + 1)
                    n = 0
                    for dh in range(3):
                        for ab, px in rs.operands(k, dh, r, 1):
                            mm = nc.tensor.matmul(qk[row % 4][:, 0:2 * HID], px, w_qk[:, ab, dh, :],
                                                  start=(n == 0), stop=(n == 5))
                            n += 1
                    mm.then_inc(rs.conved, 1)
                    if row >= 2:
                        grams(b, row - 2)
                for row in (H - 2, H - 1):
                    grams(b, row)

        @block.vector
        def _(dve):
            dve.sem_inc(evacuated, 4)
            dve.sem_inc(folded, 1)
            with dve.Fori(0, B) as b:
                def fold(part):
                    dve.wait_ge(used, H * b + BODY * (part + 1))
                    g = gram[:, bass.ds(b, 1), :].rearrange("p b n -> p (b n)")
                    if part == 0:
                        nc.vector.tensor_copy(g, gsum[0:HID, 0:HID]).then_inc(folded, 1)
                    else:
                        dve.wait_ge(folded, (H // BODY) * b + part + 1)
                        nc.vector.tensor_tensor(g, gsum[0:HID, 0:HID], g, ALU.add).then_inc(folded, 1)

                for row in range(H):
                    rs.wait_conved(dve, b, row)
                    if row >= 4:
                        dve.wait_ge(used, H * b + row - 3)
                    nc.vector.tensor_copy(rows[row % 4][:, :], qk[row % 4][:, 0:2 * HID]).then_inc(evacuated, 1)
                    if row % BODY == 2 and row > BODY:
                        fold(row // BODY - 1)
                fold(H // BODY - 1)


def attention_phase(nc, p, gram, w_v):
    with Phase(nc, "at") as ph:
        sq, diag, norm, rn = (ph.sb(n, [HID, HID]) if n == "sq" else ph.sb(n, [HID, 1]) for n in ("sq", "diag", "norm", "rn"))
        dk = ph.sb("dk", [HID, C])
        temp = ph.sb("temp", [C, 1])
        logit, prob, attn = (ph.sb(n, [C, C]) for n in ("logit", "prob", "attn"))
        top, total, inv = (ph.sb(n, [C, 1]) for n in ("top", "total", "inv"))
        proj_t, mixed = ph.sb("proj_t", [C, C]), ph.sb("mixed", [C, C])
        pl, pm = ph.ps("pl"), ph.ps("pm")
        pk = [ph.ps(f"pk{k}") for k in range(3)]
        loaded, vec, root, prod, expd = (ph.sem(n) for n in ("loaded", "vec", "root", "prod", "expd"))
        block = ph.block()
        NV = 13
        TILES = len(TILES6)

        @block.sync
        def _(sp):
            sp.dma_start(temp[:, :], p["temperature"].to_broadcast([C, 1])).then_inc(loaded, 16)
            sp.dma_start(proj_t[:, :], p["proj_t"]).then_inc(loaded, 16)

        @block.vector
        def _(dve):
            dve.wait_ge(loaded, 32)
            for b in range(B):
                v = NV * b
                nc.vector.tensor_tensor(sq[:, :], gram[:, b, :], p["ident"][:, :], ALU.mult).then_inc(vec, 1)
                dve.wait_ge(vec, v + 1)
                nc.vector.reduce_sum(diag[:, :], sq[:, :], AX_X).then_inc(vec, 1)
                dve.wait_ge(root, b + 1)
                nc.vector.tensor_scalar(sq[:, 0:1], norm[:, :], L2_EPS, None, ALU.max).then_inc(vec, 1)
                dve.wait_ge(vec, v + 3)
                nc.vector.reciprocal(rn[:, :], sq[:, 0:1]).then_inc(vec, 1)
                dve.wait_ge(vec, v + 4)
                nc.vector.tensor_scalar(dk[:, :], p["ident"][:, C:C2], rn[:, :], None, ALU.mult).then_inc(vec, 1)
                dve.wait_ge(prod, 3 * b + 1)
                nc.vector.tensor_scalar(logit[:, :], pl[0:C, 0:C], rn[0:C, :], temp[:, :], ALU.mult, ALU.mult)\
                  .then_inc(vec, 1)
                dve.wait_ge(vec, v + 6)
                nc.vector.reduce_max(top[:, :], logit[:, :], AX_X).then_inc(vec, 1)
                dve.wait_ge(vec, v + 7)
                nc.vector.tensor_scalar(logit[:, :], logit[:, :], top[:, :], None, ALU.subtract).then_inc(vec, 1)
                dve.wait_ge(expd, b + 1)
                nc.vector.reduce_sum(total[:, :], prob[:, :], AX_X).then_inc(vec, 1)
                dve.wait_ge(vec, v + 9)
                nc.vector.reciprocal(inv[:, :], total[:, :]).then_inc(vec, 1)
                dve.wait_ge(vec, v + 10)
                nc.vector.tensor_scalar(attn[:, :], prob[:, :], inv[:, :], None, ALU.mult).then_inc(vec, 1)
                dve.wait_ge(prod, 3 * b + 2)
                nc.vector.tensor_copy(mixed[:, :], pm[0:C, 0:C]).then_inc(vec, 1)
                dve.wait_ge(prod, 3 * b + 3)
                for j in range(3):
                    ins = nc.vector.tensor_copy(
                        w_v[:, b, 4 * j:4 * j + 4, :], pk[j][0:C2, 0:4 * C].rearrange("p (t n) -> p t n", t=4))
                ins.then_inc(vec, 1)

        @block.scalar
        def _(act):
            for b in range(B):
                act.wait_ge(vec, NV * b + 2)
                nc.scalar.activation(norm[:, :], diag[:, :], ACT.Sqrt).then_inc(root, 1)
                act.wait_ge(vec, NV * b + 8)
                nc.scalar.activation(prob[:, :], logit[:, :], ACT.Exp).then_inc(expd, 1)

        @block.tensor
        def _(pe):
            for b in range(B):
                pe.wait_ge(vec, NV * b + 5)
                nc.tensor.matmul(pl[0:C, 0:C], gram[:, b, 0:C], dk[:, :], start=True, stop=True).then_inc(prod, 1)
                pe.wait_ge(vec, NV * b + 11)
                nc.tensor.matmul(pm[0:C, 0:C], attn[:, :], proj_t[:, :], start=True, stop=True).then_inc(prod, 1)
                pe.wait_ge(vec, NV * b + 12)
                for t in range(TILES):
                    mm = nc.tensor.matmul(pk[t // 4][0:C2, (t % 4) * C:(t % 4 + 1) * C], p["v_taps"][:, t, :],
                                          mixed[:, :], start=True, stop=True)
                mm.then_inc(prod, 1)


def value_phase(nc, src, scale, shift, w_v, dst, stats):
    with Phase(nc, "va") as ph:
        NG = 4
        rs = RowStream(nc, ph, src, scale, shift, NG)
        w = ph.sb("w", [C2, 12, C])
        sums = [ph.ps(f"sum{k}") for k in range(4)]
        stored = [ph.sem(f"stored{k}") for k in range(SLOTS)]
        w_set, measured = ph.sem("w_set"), ph.sem("measured")
        added = ph.sem("added")
        block = ph.block()

        @block.sync
        def _(sp):
            with sp.Fori(0, B) as b:
                def store(hb):
                    k = hb % SLOTS
                    ph.hold(sp, added, 4 + NG * NB * b + NG * (hb + 1))
                    d = dst[hb][:, :, :, :, bass.ds(b, 1)].rearrange("wb hp wp c b s -> (wp c) (wb hp) (b s)")
                    sp.dma_start(d, self_raw(k)).then_inc(stored[k], 16)

                def self_raw(k):
                    return rs.raw[k][:, :].rearrange("p (k s) -> p k s", s=SUB)

                def after_copy(hb):
                    if hb:
                        store(hb - 1)

                def raw_free(hb):
                    if hb >= 0:
                        k = hb % SLOTS
                        ph.hold(sp, stored[k], 16 * (NB // SLOTS) * b + 16 * (hb // SLOTS) + 16)
                        ph.hold(sp, measured, NB * b + hb + 1)

                rs.sync_batch(sp, b, raw_free, after_copy)
                store(NB - 1)
                for k in range(SLOTS):
                    ph.hold(sp, stored[k], 16 * (NB // SLOTS) * b + 16 * (NB // SLOTS))
                ph.hold(sp, measured, NB * b + NB)

        @block.gpsimd
        def _(pool):
            rs.pool_clear(pool)
            with pool.Fori(0, B) as b:
                rs.pool_batch(pool, b)

        @block.tensor
        def _(pe):
            with pe.Fori(0, B) as b:
                pe.wait_ge(w_set, b + 1)
                for g in range(NG * NB):
                    hb, e, hp = g // NG, g // 2 % 2, g % 2
                    if g % NG == 0:
                        rs.wait_block(pe, b, hb)
                    pe.wait_ge(added, NG * NB * b + g + 1)
                    n = 0
                    for dh in range(3):
                        for ab, px in rs.operands(hb % SLOTS, dh, 8 * e + hp, 4, 2):
                            mm = nc.tensor.matmul(sums[g % 4][0:C2, :],
                                                  w[:, ab * 6 + dh * 2:ab * 6 + dh * 2 + 2, :].rearrange("p t n -> p (t n)"),
                                                  px, start=(n == 0), stop=(n == 5))
                            n += 1
                    mm.then_inc(rs.conved, 1)

        @block.vector
        def _(dve):
            dve.sem_inc(added, 4)
            with dve.Fori(0, B) as b:
                nc.vector.tensor_copy(w[:, :, :], w_v[:, bass.ds(b, 1), :, :].rearrange("p b t n -> p (b t) n"))\
                  .then_inc(w_set, 1)
                for hb in range(NB):
                    raw = rs.raw[hb % SLOTS][:, :].rearrange("p (k q i j) -> p k q i j", k=NB, q=2, i=HALF)
                    dve.wait_ge(rs.whole, NB * b + hb + 2)
                    for e in range(2):
                        for hp in range(2):
                            g = NG * hb + 2 * e + hp
                            rs.wait_conved(dve, b, g)
                            v = raw[:, :, hp, 4 * e:4 * e + 4].rearrange("p k i j -> p i k j")
                            nc.vector.tensor_tensor(v, sums[g % 4][0:C2, :].rearrange("p (i k j) -> p i k j", i=4, j=HALF),
                                                    v, ALU.add).then_inc(added, 1)
                    dve.wait_ge(added, 4 + NG * NB * b + NG * (hb + 1))
                    for part in range(4):
                        ins = nc.vector.bn_stats(
                            stats[:, bass.ds(b, 1), hb * 4 + part, :].rearrange("p b s -> p (b s)"),
                            rs.raw[hb % SLOTS][:, part * 512:(part + 1) * 512])
                    ins.then_inc(measured, 1)


def gated_phase(nc, p, src, scale, shift, mixed):
    with Phase(nc, "gf") as ph:
        NG = 4
        NS = 2 * NB
        QS = NS // 4
        NC = 2 * C
        G = W // 32
        rs = RowStream(nc, ph, src, scale, shift, 3 * NG)
        banks = [[ph.ps(f"bank{g}{t}") for t in range(3)] for g in range(2)]
        px_sum = [ph.ps(f"px_sum{j}") for j in range(2)]
        gelu_a = [ph.sb(f"gelu_a{k}", [128, 512]) for k in range(2)]
        gelu_c = [ph.sb(f"gelu_c{k}", [128, 512]) for k in range(2)]
        hid_a = [ph.sb(f"hid_a{k}", [128, G, 128]) for k in range(2)]
        hid_c = [ph.sb(f"hid_c{k}", [128, G, 128]) for k in range(2)]
        w_out = ph.sb("w_out", [128, 2, NC])
        stage = [ph.sb(f"stage{k}", [128, NC, G * QS]) for k in range(2)]
        gelued, gated = ph.sem("gelued"), ph.sem("gated")
        projected, moved = ph.sem("projected"), ph.sem("moved")
        w_in, zeroed = ph.sem("w_in"), ph.sem("zeroed")
        stored = [ph.sem(f"stored{k}") for k in range(2)]
        block = ph.block()

        @block.sync
        def _(sp):
            sp.dma_start(w_out[:, :, :], p["w_out"]).then_inc(w_in, 16)
            with sp.Fori(0, B) as b:
                def store(q):
                    ph.hold(sp, moved, 2 + 2 * NS * b + 2 * QS * (q + 1))
                    sp.dma_start(mixed[:, :, bass.ds(4 * b + q, 1), :].rearrange("p m q n -> p m (q n)"),
                                 stage[q % 2][:, :, :]).then_inc(stored[q % 2], 16)

                def after_copy(hb):
                    if hb >= 6 and hb % 4 == 2:
                        store(hb // 4 - 1)

                def raw_free(hb):
                    if hb >= 0:
                        ph.hold(sp, rs.normed, NB * b + hb + 1)

                rs.sync_batch(sp, b, raw_free, after_copy)
                store(3)
            for k in range(2):
                sp.wait_ge(stored[k], 16 + 16 * 2 * B)

        @block.gpsimd
        def _(pool):
            rs.pool_clear(pool)
            with pool.Fori(0, B) as b:
                rs.pool_batch(pool, b)

        @block.tensor
        def _(pe):
            def project(b, s):
                pe.wait_ge(gated, 2 + NG * NB * b + 2 * s + 2)
                for j in range(2):
                    pe.wait_ge(moved, 2 * NS * b + 2 * s + j + 1)
                    for g in range(4):
                        o = px_sum[j][:, g * NC:(g + 1) * NC]
                        nc.tensor.matmul(o, hid_a[s % 2][:, 4 * j + g, :], w_out[:, 0, :], start=True, stop=False)
                        mm = nc.tensor.matmul(o, hid_c[s % 2][:, 4 * j + g, :], w_out[:, 1, :], start=False, stop=True)
                    mm.then_inc(projected, 1)

            pe.wait_ge(w_in, 16)
            pe.wait_ge(zeroed, 2)
            with pe.Fori(0, B) as b:
                for g in range(NG * NB):
                    hb, e, hp = g // NG, g // 2 % 2, g % 2
                    if g % NG == 0:
                        rs.wait_block(pe, b, hb)
                    pe.wait_ge(gated, NG * NB * b + g + 1)
                    for t in (2, 0, 1):
                        n = 0
                        for dh in range(3):
                            for ab, px in rs.operands(hb % SLOTS, dh, 8 * e + hp, 4, 2):
                                mm = nc.tensor.matmul(banks[g % 2][t][:, :], p["w_hid"][:, ab, dh, 128 * t:128 * t + 128],
                                                      px, start=(n == 0), stop=(n == 5))
                                n += 1
                        mm.then_inc(rs.conved, 1)
                    if g >= 2 and g % 2 == 0:
                        project(b, g // 2 - 1)
                project(b, NS - 1)

        @block.scalar
        def _(act):
            with act.Fori(0, B) as b:
                for g in range(NG * NB):
                    k = g % 2
                    rs.wait_conved(act, b, 3 * g)
                    nc.scalar.activation(gelu_c[k][64:128, :], banks[k][2][0:64, :], ACT.Gelu).then_inc(gelued, 1)
                    rs.wait_conved(act, b, 3 * g + 1)
                    nc.scalar.activation(gelu_a[k][:, :], banks[k][0][:, :], ACT.Gelu).then_inc(gelued, 1)

        @block.vector
        def _(dve):
            def move(b, s):
                q, sq = s // QS, s % QS
                if sq == 0:
                    dve.wait_ge(stored[q % 2], 16 * (2 * b + q // 2 + 1))
                out = stage[q % 2][:, :, :].rearrange("p m (g s) -> p g m s", s=QS)
                for j in range(2):
                    dve.wait_ge(projected, 4 + 2 * NS * b + 2 * s + j + 1)
                    nc.vector.tensor_copy(out[:, 4 * j:4 * j + 4, :, sq],
                                          px_sum[j][:, 0:4 * NC].rearrange("p (g m) -> p g m", g=4)).then_inc(moved, 1)

            for k in range(2):
                nc.vector.memset(hid_c[k][0:64, :, :], 0.0).then_inc(zeroed, 1)
            dve.sem_inc(gated, 2)
            dve.sem_inc(projected, 4)
            dve.sem_inc(moved, 2)
            for k in range(2):
                dve.sem_inc(stored[k], 16)
            with dve.Fori(0, B) as b:
                for g in range(NG * NB):
                    k, s, hp = g % 2, g // 2, g % 2
                    dve.wait_ge(projected, 2 * NS * b + 2 * s + 2)

                    def hid(t, lo):
                        v = t[s % 2][lo:128, :, :].rearrange("p g (w h x) -> p (g w) h x", w=2, h=2)[:, :, hp]
                        return v.rearrange("p a (i j) -> p i a j", j=HALF)

                    def px(t, lo):
                        return t[lo:128, :].rearrange("p (i a j) -> p i a j", i=4, j=HALF)

                    dve.wait_ge(gelued, 2 * NG * NB * b + 2 * g + 1)
                    nc.vector.tensor_tensor(hid(hid_c, 64), px(gelu_c[k], 64), px(banks[k][2], 64), ALU.mult)
                    dve.wait_ge(gelued, 2 * NG * NB * b + 2 * g + 2)
                    rs.wait_conved(dve, b, 3 * g + 2)
                    nc.vector.tensor_tensor(hid(hid_a, 0), px(gelu_a[k], 0), px(banks[k][1], 0), ALU.mult)\
                      .then_inc(gated, 1)
                    if g >= 2 and g % 2 == 0:
                        move(b, g // 2 - 1)
                move(b, NS - 1)



FREQ = 8 * 5


def filter_phase(nc, p, mixed, patches, out):
    with Phase(nc, "fi") as ph:
        N = B * H // 8 * W // 32
        y = [ph.sb(f"y{k}", [128, 2, N]) for k in range(2)]
        res = [ph.sb(f"res{k}", [128, 2, N]) for k in range(2)]
        o = [ph.sb(f"o{k}", [128, 2, N]) for k in range(2)]
        wave_in = ph.sb("wave_in", [2 * FREQ, 256])
        wave_out = ph.sb("wave_out", [2 * FREQ, 256])
        same = ph.sb("same", [128, 512])
        fw = ph.sb("fw", [2 * FREQ, C])
        scaled = [ph.sb(f"scaled{k}", [2 * FREQ, 256]) for k in range(2)]
        mat = [ph.sb(f"mat{k}", [128, 512]) for k in range(2)]
        pmat = [ph.ps(f"pmat{k}") for k in range(2)]
        sums = [ph.ps(f"sum{k}") for k in range(4)]
        consts = ph.sem("consts")
        y_in = [ph.sem(f"y_in{k}") for k in range(2)]
        res_in = [ph.sem(f"res_in{k}") for k in range(2)]
        weighted, built, masked = ph.sem("weighted"), ph.sem("built"), ph.sem("masked")
        filtered, added = ph.sem("filtered"), ph.sem("added")
        stored = [ph.sem(f"stored{k}") for k in range(2)]
        block = ph.block()
        QN = 4

        @block.sync
        def _(sp):
            def load(c, k):
                src = mixed.rearrange("p (q c) n s -> p q c (n s)", q=2)
                sp.dma_start(y[k][:, :, :], src[:, :, bass.ds(c, 1), :].rearrange("p q c n -> p (q c) n")).then_inc(y_in[k], 16)
                r = patches[bass.ds(c, 1)].rearrange("c w h x q g n -> (c w h x) q (g n)")
                sp.dma_start(res[k][:, :, :], r).then_inc(res_in[k], 16)

            def store(c, k):
                ph.hold(sp, added, 4 + QN * (c + 1))
                sp.dma_start(out[bass.ds(c, 1)].rearrange("c p q n -> (c p) q n"), o[k][:, :, :]).then_inc(stored[k], 16)

            for d, s in ((wave_in[:, :], p["wave_in"]), (wave_out[:, :], p["wave_out"]), (same[:, :], p["same_patch"]),
                         (fw[0:FREQ, :], p["fft_w"]), (fw[FREQ:2 * FREQ, :], p["fft_w"])):
                sp.dma_start(d, s).then_inc(consts, 16)
            load(0, 0)
            load(1, 1)
            with sp.Fori(0, C // 2 - 1) as i:
                for k in range(2):
                    store(2 * i + k, k)
                    load(2 * i + k + 2, k)
            store(C - 2, 0)
            store(C - 1, 1)
            for k in range(2):
                sp.wait_ge(stored[k], 16 + 16 * (C // 2))

        @block.scalar
        def _(act):
            act.wait_ge(consts, 80)
            act.sem_inc(built, 2)
            with act.Fori(0, C // 2) as i:
                for k in range(2):
                    c = 2 * i + k
                    act.wait_ge(built, c + 1)
                    nc.scalar.activation(scaled[k][:, :], wave_in[:, :], ACT.Copy, scale=fw[:, bass.ds(c, 1)])\
                      .then_inc(weighted, 1)

        @block.tensor
        def _(pe):
            def build(c, k):
                pe.wait_ge(weighted, c + 1)
                pe.wait_ge(masked, c + 1)
                for po in range(2):
                    mm = nc.tensor.matmul(pmat[k][:, po * 256:(po + 1) * 256], scaled[k][:, po * 128:(po + 1) * 128],
                                          wave_out[:, :], start=True, stop=True)
                mm.then_inc(built, 1)

            def filt(i, k):
                c = 2 * i + k
                pe.wait_ge(masked, 2 + c + 1)
                pe.wait_ge(y_in[k], 16 * i + 16)
                for n in range(QN):
                    po_out, half = n // 2, n % 2
                    pe.wait_ge(added, QN * c + n + 1)
                    for po in range(2):
                        lhs = mat[k][:, po * 256 + po_out * 128:po * 256 + po_out * 128 + 128]
                        mm = nc.tensor.matmul(sums[n][:, :], lhs, y[k][:, po, half * 512:half * 512 + 512],
                                              start=(po == 0), stop=(po == 1))
                    mm.then_inc(filtered, 1)

            pe.wait_ge(consts, 80)
            build(0, 0)
            with pe.Fori(0, C // 2 - 1) as i:
                build(2 * i + 1, 1)
                filt(i, 0)
                build(2 * i + 2, 0)
                filt(i, 1)
            build(C - 1, 1)
            filt(C // 2 - 1, 0)
            filt(C // 2 - 1, 1)

        @block.vector
        def _(dve):
            def mask(c, k):
                dve.wait_ge(built, 2 + c + 1)
                dve.wait_ge(filtered, QN * c + QN)
                nc.vector.tensor_tensor(mat[k][:, :], pmat[k][:, :], same[:, :], ALU.mult).then_inc(masked, 1)

            def add(i, k):
                c = 2 * i + k
                dve.wait_ge(res_in[k], 16 * i + 16)
                dve.wait_ge(stored[k], 16 * i + 16)
                for n in range(QN):
                    po, half = n // 2, n % 2
                    dve.wait_ge(filtered, 2 * QN + QN * c + n + 1)
                    for bb in range(2):
                        b = 2 * half + bb
                        r = res[k][:, po, :].rearrange("p (g b q s) -> p b q g s", g=W // 32, b=B, q=4)[:, b]
                        z = sums[n][:, bb * 256:bb * 256 + 256].rearrange("p (q g s) -> p q g s", q=4, g=W // 32)
                        d = o[k][:, po, b * 256:b * 256 + 256].rearrange("p (q g s) -> p q g s", q=4, g=W // 32)
                        ins = nc.vector.tensor_tensor(d, z, r, ALU.add)
                    ins.then_inc(added, 1)

            dve.sem_inc(masked, 2)
            dve.sem_inc(filtered, 2 * QN)
            dve.sem_inc(added, 4)
            for k in range(2):
                dve.sem_inc(stored[k], 16)
            dve.wait_ge(consts, 80)
            mask(0, 0)
            with dve.Fori(0, C // 2 - 1) as i:
                mask(2 * i + 1, 1)
                add(i, 0)
                mask(2 * i + 2, 0)
                add(i, 1)
            mask(C - 1, 1)
            add(C // 2 - 1, 0)
            add(C // 2 - 1, 1)




def build(nc, p, out):
    dram = {n: nc.dram_tensor(n, [NB, NB, 2, 2, C, B, SUB], F32).ap() for n in ("x1", "x2", "up", "x3")}
    down = nc.dram_tensor("down", [C2, H + 2, B, PAIRS], F32).ap()
    right = nc.dram_tensor("right", [C2, W, B, PAIRS], F32).ap()
    mixed = nc.dram_tensor("mixed", [128, C2, 4 * B, SUB], F32).ap()
    patches = nc.dram_tensor("patches", [C, 2, 2, 32, 2, W // 32, B * H // 8], F32).ap()
    with Phase(nc, "all") as ph:
        ident, group_avg = ph.sb("ident", [HID, HID]), ph.sb("group_avg", [C2, C2])
        stats = ph.sb("stats", [C2, B, NSTAT, 6])
        scale, shift = ph.sb("scale", [C2, B]), ph.sb("shift", [C2, B])
        p["ident_dram"], p["ident"] = p["ident"], ident
        consts_phase(nc, ((ident, p["ident_dram"]), (group_avg, p["group_avg"])))

        with Phase(nc, "l0") as l0:
            p["w_qk"] = l0.sb("w_qk", [C2, 2, 3, 2 * HID])
            p["v_taps"] = l0.sb("v_taps", [C, len(TILES6), C2])
            gram = l0.sb("gram", [HID, B, HID])
            w_v = l0.sb("w_v", [C2, B, len(TILES6), C])
            kernels_phase(nc, p, ("qk",))
            stats_phase(nc, p["x"], stats)
            norm_phase(nc, stats, group_avg, scale, shift)
            gram_phase(nc, p["x"], scale, shift, p["w_qk"], gram)
            attention_phase(nc, p, gram, w_v)
            value_phase(nc, p["x"], scale, shift, w_v, dram["x1"], stats)

        for layer, src, dst in ((1, dram["x1"], dram["x2"]), (2, dram["x2"], dram["x3"])):
            norm_phase(nc, stats, group_avg, scale, shift)
            t = {n: p[f"{n}_taps{layer}"] for n in ("down", "right", "left")}
            forward_sweep(nc, "dn", src, "h", t["down"], down, norm=(scale, shift))
            backward_sweep(nc, "up", down, "h", t["down"], dram["up"])
            forward_sweep(nc, "rt", dram["up"], "w", t["right"], right)
            backward_sweep(nc, "lt", right, "w", t["left"], dst, residual=src, stats=stats,
                           patches=patches if layer == 2 else None)

        norm_phase(nc, stats, group_avg, scale, shift)
        with Phase(nc, "l3") as l3:
            p["w_hid"] = l3.sb("w_hid", [C2, 2, 3, 384])
            kernels_phase(nc, p, ("x1", "x2"))
            gated_phase(nc, p, dram["x3"], scale, shift, mixed)
        filter_phase(nc, p, mixed, patches, out)


def consts_phase(nc, pairs):
    with Phase(nc, "cs") as ph:
        loaded = ph.sem("loaded")
        block = ph.block()

        @block.sync
        def _(sp):
            for d, s in pairs:
                sp.dma_start(d[:, :], s).then_inc(loaded, 16)
            sp.wait_ge(loaded, 16 * len(pairs))




def sweep_taps(w, bias):
    t = np.zeros((C2 + 1, 3, C2), np.float32)
    for s in range(3):
        for pi in range(2):
            for po in range(2):
                k = 2 * (s - 1) + pi - po + 2
                if 0 <= k < 5:
                    t[pi * C:(pi + 1) * C, s, po * C:(po + 1) * C] = w[:, :, k].T
    for po in range(2):
        t[C2, 1, po * C:(po + 1) * C] = bias
    return t


def waves():
    m = np.arange(128)
    hp, hi, wi = m // 32 % 2, m // 8 % 4, m % 8
    row, patch = 2 * hi + hp, (m // 64) * 2 + wi // 4
    win, wout = np.zeros((2 * FREQ, 256)), np.zeros((2 * FREQ, 256))
    for po in range(2):
        col = 2 * (wi % 4) + po
        for f in range(FREQ):
            ky, kx = f // 5, f % 5
            coef = (1 if kx in (0, 4) else 2) / 64
            phase = 2 * np.pi * ((ky * row + kx * col) % 8) / 8
            s = slice(po * 128, po * 128 + 128)
            win[f, s], win[FREQ + f, s] = coef * np.cos(phase), coef * np.sin(phase)
            wout[f, s], wout[FREQ + f, s] = np.cos(phase), np.sin(phase)
    same = (patch[:, None] == patch[None, :]).astype(np.float32)
    return win.astype(np.float32), wout.astype(np.float32), np.tile(same, (1, 4))


def kernel(**inputs):
    import concourse.bacc as bacc
    from concourse.bass_utils import run_bass_kernel_spmd

    g = {k: np.asarray(v) for k, v in inputs.items()}
    a = {}
    x = g["x"].reshape(B, C, NB, HALF, 2, NB, HALF, 2)
    a["x"] = x.transpose(2, 5, 4, 7, 1, 0, 3, 6).reshape(NB, NB, 2, 2, C, B, SUB)
    a["qkv_w"] = g["L0_conv_qkv_w"].reshape(3 * C, C)
    a["dw_w"] = g["L0_conv_dw_w"].reshape(3 * C, 9)
    a["proj_t"] = g["L0_conv_proj_w"].reshape(C, C).T
    a["temperature"] = g["L0_conv_temperature"].reshape(1, 1)
    for layer in (1, 2):
        for n in ("down", "right", "left"):
            a[f"{n}_taps{layer}"] = sweep_taps(g[f"L{layer}_conv_{n}_w"], g[f"L{layer}_conv_{n}_b"])
    a["w_in"] = g["L3_conv_w_in"]
    a["w_dw"] = g["L3_conv_w_dw"].reshape(2 * HID, 9)
    w = np.zeros((2 * HID, 2 * C), np.float32)
    for po in range(2):
        w[po * HID:(po + 1) * HID, po * C:(po + 1) * C] = g["L3_conv_w_out"].T
    w_out = np.zeros((128, 2, 2 * C), np.float32)
    w_out[:, 0] = w[0:128]
    w_out[64:128, 1] = w[128:192]
    a["w_out"] = w_out
    a["fft_w"] = g["L3_conv_fft_w"].reshape(C, FREQ).T
    a["wave_in"], a["wave_out"], a["same_patch"] = waves()
    a["ident"] = np.eye(HID, dtype=np.float32)
    group = np.arange(C2) % C // (C // GROUPS)
    a["group_avg"] = ((group[:, None] == group[None, :]) / (2 * C // GROUPS)).astype(np.float32)
    a = {k: np.ascontiguousarray(v) for k, v in a.items()}

    nc = bacc.Bacc("TRN2", target_bir_lowering=False, num_devices=1)
    nc.disable_value_cache = True
    p = {k: nc.dram_tensor(f"in_{k}", v.shape, F32, kind="ExternalInput").ap() for k, v in a.items()}
    out = nc.dram_tensor("out", (C, 128, 2, B * H // 8 * W // 32), F32, kind="ExternalOutput").ap()
    build(nc, p, out)
    r = run_bass_kernel_spmd(nc, [{f"in_{k}": v for k, v in a.items()}], core_ids=[0])
    y = r.results[0]["out"].reshape(C, 2, 2, 4, 2, 4, 2, B, 4, W // 32, 8)
    return y.transpose(7, 0, 8, 10, 3, 2, 9, 1, 4, 5, 6).reshape(B, C, H, W)
```

```python
from contextlib import ExitStack

import numpy as np

import concourse.bass as bass
from concourse import mybir

F32 = mybir.dt.float32
F32R = mybir.dt.float32r
ACT = mybir.ActivationFunctionType
ALU = mybir.AluOpType
AX_X = mybir.AxisListType.X

B, C, H, W = 4, 48, 256, 256
C2 = 2 * C
BLK = 16
NB = H // BLK
HALF = BLK // 2
SUB = HALF * HALF
TILE = NB * 4 * B * SUB // 2
PAIRS = W // 2
PITCH = PAIRS + 2
GROUPS = 16
GN_EPS = 1e-5
L2_EPS = 1e-12
HID = 96
NSTAT = 4 * NB


class Phase:

    def __init__(self, nc, name):
        self.nc, self.name, self.ctx = nc, f"{name}{nc.next_id()}", ExitStack()
        self.sems = []

    def __enter__(self):
        self.ctx.__enter__()
        return self

    def __exit__(self, *a):
        self.ctx.__exit__(*a)
        if self.sems and a[0] is None:
            self.nc.clear_and_free_semaphores(self.sems)
            self.nc.all_engine_barrier()

    def sb(self, name, shape, dt=F32):
        return self.ctx.enter_context(self.nc.sbuf_tensor(f"{self.name}_{name}", shape, dt))

    def ps(self, name, shape=(128, 512)):
        return self.ctx.enter_context(self.nc.psum_tensor(f"{self.name}_{name}", list(shape), F32))

    def sem(self, name):
        self.sems.append(self.nc.alloc_semaphore(f"{self.name}_{name}"))
        return self.sems[-1]

    def block(self):
        self.passed = self.sem("passed")
        return self.ctx.enter_context(self.nc.Block())

    def hold(self, eng, sem, value):
        eng.wait_ge(sem, value)
        eng.sem_inc(self.passed, 1)


def row_block(t, hb):
    return t[hb].rearrange("wb hp wp c b s -> (wp c) (wb hp) (b s)")


def col_block(t, wb, hp, wp):
    return t[:, wb, hp, wp].rearrange("hb c b s -> c hb (b s)")


def step_view(tile, axis, r, b0, nb):
    v = tile.rearrange("p (k q b i j) -> p k q b i j", k=NB, q=2, b=B, i=HALF)
    v = v[:, :, r % 2, b0:b0 + nb]
    v = v[:, :, :, r // 2, :] if axis == "h" else v[:, :, :, :, r // 2]
    return v.rearrange("p k b j -> p b k j")




def stats_phase(nc, src, stats):
    with Phase(nc, "st") as ph:
        tiles = [ph.sb(f"tile{k}", [C2, TILE]) for k in range(2)]
        loaded = [ph.sem(f"loaded{k}") for k in range(2)]
        used = ph.sem("used")
        block = ph.block()

        @block.sync
        def _(sp):
            for k in range(2):
                sp.dma_start(tiles[k][:, :].rearrange("p (k s) -> p k s", s=B * SUB),
                             row_block(src, k)).then_inc(loaded[k], 16)
            with sp.Fori(1, NB // 2) as i:
                for k in range(2):
                    ph.hold(sp, used, 2 * i + k - 1)
                    sp.dma_start(tiles[k][:, :].rearrange("p (k s) -> p k s", s=B * SUB),
                                 row_block(src, 2 * i + k)).then_inc(loaded[k], 16)

        @block.vector
        def _(dve):
            with dve.Fori(0, NB // 2) as i:
                for k in range(2):
                    dve.wait_ge(loaded[k], 16 * i + 16)
                    for n in range(4 * B):
                        b, part = n // 4, n % 4
                        ins = stats_of(nc, tiles[k], stats, b, part, 2 * i + k)
                    ins.then_inc(used, 1)


def stats_of(nc, tile, stats, b, part, n):
    v = tile[:, :].rearrange("p (k b s) -> p k b s", b=B, s=SUB)
    per = 2 * NB // 4
    return nc.vector.bn_stats(stats[:, b, bass.ds(n * 4 + part, 1), :].rearrange("p a s -> p (a s)"),
                              v[:, part * per:(part + 1) * per, b, :])


def norm_phase(nc, stats, group_avg, scale, shift):
    with Phase(nc, "gn") as ph:
        mv = ph.sb("mv", [C2, B, 2])
        dev = ph.sb("dev", [C2, B])
        dev2 = ph.sb("dev2", [C2, B])
        spread = ph.sb("spread", [C2, B])
        eps = ph.sb("eps", [C2, 1])
        std = ph.sb("std", [C2, B])
        mean = ph.sb("mean", [C2, B])
        pm, pv = ph.ps("pm"), ph.ps("pv")
        vec = ph.sem("vec")
        summed = ph.sem("summed")
        rooted = ph.sem("rooted")
        block = ph.block()

        @block.vector
        def _(dve):
            nc.vector.memset(eps[:, :], GN_EPS).then_inc(vec, 1)
            for b in range(B):
                nc.vector.bn_aggr(mv[:, b, :], stats[:, b, :, :].rearrange("p n s -> p (n s)")).then_inc(vec, 1)
            dve.wait_ge(summed, 1)
            nc.vector.tensor_copy(mean[:, :], pm[0:C2, 0:B]).then_inc(vec, 1)
            dve.wait_ge(vec, 6)
            nc.vector.tensor_tensor(dev[:, :], mv[:, :, 0], mean[:, :], ALU.subtract).then_inc(vec, 1)
            dve.wait_ge(vec, 7)
            nc.vector.tensor_tensor(dev2[:, :], dev[:, :], dev[:, :], ALU.mult).then_inc(vec, 1)
            dve.wait_ge(vec, 8)
            nc.vector.tensor_tensor(spread[:, :], dev2[:, :], mv[:, :, 1], ALU.add).then_inc(vec, 1)
            dve.wait_ge(rooted, 1)
            nc.vector.reciprocal(scale[:, :], std[:, :]).then_inc(vec, 1)
            dve.wait_ge(vec, 10)
            nc.vector.scalar_tensor_tensor(out=shift[:, :], in0=mean[:, :], scalar=-1.0, in1=scale[:, :],
                                           op0=ALU.mult, op1=ALU.mult).then_inc(vec, 1)

        @block.tensor
        def _(pe):
            pe.wait_ge(vec, 5)
            nc.tensor.matmul(pm[0:C2, 0:B], group_avg[:, :], mv[:, :, 0], start=True, stop=True).then_inc(summed, 1)
            pe.wait_ge(vec, 9)
            nc.tensor.matmul(pv[0:C2, 0:B], group_avg[:, :], spread[:, :], start=True, stop=True).then_inc(summed, 1)

        @block.scalar
        def _(act):
            act.wait_ge(summed, 2)
            nc.scalar.activation(std[:, :], pv[0:C2, 0:B], ACT.Sqrt, bias=eps[:, :]).then_inc(rooted, 1)




RING = 4
CHAINS = 2


class Sweep:

    def __init__(self, nc, ph, taps_dram, shared):
        self.nc, self.ph, self.taps_dram = nc, ph, taps_dram
        self.shared = shared
        self.high = ph.sb("high", [C2 + 1, RING, B, PITCH], F32R)
        self.low = ph.sb("low", [C2 + 1, RING, B, PITCH], F32R)
        self.taps = ph.sb("taps", [C2 + 1, 3, C2])
        self.w_high = ph.sb("w_high", [C2 + 1, 3, C2], F32R)
        self.w_low = ph.sb("w_low", [C2 + 1, 3, C2], F32R)
        self.sums = [[ph.ps(f"sum{c}{k}") for k in range(2)] for c in range(CHAINS)]
        self.cleared = ph.sem("cleared")
        self.flagged = ph.sem("flagged")
        self.taps_in = ph.sem("taps_in")
        self.split = ph.sem("split")
        self.conved = [ph.sem(f"conved{c}") for c in range(CHAINS)]
        self.rounded = [ph.sem(f"rounded{c}") for c in range(CHAINS)]
        self.stepped = [ph.sem(f"stepped{c}") for c in range(CHAINS)]
        self.rest = [ph.sem(f"rest{c}") for c in range(CHAINS)]
        self.rest2 = [ph.sem(f"rest2{c}") for c in range(CHAINS)]

    def load_taps(self, sp):
        sp.dma_start(self.taps[:, :, :], self.taps_dram).then_inc(self.taps_in, 16)

    def tensor(self, pe):
        def step(blk, r, c, first):
            t = BLK * blk + r
            if not first:
                pe.wait_ge(self.rounded[c], t)
            prev = (r - 1) % RING
            n = 0
            for w, s_ in ((self.w_high, self.high), (self.w_low, self.high), (self.w_high, self.low)):
                if s_ is self.low and not first:
                    pe.wait_ge(self.rest[c], t)
                    if self.shared:
                        whole, part = r // BLK, min(r % BLK, self.shared)
                        pe.wait_ge(self.rest2[c], self.shared * (blk + whole) + part)
                for s in range(3):
                    kk = C2 + 1 if s == 1 else C2
                    mm = self.nc.tensor.matmul(self.sums[c][r % 2][0:C2, 0:2 * PAIRS], w[0:kk, s, :],
                                               s_[0:kk, prev, 2 * c:2 * c + 2, s:s + PAIRS], start=(n == 0), stop=(n == 8))
                    n += 1
            mm.then_inc(self.conved[c], 1)

        def body(n, first=False):
            for r in range(2 * BLK):
                for c in range(CHAINS):
                    if first and r == RING and c == 0:
                        pe.wait_ge(self.flagged, 1)
                    step(n, r, c, first and r == 0)

        pe.wait_ge(self.cleared, 4)
        pe.wait_ge(self.split, 2)
        body(0, first=True)
        with pe.Fori(1, NB // 2) as i:
            body(2 * i)

    def split_taps(self, dve):
        dve.wait_ge(self.taps_in, 16)
        self.nc.vector.tensor_copy(self.w_high[:, :, :], self.taps[:, :, :]).then_inc(self.split, 1)
        dve.wait_ge(self.split, 1)
        self.nc.vector.tensor_tensor(self.w_low[:, :, :], self.taps[:, :, :], self.w_high[:, :, :], ALU.subtract)\
            .then_inc(self.split, 1)
        dve.wait_ge(self.cleared, 4)

    def add(self, dve, t, r, c, row_in, row_out, view):
        dve.wait_ge(self.conved[c], t + 1)
        total = view(self.sums[c][r % 2][0:C2, 0:2 * PAIRS].rearrange("p (b n) -> p b n", b=2))
        high = view(self.high[0:C2, r % RING, 2 * c:2 * c + 2, 1:1 + PAIRS])
        self.nc.vector.tensor_tensor(high, total, row_in, ALU.add).then_inc(self.rounded[c], 1)
        self.nc.vector.tensor_tensor(view(row_out), total, row_in, ALU.add).then_inc(self.stepped[c], 1)
        if r < self.shared:
            dve.wait_ge(self.stepped[c], t + 1)
            b = 2 * c + 1
            self.nc.vector.tensor_tensor(self.low[0:C2, r % RING, b, 1:1 + PAIRS], row_out[:, 1, :],
                                         self.high[0:C2, r % RING, b, 1:1 + PAIRS], ALU.subtract)\
                .then_inc(self.rest2[c], 1)

    def clear(self, pool):
        g = self.nc.gpsimd
        g.memset(self.low[:, :, :, :].bitcast(F32), 0.0).then_inc(self.cleared, 1)
        g.memset(self.high[0:C2, :, :, :].bitcast(F32), 0.0).then_inc(self.cleared, 1)
        pool.wait_ge(self.cleared, 2)
        g.memset(self.high[C2:C2 + 1, :, :, :].bitcast(F32), 1.0).then_inc(self.cleared, 1)
        pool.wait_ge(self.cleared, 3)
        g.memset(self.high[C2:C2 + 1, RING - 1, :, :].bitcast(F32), 0.0).then_inc(self.cleared, 1)
        for c in range(CHAINS):
            pool.wait_ge(self.conved[c], 1)
        g.memset(self.high[C2:C2 + 1, RING - 1, :, :].bitcast(F32), 1.0).then_inc(self.flagged, 1)

    def take_rest(self, pool, t, r, c, state):
        pool.wait_ge(self.stepped[c], t + 1)
        nb = 1 if r < self.shared else 2
        self.nc.gpsimd.tensor_tensor(self.low[0:C2, r % RING, 2 * c:2 * c + nb, 1:1 + PAIRS], state[:, 0:nb],
                                     self.high[0:C2, r % RING, 2 * c:2 * c + nb, 1:1 + PAIRS], ALU.subtract)\
            .then_inc(self.rest[c], 1)


def forward_sweep(nc, name, src, axis, taps_dram, dst, norm=None):
    shifted = 1 if norm is not None else 0
    with Phase(nc, name) as ph:
        ins = [ph.sb(f"in{k}", [C2, TILE]) for k in range(2)]
        outs = [ph.sb(f"out{k}", [C2, BLK, B, PAIRS]) for k in range(2)]
        sw = Sweep(nc, ph, taps_dram, BLK)
        loaded = [ph.sem(f"loaded{k}") for k in range(2)]
        normed = ph.sem("normed")
        stored = [ph.sem(f"stored{k}") for k in range(2)]
        turned = ph.sem("turned")
        block = ph.block()

        @block.sync
        def _(sp):
            def load(n, k):
                if axis == "h":
                    view = ins[k][:, :].rearrange("p (k s) -> p k s", s=B * SUB)
                    sp.dma_start(view, row_block(src, n)).then_inc(loaded[k], 64)
                else:
                    v4 = ins[k][:, :].rearrange("p (k q s) -> p k q s", q=2, s=B * SUB)
                    for hp in range(2):
                        for wp in range(2):
                            sp.dma_start(v4[hp * C:(hp + 1) * C, :, wp], col_block(src, n, hp, wp))\
                              .then_inc(loaded[k], 16)

            def store(n, k):
                for c in range(CHAINS):
                    ph.hold(sp, sw.stepped[c], BLK * n + BLK)
                sp.dma_start(dst[:, bass.ds(BLK * n + shifted, BLK)], outs[k][:, :, :, :]).then_inc(stored[k], 16)

            sw.load_taps(sp)
            load(0, 0)
            load(1, 1)
            with sp.Fori(0, NB // 2 - 1) as i:
                for k in range(2):
                    store(2 * i + k, k)
                    load(2 * i + k + 2, k)
            store(NB - 2, 0)
            store(NB - 1, 1)
            for k in range(2):
                sp.wait_ge(stored[k], 16 * (NB // 2))
            if shifted:
                for pos in (H - 1, 0):
                    sp.dma_start(dst[:, pos], outs[1][:, BLK - 1, :, :]).then_inc(turned, 16)
                sp.wait_ge(turned, 32)

        if norm is not None:
            scale, shift = norm

            @block.scalar
            def _(act):
                with act.Fori(0, NB // 2) as i:
                    for k in range(2):
                        act.wait_ge(loaded[k], 64 * i + 64)
                        v = ins[k][:, :].rearrange("p (k b s) -> p k b s", b=B, s=SUB)
                        for b in range(B):
                            last = nc.scalar.activation(v[:, :, b], v[:, :, b], ACT.Identity, bias=shift[:, b:b + 1],
                                                        scale=scale[:, b:b + 1])
                        last.then_inc(normed, 1)

        @block.tensor
        def _(pe):
            sw.tensor(pe)

        @block.vector
        def _(dve):
            def body(i, first=False):
                for k in range(2):
                    n = 2 * i + k
                    if norm is not None:
                        dve.wait_ge(normed, n + 1)
                    else:
                        dve.wait_ge(loaded[k], 64 * i + 64)
                    if not first:
                        dve.wait_ge(stored[k], 16 * i)
                    for r in range(BLK):
                        for c in range(CHAINS):
                            sw.add(dve, BLK * n + r, r, c, step_view(ins[k][:, :], axis, r, 2 * c, 2),
                                   outs[k][:, r, 2 * c:2 * c + 2, :],
                                   lambda v: v.rearrange("p b (k j) -> p b k j", j=HALF))

            sw.split_taps(dve)
            body(0, first=True)
            with dve.Fori(1, NB // 2) as i:
                body(i)

        @block.gpsimd
        def _(pool):
            def body(i):
                for k in range(2):
                    for r in range(BLK):
                        for c in range(CHAINS):
                            sw.take_rest(pool, BLK * (2 * i + k) + r, r, c, outs[k][:, r, 2 * c:2 * c + 2, :])

            sw.clear(pool)
            with pool.Fori(0, NB // 2) as i:
                body(i)


def backward_sweep(nc, name, src, axis, taps_dram, dst, residual=None, stats=None, patches=None):
    with Phase(nc, name) as ph:
        ins = [ph.sb(f"in{k}", [C2, BLK, B, PAIRS]) for k in range(2)]
        state = ph.sb("state", [C2, RING, B, PAIRS])
        outs = [ph.sb(f"out{k}", [C2, TILE]) for k in range(2)]
        px = ph.sb("px", [C2, 64, 128]) if patches is not None else None
        sw = Sweep(nc, ph, taps_dram, BLK if stats is None else 0)
        loaded = [ph.sem(f"loaded{k}") for k in range(2)]
        whole = [ph.sem(f"whole{k}") for k in range(2)]
        placed = ph.sem("placed")
        measured = ph.sem("measured")
        stored = [ph.sem(f"stored{k}") for k in range(2)]
        px_made = ph.sem("px_made")
        px_stored = ph.sem("px_stored")
        block = ph.block()

        def blocks_of(t, n, k):
            if axis == "h":
                return [(row_block(t, n), outs[k][:, :].rearrange("p (k s) -> p k s", s=B * SUB))]
            v4 = outs[k][:, :].rearrange("p (k q s) -> p k q s", q=2, s=B * SUB)
            return [(col_block(t, n, hp, wp), v4[hp * C:(hp + 1) * C, :, wp]) for hp in range(2) for wp in range(2)]

        @block.sync
        def _(sp):
            def load(m, k):
                sp.dma_start(ins[k][:, :, :, :], src[:, bass.ds(BLK * (NB - 1) - BLK * m, BLK)]).then_inc(loaded[k], 16)

            def store(i, k):
                m = 2 * i + k
                if residual is not None:
                    ph.hold(sp, whole[k], 64 * i + 64)
                else:
                    ph.hold(sp, placed, BLK * m + BLK)
                pairs = blocks_of(dst, NB - 1 - m, k)
                for d, s in pairs:
                    sp.dma_start(d, s).then_inc(stored[k], 64 // len(pairs))
                if patches is not None:
                    ph.hold(sp, px_made, m + 1)
                    for hp in range(2):
                        sp.dma_start(patches[:, 1 - k, hp, :, :, NB // 2 - 1 - i].rearrange("c x q n -> c (x q) n"),
                                     px[hp * C:(hp + 1) * C, :, :]).then_inc(px_stored, 16)

            sw.load_taps(sp)
            load(0, 0)
            load(1, 1)
            with sp.Fori(0, NB // 2 - 1) as i:
                for k in range(2):
                    ph.hold(sp, placed, BLK * (2 * i + k) + BLK)
                    load(2 * i + k + 2, k)
                    store(i, k)
            for k in range(2):
                store(NB // 2 - 1, k)
            for k in range(2):
                sp.wait_ge(stored[k], 64 * (NB // 2))
            if patches is not None:
                sp.wait_ge(px_stored, 32 * NB)

        @block.tensor
        def _(pe):
            sw.tensor(pe)

        @block.vector
        def _(dve):
            def measure(k, m, n):
                last = stats_of(nc, outs[k], stats, n // 4, n % 4, m)
                if n == 4 * B - 1:
                    last.then_inc(measured, 1)

            def body(i, first=False):
                for k in range(2):
                    m = 2 * i + k
                    dve.wait_ge(loaded[k], 16 * i + 16)
                    todo = list(range(4 * B)) if stats is not None and not (first and k == 0) else []
                    for r in range(BLK):
                        for c in range(CHAINS):
                            if c == 0 and not (first and k == 0 and r < RING):
                                dve.wait_ge(placed, BLK * m + r - RING + 1)
                            sw.add(dve, BLK * m + r, r, c, ins[k][:, BLK - 1 - r, 2 * c:2 * c + 2, :],
                                   state[:, r % RING, 2 * c:2 * c + 2, :], lambda v: v)
                            if todo and r >= LATER - 1 and (c == 1 or r > LATER):
                                if len(todo) == 4 * B:
                                    dve.wait_ge(whole[1 - k], 64 * i + 64 * k)
                                measure(1 - k, m - 1, todo.pop(0))
                    assert not todo

            sw.split_taps(dve)
            body(0, first=True)
            with dve.Fori(1, NB // 2) as i:
                body(i)
            if stats is not None:
                dve.wait_ge(whole[1], 64 * (NB // 2))
                for n in range(4 * B):
                    measure(1, NB - 1, n)

        @block.gpsimd
        def _(pool):
            def add_residual(i, k, part):
                if part == 0:
                    ph.hold(pool, placed, BLK * (2 * i + k) + BLK)
                d, s = blocks_of(residual, NB - 1 - (2 * i + k), k)[part]
                pool.dma_start(s, d, accum_op=ALU.add).then_inc(whole[k], 16)

            def body(i, first=False):
                for k in range(2):
                    for r in range(BLK):
                        for c in range(CHAINS):
                            sw.take_rest(pool, BLK * (2 * i + k) + r, r, c, state[:, r % RING, 2 * c:2 * c + 2, :])
                        if residual is not None and r < 4 and not (first and k == 0):
                            add_residual(i if k else i - 1, 1 - k, r)

            sw.clear(pool)
            body(0, first=True)
            with pool.Fori(1, NB // 2) as i:
                body(i)
            if residual is not None:
                for part in range(4):
                    add_residual(NB // 2 - 1, 1, part)

        @block.scalar
        def _(act):
            def repack(i, k, first):
                m = 2 * i + k
                act.wait_ge(whole[k], 64 * i + 64)
                if not (first and k == 0):
                    act.wait_ge(px_stored, 32 * m)
                v = outs[k][:, :].rearrange("p (k q b e i j) -> p k q b e i j", k=NB, q=2, b=B, e=2, i=HALF // 2)
                o = px[:, :, :].rearrange("p (i j q) (b k e) -> p q b e k i j", i=HALF // 2, q=2, b=B, e=2)
                return [(o[:, q, b, e], v[:, :, q, b, e]) for q in range(2) for b in range(B) for e in range(2)]

            def body(i, first):
                for k in range(2):
                    m = 2 * i + k
                    if not first:
                        act.wait_ge(stored[k], 64 * i)
                        if stats is not None:
                            act.wait_ge(measured, m - 1)
                        if patches is not None:
                            act.wait_ge(px_made, m - 1)
                    moves = []
                    for r in range(BLK):
                        for c in range(CHAINS):
                            act.wait_ge(sw.stepped[c], BLK * m + r + 1)
                        row = state[:, r % RING, :, :].rearrange("p b (k j) -> p b k j", j=HALF)
                        nc.scalar.copy(step_view(outs[k][:, :], axis, BLK - 1 - r, 0, B), row).then_inc(placed, 1)
                        if patches is not None and r == LATER and not (first and k == 0):
                            moves = repack(i - 1 + k, 1 - k, first) if k == 0 else repack(i, 0, first)
                        for _ in range(2):
                            if moves:
                                o, v = moves.pop(0)
                                ins_ = nc.scalar.copy(o, v)
                                if not moves:
                                    ins_.then_inc(px_made, 1)
                    assert not moves

            body(0, True)
            with act.Fori(1, NB // 2) as i:
                body(i, False)
            if patches is not None:
                for o, v in repack(NB // 2 - 1, 1, False):
                    ins_ = nc.scalar.copy(o, v)
                ins_.then_inc(px_made, 1)


LATER = BLK // 2



SLOTS = 4
A_ROWS = BLK + 2


class RowStream:

    def __init__(self, nc, ph, src, scale, shift, per):
        self.per, self.lead = per, SLOTS * per
        self.nc, self.ph, self.src, self.scale, self.shift = nc, ph, src, scale, shift
        self.now = ph.sb("now", [C2, 2])
        self.now_set = ph.sem("now_set")
        self.raw = [ph.sb(f"raw{k}", [C2, 2 * NB * SUB]) for k in range(SLOTS)]
        self.own = [ph.sb(f"own{k}", [C2, A_ROWS, PITCH]) for k in range(SLOTS)]
        self.next_ = [ph.sb(f"next{k}", [C2, A_ROWS, PITCH]) for k in range(SLOTS)]
        self.raw_in = [ph.sem(f"raw_in{k}") for k in range(SLOTS)]
        self.cleared = ph.sem("cleared")
        self.normed = ph.sem("normed")
        self.whole = ph.sem("whole")
        self.next_in = [ph.sem(f"next_in{k}") for k in range(SLOTS)]
        self.conved = ph.sem("conved")

    def sync_batch(self, sp, b, raw_free, after_copy=None):
        def load(hb):
            k = hb % SLOTS
            d = self.raw[k][:, :].rearrange("p (k s) -> p k s", s=SUB)
            s = self.src[hb][:, :, :, :, bass.ds(b, 1)].rearrange("wb hp wp c b s -> (wp c) (wb hp) (b s)")
            sp.dma_start(d, s).then_inc(self.raw_in[k], 16)

        for hb in range(SLOTS - 1):
            load(hb)
        for hb in range(NB):
            k = hb % SLOTS
            n = A_ROWS * PITCH - 1
            self.ph.hold(sp, self.whole, NB * b + hb + 2)
            self.wait_free(sp, b, hb)
            own = self.own[k][:, :, :].rearrange("p r j -> p (r j)")
            nxt = self.next_[k][:, :, :].rearrange("p r j -> p (r j)")
            sp.dma_start(nxt[0:C, 0:n], own[0:C, 1:n + 1]).then_inc(self.next_in[k], 16)
            sp.dma_start(nxt[C:C2, 1:n + 1], own[C:C2, 0:n]).then_inc(self.next_in[k], 16)
            if after_copy is not None:
                after_copy(hb)
            if hb + SLOTS - 1 < NB:
                raw_free(hb - 1)
                load(hb + SLOTS - 1)

    def pool_clear(self, pool):
        for k in range(SLOTS):
            ins = self.nc.gpsimd.memset(self.own[k][:, :, :], 0.0)
        ins.then_inc(self.cleared, 1)
        pool.sem_inc(self.conved, self.lead)
        pool.sem_inc(self.whole, 1)
        pool.wait_ge(self.cleared, 1)

    def pool_batch(self, pool, b):
        nc = self.nc
        self.ph.hold(pool, self.whole, NB * b + 1)
        nc.gpsimd.tensor_copy(self.now[:, 0:1], self.scale[:, bass.ds(b, 1)])
        nc.gpsimd.tensor_copy(self.now[:, 1:2], self.shift[:, bass.ds(b, 1)]).then_inc(self.now_set, 1)
        self.ph.hold(pool, self.now_set, b + 1)

        def norm(out, in_):
            return nc.gpsimd.tensor_scalar(out, in_, self.now[:, 0:1], self.now[:, 1:2], ALU.mult, ALU.add)

        for hb in range(NB):
            k, before = hb % SLOTS, (hb - 1) % SLOTS
            raw = self.raw[k][:, :].rearrange("p (k q i j) -> p k q i j", k=NB, q=2, i=HALF)
            self.ph.hold(pool, self.raw_in[k], 16 * (NB // SLOTS) * b + 16 * (hb // SLOTS) + 16)
            if hb:
                norm(self.own[before][:, A_ROWS - 1, 1:1 + PAIRS].rearrange("p (k j) -> p k j", j=HALF),
                     raw[:, :, 0, 0, :]).then_inc(self.whole, 1)
            self.wait_free(pool, b, hb)
            for hp in range(2):
                rows = self.own[k][:, 1 + hp:1 + hp + BLK - 1:2, 1:1 + PAIRS]
                norm(rows.rearrange("p i (k j) -> p i k j", j=HALF), raw[:, :, hp].rearrange("p k i j -> p i k j"))
            if hb:
                self.ph.hold(pool, self.normed, NB * b + hb)
                ins = nc.gpsimd.tensor_copy(self.own[k][:, 0, :], self.own[before][:, BLK, :])
            else:
                ins = nc.gpsimd.memset(self.own[k][:, 0, :], 0.0)
            ins.then_inc(self.normed, 1)
            if hb == NB - 1:
                nc.gpsimd.memset(self.own[k][:, A_ROWS - 1, :], 0.0).then_inc(self.whole, 1)

    def wait_free(self, eng, b, hb):
        self.ph.hold(eng, self.conved, self.per * (NB * b + hb + 1))

    def wait_conved(self, eng, b, g):
        eng.wait_ge(self.conved, self.lead + self.per * NB * b + g + 1)

    def wait_block(self, pe, b, hb):
        pe.wait_ge(self.next_in[hb % SLOTS], 32 * (NB // SLOTS) * b + 32 * (hb // SLOTS) + 32)

    def operands(self, k, dh, first, rows, step=1):
        r0 = first + dh
        for ab, t in enumerate((self.own, self.next_)):
            if rows == 1:
                yield ab, t[k][:, r0, 1:1 + PAIRS]
            else:
                yield ab, t[k][:, r0:r0 + step * (rows - 1) + 1:step, 1:1 + PAIRS]


def tap_of(ab, dh, pi, po):
    if ab == 0:
        return 3 * dh + 1 + pi - po
    return {(0, 1): 3 * dh + 2, (1, 0): 3 * dh}.get((pi, po))


TILES6 = [(ab, dh, po) for ab in range(2) for dh in range(3) for po in range(2)]


def kernels_phase(nc, p, names):
    rows = {"qk": ("qkv_w", "dw_w", 0), "v": ("qkv_w", "dw_w", 2 * C), "x1": ("w_in", "w_dw", 0), "x2": ("w_in", "w_dw", HID)}
    with_v = names == ("qk",)
    with Phase(nc, "kn") as ph:
        every = names + ("v",) * with_v
        size = {n: C if n == "v" else HID for n in every}
        w1 = {n: ph.sb(f"w1_{n}", [size[n], C2]) for n in every}
        dw = {n: ph.sb(f"dw_{n}", [size[n], 9]) for n in every}
        scaled = {n: p["v_taps"] if n == "v" else ph.sb(f"scaled_{n}", [HID, len(TILES6), C2]) for n in every}
        sums = [ph.ps(f"sum{k}") for k in range(4)]
        loaded, made, multiplied, copied = ph.sem("loaded"), ph.sem("made"), ph.sem("multiplied"), ph.sem("copied")
        block = ph.block()

        @block.sync
        def _(sp):
            for n in every:
                w, d, at = rows[n]
                for pi in range(2):
                    sp.dma_start(w1[n][:, pi * C:(pi + 1) * C], p[w][at:at + size[n]]).then_inc(loaded, 16)
                sp.dma_start(dw[n][:, :], p[d][at:at + size[n]]).then_inc(loaded, 16)

        @block.vector
        def _(dve):
            dve.wait_ge(loaded, 3 * len(every) * 16)
            for n in every:
                for j, (ab, dh, po) in enumerate(TILES6):
                    for pi in range(2):
                        t = tap_of(ab, dh, pi, po)
                        o = scaled[n][:, j, pi * C:(pi + 1) * C]
                        if t is None:
                            ins = nc.vector.memset(o, 0.0)
                        else:
                            ins = nc.vector.tensor_scalar(o, w1[n][:, pi * C:(pi + 1) * C], dw[n][:, t:t + 1], None, ALU.mult)
                ins.then_inc(made, 1)
            i = 0
            for n in names:
                for ab, dh, po in TILES6:
                    dve.wait_ge(multiplied, i + 1)
                    s = sums[i % 4][0:C2, 0:HID]
                    if n == "qk":
                        ins = nc.vector.tensor_copy(p["w_qk"][:, ab, dh, po * HID:(po + 1) * HID], s)
                    else:
                        w3, x = p["w_hid"][:, ab, dh], int(n == "x2")
                        if po == 0:
                            ins = nc.vector.tensor_copy(w3[:, 128 * x:128 * x + HID], s)
                        else:
                            nc.vector.tensor_copy(w3[:, 128 * x + HID:128 * x + 128], s[:, 0:32])
                            ins = nc.vector.tensor_copy(w3[:, 256 + 64 * x:256 + 64 * x + 64], s[:, 32:HID])
                    ins.then_inc(copied, 1)
                    i += 1

        @block.tensor
        def _(pe):
            i = 0
            for j, n in enumerate(names):
                pe.wait_ge(made, j + 1)
                for t in range(len(TILES6)):
                    if i >= 4:
                        pe.wait_ge(copied, i - 3)
                    nc.tensor.matmul(sums[i % 4][0:C2, 0:HID], scaled[n][:, t, :], p["ident"][:, :],
                                     start=True, stop=True).then_inc(multiplied, 1)
                    i += 1


def gram_phase(nc, src, scale, shift, w_qk, gram):
    with Phase(nc, "qk") as ph:
        rs = RowStream(nc, ph, src, scale, shift, BLK)
        qk = [ph.ps(f"qk{k}") for k in range(4)]
        gsum = ph.ps("gsum")
        rows = [ph.sb(f"rows{k}", [128, 2 * HID]) for k in range(4)]
        evacuated, used, folded = (ph.sem(n) for n in ("evacuated", "used", "folded"))
        block = ph.block()
        BODY = SLOTS * BLK

        @block.sync
        def _(sp):
            with sp.Fori(0, B) as b:
                def raw_free(hb):
                    if hb >= 0:
                        ph.hold(sp, rs.normed, NB * b + hb + 1)

                rs.sync_batch(sp, b, raw_free)

        @block.gpsimd
        def _(pool):
            rs.pool_clear(pool)
            with pool.Fori(0, B) as b:
                rs.pool_batch(pool, b)

        @block.tensor
        def _(pe):
            def grams(b, row):
                pe.wait_ge(evacuated, H * b + row + 1 + 4)
                r = row % BODY
                if r == 0:
                    pe.wait_ge(folded, (H // BODY) * b + row // BODY + 1)
                for par in range(2):
                    q = rows[row % 4][:, par * HID:(par + 1) * HID]
                    mm = nc.tensor.matmul(gsum[0:HID, 0:HID], q, q, start=(r == 0 and par == 0),
                                          stop=(r == BODY - 1 and par == 1))
                mm.then_inc(used, 1)

            with pe.Fori(0, B) as b:
                for row in range(H):
                    hb, r = row // BLK, row % BLK
                    k = hb % SLOTS
                    if r == 0:
                        rs.wait_block(pe, b, hb)
                    pe.wait_ge(evacuated, H * b + row + 1)
                    n = 0
                    for dh in range(3):
                        for ab, px in rs.operands(k, dh, r, 1):
                            mm = nc.tensor.matmul(qk[row % 4][:, 0:2 * HID], px, w_qk[:, ab, dh, :],
                                                  start=(n == 0), stop=(n == 5))
                            n += 1
                    mm.then_inc(rs.conved, 1)
                    if row >= 2:
                        grams(b, row - 2)
                for row in (H - 2, H - 1):
                    grams(b, row)

        @block.vector
        def _(dve):
            dve.sem_inc(evacuated, 4)
            dve.sem_inc(folded, 1)
            with dve.Fori(0, B) as b:
                def fold(part):
                    dve.wait_ge(used, H * b + BODY * (part + 1))
                    g = gram[:, bass.ds(b, 1), :].rearrange("p b n -> p (b n)")
                    if part == 0:
                        nc.vector.tensor_copy(g, gsum[0:HID, 0:HID]).then_inc(folded, 1)
                    else:
                        dve.wait_ge(folded, (H // BODY) * b + part + 1)
                        nc.vector.tensor_tensor(g, gsum[0:HID, 0:HID], g, ALU.add).then_inc(folded, 1)

                for row in range(H):
                    rs.wait_conved(dve, b, row)
                    if row >= 4:
                        dve.wait_ge(used, H * b + row - 3)
                    nc.vector.tensor_copy(rows[row % 4][:, :], qk[row % 4][:, 0:2 * HID]).then_inc(evacuated, 1)
                    if row % BODY == 2 and row > BODY:
                        fold(row // BODY - 1)
                fold(H // BODY - 1)


def attention_phase(nc, p, gram, w_v):
    with Phase(nc, "at") as ph:
        sq, diag, norm, rn = (ph.sb(n, [HID, HID]) if n == "sq" else ph.sb(n, [HID, 1]) for n in ("sq", "diag", "norm", "rn"))
        dk = ph.sb("dk", [HID, C])
        temp = ph.sb("temp", [C, 1])
        logit, prob, attn = (ph.sb(n, [C, C]) for n in ("logit", "prob", "attn"))
        top, total, inv = (ph.sb(n, [C, 1]) for n in ("top", "total", "inv"))
        proj_t, mixed = ph.sb("proj_t", [C, C]), ph.sb("mixed", [C, C])
        pl, pm = ph.ps("pl"), ph.ps("pm")
        pk = [ph.ps(f"pk{k}") for k in range(3)]
        loaded, vec, root, prod, expd = (ph.sem(n) for n in ("loaded", "vec", "root", "prod", "expd"))
        block = ph.block()
        NV = 13
        TILES = len(TILES6)

        @block.sync
        def _(sp):
            sp.dma_start(temp[:, :], p["temperature"].to_broadcast([C, 1])).then_inc(loaded, 16)
            sp.dma_start(proj_t[:, :], p["proj_t"]).then_inc(loaded, 16)

        @block.vector
        def _(dve):
            dve.wait_ge(loaded, 32)
            for b in range(B):
                v = NV * b
                nc.vector.tensor_tensor(sq[:, :], gram[:, b, :], p["ident"][:, :], ALU.mult).then_inc(vec, 1)
                dve.wait_ge(vec, v + 1)
                nc.vector.reduce_sum(diag[:, :], sq[:, :], AX_X).then_inc(vec, 1)
                dve.wait_ge(root, b + 1)
                nc.vector.tensor_scalar(sq[:, 0:1], norm[:, :], L2_EPS, None, ALU.max).then_inc(vec, 1)
                dve.wait_ge(vec, v + 3)
                nc.vector.reciprocal(rn[:, :], sq[:, 0:1]).then_inc(vec, 1)
                dve.wait_ge(vec, v + 4)
                nc.vector.tensor_scalar(dk[:, :], p["ident"][:, C:C2], rn[:, :], None, ALU.mult).then_inc(vec, 1)
                dve.wait_ge(prod, 3 * b + 1)
                nc.vector.tensor_scalar(logit[:, :], pl[0:C, 0:C], rn[0:C, :], temp[:, :], ALU.mult, ALU.mult)\
                  .then_inc(vec, 1)
                dve.wait_ge(vec, v + 6)
                nc.vector.reduce_max(top[:, :], logit[:, :], AX_X).then_inc(vec, 1)
                dve.wait_ge(vec, v + 7)
                nc.vector.tensor_scalar(logit[:, :], logit[:, :], top[:, :], None, ALU.subtract).then_inc(vec, 1)
                dve.wait_ge(expd, b + 1)
                nc.vector.reduce_sum(total[:, :], prob[:, :], AX_X).then_inc(vec, 1)
                dve.wait_ge(vec, v + 9)
                nc.vector.reciprocal(inv[:, :], total[:, :]).then_inc(vec, 1)
                dve.wait_ge(vec, v + 10)
                nc.vector.tensor_scalar(attn[:, :], prob[:, :], inv[:, :], None, ALU.mult).then_inc(vec, 1)
                dve.wait_ge(prod, 3 * b + 2)
                nc.vector.tensor_copy(mixed[:, :], pm[0:C, 0:C]).then_inc(vec, 1)
                dve.wait_ge(prod, 3 * b + 3)
                for j in range(3):
                    ins = nc.vector.tensor_copy(
                        w_v[:, b, 4 * j:4 * j + 4, :], pk[j][0:C2, 0:4 * C].rearrange("p (t n) -> p t n", t=4))
                ins.then_inc(vec, 1)

        @block.scalar
        def _(act):
            for b in range(B):
                act.wait_ge(vec, NV * b + 2)
                nc.scalar.activation(norm[:, :], diag[:, :], ACT.Sqrt).then_inc(root, 1)
                act.wait_ge(vec, NV * b + 8)
                nc.scalar.activation(prob[:, :], logit[:, :], ACT.Exp).then_inc(expd, 1)

        @block.tensor
        def _(pe):
            for b in range(B):
                pe.wait_ge(vec, NV * b + 5)
                nc.tensor.matmul(pl[0:C, 0:C], gram[:, b, 0:C], dk[:, :], start=True, stop=True).then_inc(prod, 1)
                pe.wait_ge(vec, NV * b + 11)
                nc.tensor.matmul(pm[0:C, 0:C], attn[:, :], proj_t[:, :], start=True, stop=True).then_inc(prod, 1)
                pe.wait_ge(vec, NV * b + 12)
                for t in range(TILES):
                    mm = nc.tensor.matmul(pk[t // 4][0:C2, (t % 4) * C:(t % 4 + 1) * C], p["v_taps"][:, t, :],
                                          mixed[:, :], start=True, stop=True)
                mm.then_inc(prod, 1)


def value_phase(nc, src, scale, shift, w_v, dst, stats):
    with Phase(nc, "va") as ph:
        NG = 4
        rs = RowStream(nc, ph, src, scale, shift, NG)
        w = ph.sb("w", [C2, 12, C])
        sums = [ph.ps(f"sum{k}") for k in range(4)]
        stored = [ph.sem(f"stored{k}") for k in range(SLOTS)]
        w_set, measured = ph.sem("w_set"), ph.sem("measured")
        added = ph.sem("added")
        block = ph.block()

        @block.sync
        def _(sp):
            with sp.Fori(0, B) as b:
                def store(hb):
                    k = hb % SLOTS
                    ph.hold(sp, added, 4 + NG * NB * b + NG * (hb + 1))
                    d = dst[hb][:, :, :, :, bass.ds(b, 1)].rearrange("wb hp wp c b s -> (wp c) (wb hp) (b s)")
                    sp.dma_start(d, self_raw(k)).then_inc(stored[k], 16)

                def self_raw(k):
                    return rs.raw[k][:, :].rearrange("p (k s) -> p k s", s=SUB)

                def after_copy(hb):
                    if hb:
                        store(hb - 1)

                def raw_free(hb):
                    if hb >= 0:
                        k = hb % SLOTS
                        ph.hold(sp, stored[k], 16 * (NB // SLOTS) * b + 16 * (hb // SLOTS) + 16)
                        ph.hold(sp, measured, NB * b + hb + 1)

                rs.sync_batch(sp, b, raw_free, after_copy)
                store(NB - 1)
                for k in range(SLOTS):
                    ph.hold(sp, stored[k], 16 * (NB // SLOTS) * b + 16 * (NB // SLOTS))
                ph.hold(sp, measured, NB * b + NB)

        @block.gpsimd
        def _(pool):
            rs.pool_clear(pool)
            with pool.Fori(0, B) as b:
                rs.pool_batch(pool, b)

        @block.tensor
        def _(pe):
            with pe.Fori(0, B) as b:
                pe.wait_ge(w_set, b + 1)
                for g in range(NG * NB):
                    hb, e, hp = g // NG, g // 2 % 2, g % 2
                    if g % NG == 0:
                        rs.wait_block(pe, b, hb)
                    pe.wait_ge(added, NG * NB * b + g + 1)
                    n = 0
                    for dh in range(3):
                        for ab, px in rs.operands(hb % SLOTS, dh, 8 * e + hp, 4, 2):
                            mm = nc.tensor.matmul(sums[g % 4][0:C2, :],
                                                  w[:, ab * 6 + dh * 2:ab * 6 + dh * 2 + 2, :].rearrange("p t n -> p (t n)"),
                                                  px, start=(n == 0), stop=(n == 5))
                            n += 1
                    mm.then_inc(rs.conved, 1)

        @block.vector
        def _(dve):
            dve.sem_inc(added, 4)
            with dve.Fori(0, B) as b:
                nc.vector.tensor_copy(w[:, :, :], w_v[:, bass.ds(b, 1), :, :].rearrange("p b t n -> p (b t) n"))\
                  .then_inc(w_set, 1)
                for hb in range(NB):
                    raw = rs.raw[hb % SLOTS][:, :].rearrange("p (k q i j) -> p k q i j", k=NB, q=2, i=HALF)
                    dve.wait_ge(rs.whole, NB * b + hb + 2)
                    for e in range(2):
                        for hp in range(2):
                            g = NG * hb + 2 * e + hp
                            rs.wait_conved(dve, b, g)
                            v = raw[:, :, hp, 4 * e:4 * e + 4].rearrange("p k i j -> p i k j")
                            nc.vector.tensor_tensor(v, sums[g % 4][0:C2, :].rearrange("p (i k j) -> p i k j", i=4, j=HALF),
                                                    v, ALU.add).then_inc(added, 1)
                    dve.wait_ge(added, 4 + NG * NB * b + NG * (hb + 1))
                    for part in range(4):
                        ins = nc.vector.bn_stats(
                            stats[:, bass.ds(b, 1), hb * 4 + part, :].rearrange("p b s -> p (b s)"),
                            rs.raw[hb % SLOTS][:, part * 512:(part + 1) * 512])
                    ins.then_inc(measured, 1)


def gated_phase(nc, p, src, scale, shift, mixed):
    with Phase(nc, "gf") as ph:
        NG = 4
        NS = 2 * NB
        QS = NS // 4
        NC = 2 * C
        G = W // 32
        rs = RowStream(nc, ph, src, scale, shift, 3 * NG)
        banks = [[ph.ps(f"bank{g}{t}") for t in range(3)] for g in range(2)]
        px_sum = [ph.ps(f"px_sum{j}") for j in range(2)]
        gelu_a = [ph.sb(f"gelu_a{k}", [128, 512]) for k in range(2)]
        gelu_c = [ph.sb(f"gelu_c{k}", [128, 512]) for k in range(2)]
        hid_a = [ph.sb(f"hid_a{k}", [128, G, 128]) for k in range(2)]
        hid_c = [ph.sb(f"hid_c{k}", [128, G, 128]) for k in range(2)]
        w_out = ph.sb("w_out", [128, 2, NC])
        stage = [ph.sb(f"stage{k}", [128, NC, G * QS]) for k in range(2)]
        gelued, gated = ph.sem("gelued"), ph.sem("gated")
        projected, moved = ph.sem("projected"), ph.sem("moved")
        w_in, zeroed = ph.sem("w_in"), ph.sem("zeroed")
        stored = [ph.sem(f"stored{k}") for k in range(2)]
        block = ph.block()

        @block.sync
        def _(sp):
            sp.dma_start(w_out[:, :, :], p["w_out"]).then_inc(w_in, 16)
            with sp.Fori(0, B) as b:
                def store(q):
                    ph.hold(sp, moved, 2 + 2 * NS * b + 2 * QS * (q + 1))
                    sp.dma_start(mixed[:, :, bass.ds(4 * b + q, 1), :].rearrange("p m q n -> p m (q n)"),
                                 stage[q % 2][:, :, :]).then_inc(stored[q % 2], 16)

                def after_copy(hb):
                    if hb >= 6 and hb % 4 == 2:
                        store(hb // 4 - 1)

                def raw_free(hb):
                    if hb >= 0:
                        ph.hold(sp, rs.normed, NB * b + hb + 1)

                rs.sync_batch(sp, b, raw_free, after_copy)
                store(3)
            for k in range(2):
                sp.wait_ge(stored[k], 16 + 16 * 2 * B)

        @block.gpsimd
        def _(pool):
            rs.pool_clear(pool)
            with pool.Fori(0, B) as b:
                rs.pool_batch(pool, b)

        @block.tensor
        def _(pe):
            def project(b, s):
                pe.wait_ge(gated, 2 + NG * NB * b + 2 * s + 2)
                for j in range(2):
                    pe.wait_ge(moved, 2 * NS * b + 2 * s + j + 1)
                    for g in range(4):
                        o = px_sum[j][:, g * NC:(g + 1) * NC]
                        nc.tensor.matmul(o, hid_a[s % 2][:, 4 * j + g, :], w_out[:, 0, :], start=True, stop=False)
                        mm = nc.tensor.matmul(o, hid_c[s % 2][:, 4 * j + g, :], w_out[:, 1, :], start=False, stop=True)
                    mm.then_inc(projected, 1)

            pe.wait_ge(w_in, 16)
            pe.wait_ge(zeroed, 2)
            with pe.Fori(0, B) as b:
                for g in range(NG * NB):
                    hb, e, hp = g // NG, g // 2 % 2, g % 2
                    if g % NG == 0:
                        rs.wait_block(pe, b, hb)
                    pe.wait_ge(gated, NG * NB * b + g + 1)
                    for t in (2, 0, 1):
                        n = 0
                        for dh in range(3):
                            for ab, px in rs.operands(hb % SLOTS, dh, 8 * e + hp, 4, 2):
                                mm = nc.tensor.matmul(banks[g % 2][t][:, :], p["w_hid"][:, ab, dh, 128 * t:128 * t + 128],
                                                      px, start=(n == 0), stop=(n == 5))
                                n += 1
                        mm.then_inc(rs.conved, 1)
                    if g >= 2 and g % 2 == 0:
                        project(b, g // 2 - 1)
                project(b, NS - 1)

        @block.scalar
        def _(act):
            with act.Fori(0, B) as b:
                for g in range(NG * NB):
                    k = g % 2
                    rs.wait_conved(act, b, 3 * g)
                    nc.scalar.activation(gelu_c[k][64:128, :], banks[k][2][0:64, :], ACT.Gelu).then_inc(gelued, 1)
                    rs.wait_conved(act, b, 3 * g + 1)
                    nc.scalar.activation(gelu_a[k][:, :], banks[k][0][:, :], ACT.Gelu).then_inc(gelued, 1)

        @block.vector
        def _(dve):
            def move(b, s):
                q, sq = s // QS, s % QS
                if sq == 0:
                    dve.wait_ge(stored[q % 2], 16 * (2 * b + q // 2 + 1))
                out = stage[q % 2][:, :, :].rearrange("p m (g s) -> p g m s", s=QS)
                for j in range(2):
                    dve.wait_ge(projected, 4 + 2 * NS * b + 2 * s + j + 1)
                    nc.vector.tensor_copy(out[:, 4 * j:4 * j + 4, :, sq],
                                          px_sum[j][:, 0:4 * NC].rearrange("p (g m) -> p g m", g=4)).then_inc(moved, 1)

            for k in range(2):
                nc.vector.memset(hid_c[k][0:64, :, :], 0.0).then_inc(zeroed, 1)
            dve.sem_inc(gated, 2)
            dve.sem_inc(projected, 4)
            dve.sem_inc(moved, 2)
            for k in range(2):
                dve.sem_inc(stored[k], 16)
            with dve.Fori(0, B) as b:
                for g in range(NG * NB):
                    k, s, hp = g % 2, g // 2, g % 2
                    dve.wait_ge(projected, 2 * NS * b + 2 * s + 2)

                    def hid(t, lo):
                        v = t[s % 2][lo:128, :, :].rearrange("p g (w h x) -> p (g w) h x", w=2, h=2)[:, :, hp]
                        return v.rearrange("p a (i j) -> p i a j", j=HALF)

                    def px(t, lo):
                        return t[lo:128, :].rearrange("p (i a j) -> p i a j", i=4, j=HALF)

                    dve.wait_ge(gelued, 2 * NG * NB * b + 2 * g + 1)
                    nc.vector.tensor_tensor(hid(hid_c, 64), px(gelu_c[k], 64), px(banks[k][2], 64), ALU.mult)
                    dve.wait_ge(gelued, 2 * NG * NB * b + 2 * g + 2)
                    rs.wait_conved(dve, b, 3 * g + 2)
                    nc.vector.tensor_tensor(hid(hid_a, 0), px(gelu_a[k], 0), px(banks[k][1], 0), ALU.mult)\
                      .then_inc(gated, 1)
                    if g >= 2 and g % 2 == 0:
                        move(b, g // 2 - 1)
                move(b, NS - 1)



FREQ = 8 * 5


def filter_phase(nc, p, mixed, patches, out):
    with Phase(nc, "fi") as ph:
        N = B * H // 8 * W // 32
        y = [ph.sb(f"y{k}", [128, 2, N]) for k in range(2)]
        res = [ph.sb(f"res{k}", [128, 2, N]) for k in range(2)]
        o = [ph.sb(f"o{k}", [128, 2, N]) for k in range(2)]
        wave_in = ph.sb("wave_in", [2 * FREQ, 256])
        wave_out = ph.sb("wave_out", [2 * FREQ, 256])
        same = ph.sb("same", [128, 512])
        fw = ph.sb("fw", [2 * FREQ, C])
        scaled = [ph.sb(f"scaled{k}", [2 * FREQ, 256]) for k in range(2)]
        mat = [ph.sb(f"mat{k}", [128, 512]) for k in range(2)]
        pmat = [ph.ps(f"pmat{k}") for k in range(2)]
        sums = [ph.ps(f"sum{k}") for k in range(4)]
        consts = ph.sem("consts")
        y_in = [ph.sem(f"y_in{k}") for k in range(2)]
        res_in = [ph.sem(f"res_in{k}") for k in range(2)]
        weighted, built, masked = ph.sem("weighted"), ph.sem("built"), ph.sem("masked")
        filtered, added = ph.sem("filtered"), ph.sem("added")
        stored = [ph.sem(f"stored{k}") for k in range(2)]
        block = ph.block()
        QN = 4

        @block.sync
        def _(sp):
            def load(c, k):
                src = mixed.rearrange("p (q c) n s -> p q c (n s)", q=2)
                sp.dma_start(y[k][:, :, :], src[:, :, bass.ds(c, 1), :].rearrange("p q c n -> p (q c) n")).then_inc(y_in[k], 16)
                r = patches[bass.ds(c, 1)].rearrange("c w h x q g n -> (c w h x) q (g n)")
                sp.dma_start(res[k][:, :, :], r).then_inc(res_in[k], 16)

            def store(c, k):
                ph.hold(sp, added, 4 + QN * (c + 1))
                sp.dma_start(out[bass.ds(c, 1)].rearrange("c p q n -> (c p) q n"), o[k][:, :, :]).then_inc(stored[k], 16)

            for d, s in ((wave_in[:, :], p["wave_in"]), (wave_out[:, :], p["wave_out"]), (same[:, :], p["same_patch"]),
                         (fw[0:FREQ, :], p["fft_w"]), (fw[FREQ:2 * FREQ, :], p["fft_w"])):
                sp.dma_start(d, s).then_inc(consts, 16)
            load(0, 0)
            load(1, 1)
            with sp.Fori(0, C // 2 - 1) as i:
                for k in range(2):
                    store(2 * i + k, k)
                    load(2 * i + k + 2, k)
            store(C - 2, 0)
            store(C - 1, 1)
            for k in range(2):
                sp.wait_ge(stored[k], 16 + 16 * (C // 2))

        @block.scalar
        def _(act):
            act.wait_ge(consts, 80)
            act.sem_inc(built, 2)
            with act.Fori(0, C // 2) as i:
                for k in range(2):
                    c = 2 * i + k
                    act.wait_ge(built, c + 1)
                    nc.scalar.activation(scaled[k][:, :], wave_in[:, :], ACT.Copy, scale=fw[:, bass.ds(c, 1)])\
                      .then_inc(weighted, 1)

        @block.tensor
        def _(pe):
            def build(c, k):
                pe.wait_ge(weighted, c + 1)
                pe.wait_ge(masked, c + 1)
                for po in range(2):
                    mm = nc.tensor.matmul(pmat[k][:, po * 256:(po + 1) * 256], scaled[k][:, po * 128:(po + 1) * 128],
                                          wave_out[:, :], start=True, stop=True)
                mm.then_inc(built, 1)

            def filt(i, k):
                c = 2 * i + k
                pe.wait_ge(masked, 2 + c + 1)
                pe.wait_ge(y_in[k], 16 * i + 16)
                for n in range(QN):
                    po_out, half = n // 2, n % 2
                    pe.wait_ge(added, QN * c + n + 1)
                    for po in range(2):
                        lhs = mat[k][:, po * 256 + po_out * 128:po * 256 + po_out * 128 + 128]
                        mm = nc.tensor.matmul(sums[n][:, :], lhs, y[k][:, po, half * 512:half * 512 + 512],
                                              start=(po == 0), stop=(po == 1))
                    mm.then_inc(filtered, 1)

            pe.wait_ge(consts, 80)
            build(0, 0)
            with pe.Fori(0, C // 2 - 1) as i:
                build(2 * i + 1, 1)
                filt(i, 0)
                build(2 * i + 2, 0)
                filt(i, 1)
            build(C - 1, 1)
            filt(C // 2 - 1, 0)
            filt(C // 2 - 1, 1)

        @block.vector
        def _(dve):
            def mask(c, k):
                dve.wait_ge(built, 2 + c + 1)
                dve.wait_ge(filtered, QN * c + QN)
                nc.vector.tensor_tensor(mat[k][:, :], pmat[k][:, :], same[:, :], ALU.mult).then_inc(masked, 1)

            def add(i, k):
                c = 2 * i + k
                dve.wait_ge(res_in[k], 16 * i + 16)
                dve.wait_ge(stored[k], 16 * i + 16)
                for n in range(QN):
                    po, half = n // 2, n % 2
                    dve.wait_ge(filtered, 2 * QN + QN * c + n + 1)
                    for bb in range(2):
                        b = 2 * half + bb
                        r = res[k][:, po, :].rearrange("p (g b q s) -> p b q g s", g=W // 32, b=B, q=4)[:, b]
                        z = sums[n][:, bb * 256:bb * 256 + 256].rearrange("p (q g s) -> p q g s", q=4, g=W // 32)
                        d = o[k][:, po, b * 256:b * 256 + 256].rearrange("p (q g s) -> p q g s", q=4, g=W // 32)
                        ins = nc.vector.tensor_tensor(d, z, r, ALU.add)
                    ins.then_inc(added, 1)

            dve.sem_inc(masked, 2)
            dve.sem_inc(filtered, 2 * QN)
            dve.sem_inc(added, 4)
            for k in range(2):
                dve.sem_inc(stored[k], 16)
            dve.wait_ge(consts, 80)
            mask(0, 0)
            with dve.Fori(0, C // 2 - 1) as i:
                mask(2 * i + 1, 1)
                add(i, 0)
                mask(2 * i + 2, 0)
                add(i, 1)
            mask(C - 1, 1)
            add(C // 2 - 1, 0)
            add(C // 2 - 1, 1)




def build(nc, p, out):
    dram = {n: nc.dram_tensor(n, [NB, NB, 2, 2, C, B, SUB], F32).ap() for n in ("x1", "x2", "up", "x3")}
    down = nc.dram_tensor("down", [C2, H + 2, B, PAIRS], F32).ap()
    right = nc.dram_tensor("right", [C2, W, B, PAIRS], F32).ap()
    mixed = nc.dram_tensor("mixed", [128, C2, 4 * B, SUB], F32).ap()
    patches = nc.dram_tensor("patches", [C, 2, 2, 32, 2, W // 32, B * H // 8], F32).ap()
    with Phase(nc, "all") as ph:
        ident, group_avg = ph.sb("ident", [HID, HID]), ph.sb("group_avg", [C2, C2])
        stats = ph.sb("stats", [C2, B, NSTAT, 6])
        scale, shift = ph.sb("scale", [C2, B]), ph.sb("shift", [C2, B])
        p["ident_dram"], p["ident"] = p["ident"], ident
        consts_phase(nc, ((ident, p["ident_dram"]), (group_avg, p["group_avg"])))

        with Phase(nc, "l0") as l0:
            p["w_qk"] = l0.sb("w_qk", [C2, 2, 3, 2 * HID])
            p["v_taps"] = l0.sb("v_taps", [C, len(TILES6), C2])
            gram = l0.sb("gram", [HID, B, HID])
            w_v = l0.sb("w_v", [C2, B, len(TILES6), C])
            kernels_phase(nc, p, ("qk",))
            stats_phase(nc, p["x"], stats)
            norm_phase(nc, stats, group_avg, scale, shift)
            gram_phase(nc, p["x"], scale, shift, p["w_qk"], gram)
            attention_phase(nc, p, gram, w_v)
            value_phase(nc, p["x"], scale, shift, w_v, dram["x1"], stats)

        for layer, src, dst in ((1, dram["x1"], dram["x2"]), (2, dram["x2"], dram["x3"])):
            norm_phase(nc, stats, group_avg, scale, shift)
            t = {n: p[f"{n}_taps{layer}"] for n in ("down", "right", "left")}
            forward_sweep(nc, "dn", src, "h", t["down"], down, norm=(scale, shift))
            backward_sweep(nc, "up", down, "h", t["down"], dram["up"])
            forward_sweep(nc, "rt", dram["up"], "w", t["right"], right)
            backward_sweep(nc, "lt", right, "w", t["left"], dst, residual=src, stats=stats,
                           patches=patches if layer == 2 else None)

        norm_phase(nc, stats, group_avg, scale, shift)
        with Phase(nc, "l3") as l3:
            p["w_hid"] = l3.sb("w_hid", [C2, 2, 3, 384])
            kernels_phase(nc, p, ("x1", "x2"))
            gated_phase(nc, p, dram["x3"], scale, shift, mixed)
        filter_phase(nc, p, mixed, patches, out)


def consts_phase(nc, pairs):
    with Phase(nc, "cs") as ph:
        loaded = ph.sem("loaded")
        block = ph.block()

        @block.sync
        def _(sp):
            for d, s in pairs:
                sp.dma_start(d[:, :], s).then_inc(loaded, 16)
            sp.wait_ge(loaded, 16 * len(pairs))




def sweep_taps(w, bias):
    t = np.zeros((C2 + 1, 3, C2), np.float32)
    for s in range(3):
        for pi in range(2):
            for po in range(2):
                k = 2 * (s - 1) + pi - po + 2
                if 0 <= k < 5:
                    t[pi * C:(pi + 1) * C, s, po * C:(po + 1) * C] = w[:, :, k].T
    for po in range(2):
        t[C2, 1, po * C:(po + 1) * C] = bias
    return t


def waves():
    m = np.arange(128)
    hp, hi, wi = m // 32 % 2, m // 8 % 4, m % 8
    row, patch = 2 * hi + hp, (m // 64) * 2 + wi // 4
    win, wout = np.zeros((2 * FREQ, 256)), np.zeros((2 * FREQ, 256))
    for po in range(2):
        col = 2 * (wi % 4) + po
        for f in range(FREQ):
            ky, kx = f // 5, f % 5
            coef = (1 if kx in (0, 4) else 2) / 64
            phase = 2 * np.pi * ((ky * row + kx * col) % 8) / 8
            s = slice(po * 128, po * 128 + 128)
            win[f, s], win[FREQ + f, s] = coef * np.cos(phase), coef * np.sin(phase)
            wout[f, s], wout[FREQ + f, s] = np.cos(phase), np.sin(phase)
    same = (patch[:, None] == patch[None, :]).astype(np.float32)
    return win.astype(np.float32), wout.astype(np.float32), np.tile(same, (1, 4))


def kernel(**inputs):
    import concourse.bacc as bacc
    from concourse.bass_utils import run_bass_kernel_spmd

    g = {k: np.asarray(v) for k, v in inputs.items()}
    a = {}
    x = g["x"].reshape(B, C, NB, HALF, 2, NB, HALF, 2)
    a["x"] = x.transpose(2, 5, 4, 7, 1, 0, 3, 6).reshape(NB, NB, 2, 2, C, B, SUB)
    a["qkv_w"] = g["L0_conv_qkv_w"].reshape(3 * C, C)
    a["dw_w"] = g["L0_conv_dw_w"].reshape(3 * C, 9)
    a["proj_t"] = g["L0_conv_proj_w"].reshape(C, C).T
    a["temperature"] = g["L0_conv_temperature"].reshape(1, 1)
    for layer in (1, 2):
        for n in ("down", "right", "left"):
            a[f"{n}_taps{layer}"] = sweep_taps(g[f"L{layer}_conv_{n}_w"], g[f"L{layer}_conv_{n}_b"])
    a["w_in"] = g["L3_conv_w_in"]
    a["w_dw"] = g["L3_conv_w_dw"].reshape(2 * HID, 9)
    w = np.zeros((2 * HID, 2 * C), np.float32)
    for po in range(2):
        w[po * HID:(po + 1) * HID, po * C:(po + 1) * C] = g["L3_conv_w_out"].T
    w_out = np.zeros((128, 2, 2 * C), np.float32)
    w_out[:, 0] = w[0:128]
    w_out[64:128, 1] = w[128:192]
    a["w_out"] = w_out
    a["fft_w"] = g["L3_conv_fft_w"].reshape(C, FREQ).T
    a["wave_in"], a["wave_out"], a["same_patch"] = waves()
    a["ident"] = np.eye(HID, dtype=np.float32)
    group = np.arange(C2) % C // (C // GROUPS)
    a["group_avg"] = ((group[:, None] == group[None, :]) / (2 * C // GROUPS)).astype(np.float32)
    a = {k: np.ascontiguousarray(v) for k, v in a.items()}

    nc = bacc.Bacc("TRN2", target_bir_lowering=False, num_devices=1)
    nc.disable_value_cache = True
    p = {k: nc.dram_tensor(f"in_{k}", v.shape, F32, kind="ExternalInput").ap() for k, v in a.items()}
    out = nc.dram_tensor("out", (C, 128, 2, B * H // 8 * W // 32), F32, kind="ExternalOutput").ap()
    build(nc, p, out)
    r = run_bass_kernel_spmd(nc, [{f"in_{k}": v for k, v in a.items()}], core_ids=[0])
    y = r.results[0]["out"].reshape(C, 2, 2, 4, 2, 4, 2, B, 4, W // 32, 8)
    return y.transpose(7, 0, 8, 10, 3, 2, 9, 1, 4, 5, 6).reshape(B, C, H, W)
```

```python
from contextlib import ExitStack

import numpy as np

import concourse.bass as bass
from concourse import mybir

F32 = mybir.dt.float32
F32R = mybir.dt.float32r
ACT = mybir.ActivationFunctionType
ALU = mybir.AluOpType
AX_X = mybir.AxisListType.X

B, C, H, W = 4, 48, 256, 256
C2 = 2 * C
BLK = 16
NB = H // BLK
HALF = BLK // 2
SUB = HALF * HALF
TILE = NB * 4 * B * SUB // 2
PAIRS = W // 2
PITCH = PAIRS + 2
GROUPS = 16
GN_EPS = 1e-5
L2_EPS = 1e-12
HID = 96
NSTAT = 4 * NB


class Phase:

    def __init__(self, nc, name):
        self.nc, self.name, self.ctx = nc, f"{name}{nc.next_id()}", ExitStack()
        self.sems = []

    def __enter__(self):
        self.ctx.__enter__()
        return self

    def __exit__(self, *a):
        self.ctx.__exit__(*a)
        if self.sems and a[0] is None:
            self.nc.clear_and_free_semaphores(self.sems)
            self.nc.all_engine_barrier()

    def sb(self, name, shape, dt=F32):
        return self.ctx.enter_context(self.nc.sbuf_tensor(f"{self.name}_{name}", shape, dt))

    def ps(self, name, shape=(128, 512)):
        return self.ctx.enter_context(self.nc.psum_tensor(f"{self.name}_{name}", list(shape), F32))

    def sem(self, name):
        self.sems.append(self.nc.alloc_semaphore(f"{self.name}_{name}"))
        return self.sems[-1]

    def block(self):
        self.passed = self.sem("passed")
        return self.ctx.enter_context(self.nc.Block())

    def hold(self, eng, sem, value):
        eng.wait_ge(sem, value)
        eng.sem_inc(self.passed, 1)


def row_block(t, hb):
    return t[hb].rearrange("wb hp wp c b s -> (wp c) (wb hp) (b s)")


def col_block(t, wb, hp, wp):
    return t[:, wb, hp, wp].rearrange("hb c b s -> c hb (b s)")


def step_view(tile, axis, r, b0, nb):
    v = tile.rearrange("p (k q b i j) -> p k q b i j", k=NB, q=2, b=B, i=HALF)
    v = v[:, :, r % 2, b0:b0 + nb]
    v = v[:, :, :, r // 2, :] if axis == "h" else v[:, :, :, :, r // 2]
    return v.rearrange("p k b j -> p b k j")




def stats_phase(nc, src, stats):
    with Phase(nc, "st") as ph:
        tiles = [ph.sb(f"tile{k}", [C2, TILE]) for k in range(2)]
        loaded = [ph.sem(f"loaded{k}") for k in range(2)]
        used = ph.sem("used")
        block = ph.block()

        @block.sync
        def _(sp):
            for k in range(2):
                sp.dma_start(tiles[k][:, :].rearrange("p (k s) -> p k s", s=B * SUB),
                             row_block(src, k)).then_inc(loaded[k], 16)
            with sp.Fori(1, NB // 2) as i:
                for k in range(2):
                    ph.hold(sp, used, 2 * i + k - 1)
                    sp.dma_start(tiles[k][:, :].rearrange("p (k s) -> p k s", s=B * SUB),
                                 row_block(src, 2 * i + k)).then_inc(loaded[k], 16)

        @block.vector
        def _(dve):
            with dve.Fori(0, NB // 2) as i:
                for k in range(2):
                    dve.wait_ge(loaded[k], 16 * i + 16)
                    for n in range(4 * B):
                        b, part = n // 4, n % 4
                        ins = stats_of(nc, tiles[k], stats, b, part, 2 * i + k)
                    ins.then_inc(used, 1)


def stats_of(nc, tile, stats, b, part, n):
    v = tile[:, :].rearrange("p (k b s) -> p k b s", b=B, s=SUB)
    per = 2 * NB // 4
    return nc.vector.bn_stats(stats[:, b, bass.ds(n * 4 + part, 1), :].rearrange("p a s -> p (a s)"),
                              v[:, part * per:(part + 1) * per, b, :])


def norm_phase(nc, stats, group_avg, scale, shift):
    with Phase(nc, "gn") as ph:
        mv = ph.sb("mv", [C2, B, 2])
        dev = ph.sb("dev", [C2, B])
        dev2 = ph.sb("dev2", [C2, B])
        spread = ph.sb("spread", [C2, B])
        eps = ph.sb("eps", [C2, 1])
        std = ph.sb("std", [C2, B])
        mean = ph.sb("mean", [C2, B])
        pm, pv = ph.ps("pm"), ph.ps("pv")
        vec = ph.sem("vec")
        summed = ph.sem("summed")
        rooted = ph.sem("rooted")
        block = ph.block()

        @block.vector
        def _(dve):
            nc.vector.memset(eps[:, :], GN_EPS).then_inc(vec, 1)
            for b in range(B):
                nc.vector.bn_aggr(mv[:, b, :], stats[:, b, :, :].rearrange("p n s -> p (n s)")).then_inc(vec, 1)
            dve.wait_ge(summed, 1)
            nc.vector.tensor_copy(mean[:, :], pm[0:C2, 0:B]).then_inc(vec, 1)
            dve.wait_ge(vec, 6)
            nc.vector.tensor_tensor(dev[:, :], mv[:, :, 0], mean[:, :], ALU.subtract).then_inc(vec, 1)
            dve.wait_ge(vec, 7)
            nc.vector.tensor_tensor(dev2[:, :], dev[:, :], dev[:, :], ALU.mult).then_inc(vec, 1)
            dve.wait_ge(vec, 8)
            nc.vector.tensor_tensor(spread[:, :], dev2[:, :], mv[:, :, 1], ALU.add).then_inc(vec, 1)
            dve.wait_ge(rooted, 1)
            nc.vector.reciprocal(scale[:, :], std[:, :]).then_inc(vec, 1)
            dve.wait_ge(vec, 10)
            nc.vector.scalar_tensor_tensor(out=shift[:, :], in0=mean[:, :], scalar=-1.0, in1=scale[:, :],
                                           op0=ALU.mult, op1=ALU.mult).then_inc(vec, 1)

        @block.tensor
        def _(pe):
            pe.wait_ge(vec, 5)
            nc.tensor.matmul(pm[0:C2, 0:B], group_avg[:, :], mv[:, :, 0], start=True, stop=True).then_inc(summed, 1)
            pe.wait_ge(vec, 9)
            nc.tensor.matmul(pv[0:C2, 0:B], group_avg[:, :], spread[:, :], start=True, stop=True).then_inc(summed, 1)

        @block.scalar
        def _(act):
            act.wait_ge(summed, 2)
            nc.scalar.activation(std[:, :], pv[0:C2, 0:B], ACT.Sqrt, bias=eps[:, :]).then_inc(rooted, 1)




RING = 4
CHAINS = 2


class Sweep:

    def __init__(self, nc, ph, taps_dram, shared):
        self.nc, self.ph, self.taps_dram = nc, ph, taps_dram
        self.shared = shared
        self.high = ph.sb("high", [C2 + 1, RING, B, PITCH], F32R)
        self.low = ph.sb("low", [C2 + 1, RING, B, PITCH], F32R)
        self.taps = ph.sb("taps", [C2 + 1, 3, C2])
        self.w_high = ph.sb("w_high", [C2 + 1, 3, C2], F32R)
        self.w_low = ph.sb("w_low", [C2 + 1, 3, C2], F32R)
        self.sums = [[ph.ps(f"sum{c}{k}") for k in range(2)] for c in range(CHAINS)]
        self.cleared = ph.sem("cleared")
        self.flagged = ph.sem("flagged")
        self.taps_in = ph.sem("taps_in")
        self.split = ph.sem("split")
        self.conved = [ph.sem(f"conved{c}") for c in range(CHAINS)]
        self.rounded = [ph.sem(f"rounded{c}") for c in range(CHAINS)]
        self.stepped = [ph.sem(f"stepped{c}") for c in range(CHAINS)]
        self.rest = [ph.sem(f"rest{c}") for c in range(CHAINS)]
        self.rest2 = [ph.sem(f"rest2{c}") for c in range(CHAINS)]

    def load_taps(self, sp):
        sp.dma_start(self.taps[:, :, :], self.taps_dram).then_inc(self.taps_in, 16)

    def tensor(self, pe):
        def step(blk, r, c, first):
            t = BLK * blk + r
            if not first:
                pe.wait_ge(self.rounded[c], t)
            prev = (r - 1) % RING
            n = 0
            for w, s_ in ((self.w_high, self.high), (self.w_low, self.high), (self.w_high, self.low)):
                if s_ is self.low and not first:
                    pe.wait_ge(self.rest[c], t)
                    if self.shared:
                        whole, part = r // BLK, min(r % BLK, self.shared)
                        pe.wait_ge(self.rest2[c], self.shared * (blk + whole) + part)
                for s in range(3):
                    kk = C2 + 1 if s == 1 else C2
                    mm = self.nc.tensor.matmul(self.sums[c][r % 2][0:C2, 0:2 * PAIRS], w[0:kk, s, :],
                                               s_[0:kk, prev, 2 * c:2 * c + 2, s:s + PAIRS], start=(n == 0), stop=(n == 8))
                    n += 1
            mm.then_inc(self.conved[c], 1)

        def body(n, first=False):
            for r in range(2 * BLK):
                for c in range(CHAINS):
                    if first and r == RING and c == 0:
                        pe.wait_ge(self.flagged, 1)
                    step(n, r, c, first and r == 0)

        pe.wait_ge(self.cleared, 4)
        pe.wait_ge(self.split, 2)
        body(0, first=True)
        with pe.Fori(1, NB // 2) as i:
            body(2 * i)

    def split_taps(self, dve):
        dve.wait_ge(self.taps_in, 16)
        self.nc.vector.tensor_copy(self.w_high[:, :, :], self.taps[:, :, :]).then_inc(self.split, 1)
        dve.wait_ge(self.split, 1)
        self.nc.vector.tensor_tensor(self.w_low[:, :, :], self.taps[:, :, :], self.w_high[:, :, :], ALU.subtract)\
            .then_inc(self.split, 1)
        dve.wait_ge(self.cleared, 4)

    def add(self, dve, t, r, c, row_in, row_out, view):
        dve.wait_ge(self.conved[c], t + 1)
        total = view(self.sums[c][r % 2][0:C2, 0:2 * PAIRS].rearrange("p (b n) -> p b n", b=2))
        high = view(self.high[0:C2, r % RING, 2 * c:2 * c + 2, 1:1 + PAIRS])
        self.nc.vector.tensor_tensor(high, total, row_in, ALU.add).then_inc(self.rounded[c], 1)
        self.nc.vector.tensor_tensor(view(row_out), total, row_in, ALU.add).then_inc(self.stepped[c], 1)
        if r < self.shared:
            dve.wait_ge(self.stepped[c], t + 1)
            b = 2 * c + 1
            self.nc.vector.tensor_tensor(self.low[0:C2, r % RING, b, 1:1 + PAIRS], row_out[:, 1, :],
                                         self.high[0:C2, r % RING, b, 1:1 + PAIRS], ALU.subtract)\
                .then_inc(self.rest2[c], 1)

    def clear(self, pool):
        g = self.nc.gpsimd
        g.memset(self.low[:, :, :, :].bitcast(F32), 0.0).then_inc(self.cleared, 1)
        g.memset(self.high[0:C2, :, :, :].bitcast(F32), 0.0).then_inc(self.cleared, 1)
        pool.wait_ge(self.cleared, 2)
        g.memset(self.high[C2:C2 + 1, :, :, :].bitcast(F32), 1.0).then_inc(self.cleared, 1)
        pool.wait_ge(self.cleared, 3)
        g.memset(self.high[C2:C2 + 1, RING - 1, :, :].bitcast(F32), 0.0).then_inc(self.cleared, 1)
        for c in range(CHAINS):
            pool.wait_ge(self.conved[c], 1)
        g.memset(self.high[C2:C2 + 1, RING - 1, :, :].bitcast(F32), 1.0).then_inc(self.flagged, 1)

    def take_rest(self, pool, t, r, c, state):
        pool.wait_ge(self.stepped[c], t + 1)
        nb = 1 if r < self.shared else 2
        self.nc.gpsimd.tensor_tensor(self.low[0:C2, r % RING, 2 * c:2 * c + nb, 1:1 + PAIRS], state[:, 0:nb],
                                     self.high[0:C2, r % RING, 2 * c:2 * c + nb, 1:1 + PAIRS], ALU.subtract)\
            .then_inc(self.rest[c], 1)


def forward_sweep(nc, name, src, axis, taps_dram, dst, norm=None):
    shifted = 1 if norm is not None else 0
    with Phase(nc, name) as ph:
        ins = [ph.sb(f"in{k}", [C2, TILE]) for k in range(2)]
        outs = [ph.sb(f"out{k}", [C2, BLK, B, PAIRS]) for k in range(2)]
        sw = Sweep(nc, ph, taps_dram, BLK)
        loaded = [ph.sem(f"loaded{k}") for k in range(2)]
        normed = ph.sem("normed")
        stored = [ph.sem(f"stored{k}") for k in range(2)]
        turned = ph.sem("turned")
        block = ph.block()

        @block.sync
        def _(sp):
            def load(n, k):
                if axis == "h":
                    view = ins[k][:, :].rearrange("p (k s) -> p k s", s=B * SUB)
                    sp.dma_start(view, row_block(src, n)).then_inc(loaded[k], 64)
                else:
                    v4 = ins[k][:, :].rearrange("p (k q s) -> p k q s", q=2, s=B * SUB)
                    for hp in range(2):
                        for wp in range(2):
                            sp.dma_start(v4[hp * C:(hp + 1) * C, :, wp], col_block(src, n, hp, wp))\
                              .then_inc(loaded[k], 16)

            def store(n, k):
                for c in range(CHAINS):
                    ph.hold(sp, sw.stepped[c], BLK * n + BLK)
                sp.dma_start(dst[:, bass.ds(BLK * n + shifted, BLK)], outs[k][:, :, :, :]).then_inc(stored[k], 16)

            sw.load_taps(sp)
            load(0, 0)
            load(1, 1)
            with sp.Fori(0, NB // 2 - 1) as i:
                for k in range(2):
                    store(2 * i + k, k)
                    load(2 * i + k + 2, k)
            store(NB - 2, 0)
            store(NB - 1, 1)
            for k in range(2):
                sp.wait_ge(stored[k], 16 * (NB // 2))
            if shifted:
                for pos in (H - 1, 0):
                    sp.dma_start(dst[:, pos], outs[1][:, BLK - 1, :, :]).then_inc(turned, 16)
                sp.wait_ge(turned, 32)

        if norm is not None:
            scale, shift = norm

            @block.scalar
            def _(act):
                with act.Fori(0, NB // 2) as i:
                    for k in range(2):
                        act.wait_ge(loaded[k], 64 * i + 64)
                        v = ins[k][:, :].rearrange("p (k b s) -> p k b s", b=B, s=SUB)
                        for b in range(B):
                            last = nc.scalar.activation(v[:, :, b], v[:, :, b], ACT.Identity, bias=shift[:, b:b + 1],
                                                        scale=scale[:, b:b + 1])
                        last.then_inc(normed, 1)

        @block.tensor
        def _(pe):
            sw.tensor(pe)

        @block.vector
        def _(dve):
            def body(i, first=False):
                for k in range(2):
                    n = 2 * i + k
                    if norm is not None:
                        dve.wait_ge(normed, n + 1)
                    else:
                        dve.wait_ge(loaded[k], 64 * i + 64)
                    if not first:
                        dve.wait_ge(stored[k], 16 * i)
                    for r in range(BLK):
                        for c in range(CHAINS):
                            sw.add(dve, BLK * n + r, r, c, step_view(ins[k][:, :], axis, r, 2 * c, 2),
                                   outs[k][:, r, 2 * c:2 * c + 2, :],
                                   lambda v: v.rearrange("p b (k j) -> p b k j", j=HALF))

            sw.split_taps(dve)
            body(0, first=True)
            with dve.Fori(1, NB // 2) as i:
                body(i)

        @block.gpsimd
        def _(pool):
            def body(i):
                for k in range(2):
                    for r in range(BLK):
                        for c in range(CHAINS):
                            sw.take_rest(pool, BLK * (2 * i + k) + r, r, c, outs[k][:, r, 2 * c:2 * c + 2, :])

            sw.clear(pool)
            with pool.Fori(0, NB // 2) as i:
                body(i)


def backward_sweep(nc, name, src, axis, taps_dram, dst, residual=None, stats=None, patches=None):
    with Phase(nc, name) as ph:
        ins = [ph.sb(f"in{k}", [C2, BLK, B, PAIRS]) for k in range(2)]
        state = ph.sb("state", [C2, RING, B, PAIRS])
        outs = [ph.sb(f"out{k}", [C2, TILE]) for k in range(2)]
        px = ph.sb("px", [C2, 64, 128]) if patches is not None else None
        sw = Sweep(nc, ph, taps_dram, BLK if stats is None else LATER - 3)
        loaded = [ph.sem(f"loaded{k}") for k in range(2)]
        whole = [ph.sem(f"whole{k}") for k in range(2)]
        placed = ph.sem("placed")
        measured = ph.sem("measured")
        stored = [ph.sem(f"stored{k}") for k in range(2)]
        px_made = ph.sem("px_made")
        px_stored = ph.sem("px_stored")
        block = ph.block()

        def blocks_of(t, n, k):
            if axis == "h":
                return [(row_block(t, n), outs[k][:, :].rearrange("p (k s) -> p k s", s=B * SUB))]
            v4 = outs[k][:, :].rearrange("p (k q s) -> p k q s", q=2, s=B * SUB)
            return [(col_block(t, n, hp, wp), v4[hp * C:(hp + 1) * C, :, wp]) for hp in range(2) for wp in range(2)]

        @block.sync
        def _(sp):
            def load(m, k):
                sp.dma_start(ins[k][:, :, :, :], src[:, bass.ds(BLK * (NB - 1) - BLK * m, BLK)]).then_inc(loaded[k], 16)

            def store(i, k):
                m = 2 * i + k
                if residual is not None:
                    ph.hold(sp, whole[k], 64 * i + 64)
                else:
                    ph.hold(sp, placed, BLK * m + BLK)
                pairs = blocks_of(dst, NB - 1 - m, k)
                for d, s in pairs:
                    sp.dma_start(d, s).then_inc(stored[k], 64 // len(pairs))

            def store_patches(i, k):
                if patches is not None:
                    ph.hold(sp, px_made, 2 * i + k + 1)
                    for hp in range(2):
                        sp.dma_start(patches[:, 1 - k, hp, :, :, NB // 2 - 1 - i].rearrange("c x q n -> c (x q) n"),
                                     px[hp * C:(hp + 1) * C, :, :]).then_inc(px_stored, 16)

            sw.load_taps(sp)
            load(0, 0)
            load(1, 1)
            with sp.Fori(0, NB // 2 - 1) as i:
                for k in range(2):
                    ph.hold(sp, placed, BLK * (2 * i + k) + BLK)
                    if residual is None:
                        load(2 * i + k + 2, k)
                        store(i, k)
                    else:
                        store(i, k)
                        load(2 * i + k + 2, k)
                    store_patches(i, k)
            for k in range(2):
                store(NB // 2 - 1, k)
                store_patches(NB // 2 - 1, k)
            for k in range(2):
                sp.wait_ge(stored[k], 64 * (NB // 2))
            if patches is not None:
                sp.wait_ge(px_stored, 32 * NB)

        @block.tensor
        def _(pe):
            sw.tensor(pe)

        @block.vector
        def _(dve):
            def measure(k, m, n):
                last = stats_of(nc, outs[k], stats, n // 4, n % 4, m)
                if n == 4 * B - 1:
                    last.then_inc(measured, 1)

            def body(i, first=False):
                for k in range(2):
                    m = 2 * i + k
                    dve.wait_ge(loaded[k], 16 * i + 16)
                    todo = list(range(4 * B)) if stats is not None and not (first and k == 0) else []
                    for r in range(BLK):
                        for c in range(CHAINS):
                            if c == 0 and not (first and k == 0 and r < RING):
                                dve.wait_ge(placed, BLK * m + r - RING + 1)
                            sw.add(dve, BLK * m + r, r, c, ins[k][:, BLK - 1 - r, 2 * c:2 * c + 2, :],
                                   state[:, r % RING, 2 * c:2 * c + 2, :], lambda v: v)
                            if todo and r >= LATER - 1 and (c == 1 or r > LATER):
                                if len(todo) == 4 * B:
                                    dve.wait_ge(whole[1 - k], 64 * i + 64 * k)
                                measure(1 - k, m - 1, todo.pop(0))
                    assert not todo

            sw.split_taps(dve)
            body(0, first=True)
            with dve.Fori(1, NB // 2) as i:
                body(i)
            if stats is not None:
                dve.wait_ge(whole[1], 64 * (NB // 2))
                for n in range(4 * B):
                    measure(1, NB - 1, n)

        @block.gpsimd
        def _(pool):
            def add_residual(i, k, part):
                if part == 0:
                    ph.hold(pool, placed, BLK * (2 * i + k) + BLK)
                d, s = blocks_of(residual, NB - 1 - (2 * i + k), k)[part]
                pool.dma_start(s, d, accum_op=ALU.add).then_inc(whole[k], 16)

            def body(i, first=False):
                for k in range(2):
                    for r in range(BLK):
                        for c in range(CHAINS):
                            sw.take_rest(pool, BLK * (2 * i + k) + r, r, c, state[:, r % RING, 2 * c:2 * c + 2, :])
                        if residual is not None and r < 4 and not (first and k == 0):
                            add_residual(i if k else i - 1, 1 - k, r)

            sw.clear(pool)
            body(0, first=True)
            with pool.Fori(1, NB // 2) as i:
                body(i)
            if residual is not None:
                for part in range(4):
                    add_residual(NB // 2 - 1, 1, part)

        @block.scalar
        def _(act):
            def repack(i, k, first):
                m = 2 * i + k
                act.wait_ge(whole[k], 64 * i + 64)
                if not (first and k == 0):
                    act.wait_ge(px_stored, 32 * m)
                v = outs[k][:, :].rearrange("p (k q b e i j) -> p k q b e i j", k=NB, q=2, b=B, e=2, i=HALF // 2)
                o = px[:, :, :].rearrange("p (i j q) (b k e) -> p q b e k i j", i=HALF // 2, q=2, b=B, e=2)
                return [(o[:, q, b, e], v[:, :, q, b, e]) for q in range(2) for b in range(B) for e in range(2)]

            def body(i, first):
                for k in range(2):
                    m = 2 * i + k
                    if not first:
                        act.wait_ge(stored[k], 64 * i)
                        if stats is not None:
                            act.wait_ge(measured, m - 1)
                        if patches is not None:
                            act.wait_ge(px_made, m - 1)
                    moves = []
                    for r in range(BLK):
                        for c in range(CHAINS):
                            act.wait_ge(sw.stepped[c], BLK * m + r + 1)
                        row = state[:, r % RING, :, :].rearrange("p b (k j) -> p b k j", j=HALF)
                        nc.scalar.copy(step_view(outs[k][:, :], axis, BLK - 1 - r, 0, B), row).then_inc(placed, 1)
                        if patches is not None and r == LATER and not (first and k == 0):
                            moves = repack(i - 1 + k, 1 - k, first) if k == 0 else repack(i, 0, first)
                        for _ in range(2):
                            if moves:
                                o, v = moves.pop(0)
                                ins_ = nc.scalar.copy(o, v)
                                if not moves:
                                    ins_.then_inc(px_made, 1)
                    assert not moves

            body(0, True)
            with act.Fori(1, NB // 2) as i:
                body(i, False)
            if patches is not None:
                for o, v in repack(NB // 2 - 1, 1, False):
                    ins_ = nc.scalar.copy(o, v)
                ins_.then_inc(px_made, 1)


LATER = BLK // 2



STRIP = 8
NSTRIP = H // STRIP
SLOTS = 2
QK_COLS = 256
LEAD = 2


class RowStream:

    def __init__(self, nc, ph, src, scale, shift, per, plain=False, raws=2):
        self.nc, self.ph, self.src, self.scale, self.shift = nc, ph, src, scale, shift
        self.per, self.lead, self.plain, self.raws = per, SLOTS * per, plain, raws
        self.rows = STRIP + 2 if plain else 2 * STRIP
        self.raw = [ph.sb(f"raw{k}", [C2, 2 * NB * SUB]) for k in range(raws)]
        self.block = [ph.sb(f"block{k}", [C2, BLK + 2, PITCH]) for k in range(2)]
        self.sums4 = None if plain else ph.sb("sums4", [C2, self.rows, PITCH])
        self.parts = {(w, q): [ph.sb(f"{w}_{q}{k}", [C2, self.rows, PITCH], F32R) for k in range(SLOTS)]
                      for w in ("own", "next") for q in ("high", "low")}
        self.zero = ph.sb("zero", [C2, PITCH])
        self.raw_in = [ph.sem(f"raw_in{k}") for k in range(raws)]
        self.cleared, self.normed = ph.sem("cleared"), ph.sem("normed")
        self.whole = ph.sem("whole")
        self.summed = ph.sem("summed")
        self.rounded, self.rest = ph.sem("rounded"), ph.sem("rest")
        self.next_high = [ph.sem(f"next_high{k}") for k in range(SLOTS)]
        self.next_low = [ph.sem(f"next_low{k}") for k in range(SLOTS)]
        self.conved = ph.sem("conved")
        self.read = self.rest if plain else self.summed

    def loads_of(self, k):
        return len(range(k, NB, self.raws))

    def load(self, sp, b, hb):
        k = hb % self.raws
        d = self.raw[k][:, :].rearrange("p (k s) -> p k s", s=SUB)
        s = self.src[hb][:, :, :, :, bass.ds(b, 1)].rearrange("wb hp wp c b s -> (wp c) (wb hp) (b s)")
        sp.dma_start(d, s).then_inc(self.raw_in[k], 16)

    def sync(self, sp, before_load, after_batch=None, between=None):
        for hb in range(LEAD):
            self.load(sp, 0, hb)
        with sp.Fori(0, B - 1) as b:
            self.sync_batch(sp, b, before_load, between, False)
            if after_batch:
                after_batch(b)
        self.sync_batch(sp, B - 1, before_load, between, True)
        if after_batch:
            after_batch(B - 1)

    def sync_batch(self, sp, b, before_load, between, last):
        n = self.rows * PITCH - 1
        for u in range(NSTRIP):
            for q, made, done in (("high", self.rounded, self.next_high), ("low", self.rest, self.next_low)):
                self.ph.hold(sp, made, AHEAD + NSTRIP * b + u + 1)
                own = self.parts["own", q][u % SLOTS][:, :, :].rearrange("p r j -> p (r j)").bitcast(F32)
                nxt = self.parts["next", q][u % SLOTS][:, :, :].rearrange("p r j -> p (r j)").bitcast(F32)
                sp.dma_start(nxt[0:C, 0:n], own[0:C, 1:n + 1]).then_inc(done[u % SLOTS], 16)
                sp.dma_start(nxt[C:C2, 1:n + 1], own[C:C2, 0:n]).then_inc(done[u % SLOTS], 16)
            if u % 2 == 0:
                before_load(b, u // 2)
                if u // 2 + LEAD < NB:
                    self.load(sp, b, u // 2 + LEAD)
                elif not last:
                    self.load(sp, b + 1, u // 2 + LEAD - NB)
            elif between:
                between(b, u // 2)

    def wait_normed(self, sp, b, hb):
        self.ph.hold(sp, self.normed, NB * b + hb + 1)

    def norm(self, act, b, hb):
        nc, k = self.nc, hb % 2
        scale, shift = self.scale[:, bass.ds(b, 1)], self.shift[:, bass.ds(b, 1)]
        if hb == NB:
            nc.scalar.copy(self.block[1 - k][:, BLK + 1, :], self.zero[:, :]).then_inc(self.whole, 1)
            return
        kr = hb % self.raws
        raw = self.raw[kr][:, :].rearrange("p (k q i j) -> p k q i j", k=NB, q=2, i=HALF)
        self.ph.hold(act, self.raw_in[kr], 16 * self.loads_of(kr) * b + 16 * (hb // self.raws) + 16)
        if hb:
            nc.scalar.activation(self.block[1 - k][:, BLK + 1, 1:1 + PAIRS].rearrange("p (k j) -> p k j", j=HALF),
                                 raw[:, :, 0, 0, :], ACT.Identity, bias=shift, scale=scale).then_inc(self.whole, 1)
        self.ph.hold(act, self.read, AHEAD + NSTRIP * b + 2 * hb - 2)
        for hp in range(2):
            rows = self.block[k][:, 1 + hp:1 + hp + BLK - 1:2, 1:1 + PAIRS]
            nc.scalar.activation(rows.rearrange("p i (k j) -> p i k j", j=HALF),
                                 raw[:, :, hp].rearrange("p k i j -> p i k j"), ACT.Identity, bias=shift, scale=scale)
        if hb:
            self.ph.hold(act, self.normed, NB * b + hb)
            nc.scalar.copy(self.block[k][:, 0, :], self.block[1 - k][:, BLK, :]).then_inc(self.normed, 1)
        else:
            nc.scalar.copy(self.block[k][:, 0, :], self.zero[:, :]).then_inc(self.normed, 1)

    def wait_rows(self, eng, b, u):
        self.ph.hold(eng, self.whole if u % 2 else self.normed, NB * b + u // 2 + 1)

    def prepare(self, act, b, u):
        if u == 0:
            self.norm(act, b, 0)
        if u % 2 == 0:
            self.norm(act, b, u // 2 + 1)
        if self.plain:
            self.wait_rows(act, b, u)
            rows = self.block[u // 2 % 2][:, STRIP * (u % 2):STRIP * (u % 2) + self.rows, :]
        else:
            self.ph.hold(act, self.summed, AHEAD + NSTRIP * b + u + 1)
            rows = self.sums4[:, :, :]
        self.ph.hold(act, self.conved, self.per * (NSTRIP * b + u + 1))
        self.nc.scalar.copy(self.parts["own", "high"][u % SLOTS][:, :, :], rows).then_inc(self.rounded, 1)

    def pool_clear(self, pool):
        g = self.nc.gpsimd
        g.memset(self.zero[:, :], 0.0)
        for k in range(2):
            last = g.memset(self.block[k][:, :, :], 0.0)
        last.then_inc(self.cleared, 1)
        pool.sem_inc(self.conved, self.lead)
        for s in {id(x): x for x in (self.summed, self.rounded, self.rest)}.values():
            pool.sem_inc(s, AHEAD)

    def pool_batch(self, pool, b):
        g = self.nc.gpsimd
        for u in range(NSTRIP):
            k, at = u // 2 % 2, STRIP * (u % 2)
            if self.plain:
                rows = self.block[k][:, at:at + self.rows, :]
            else:
                rows = self.sums4[:, :, :]
                self.wait_rows(pool, b, u)
                self.ph.hold(pool, self.rounded, AHEAD + NSTRIP * b + u)
                self.ph.hold(pool, self.rest, AHEAD + NSTRIP * b + u)
                d = [self.block[k][:, at + i:at + i + STRIP - 1:2, :] for i in range(4)]
                for t, (x, y, op) in enumerate(((0, 2, ALU.subtract), (1, 2, ALU.add), (2, 1, ALU.subtract),
                                                (1, 3, ALU.subtract))):
                    last = g.tensor_tensor(self.sums4[:, 4 * t:4 * t + 4, :], d[x], d[y], op)
                last.then_inc(self.summed, 1)
                self.ph.hold(pool, self.summed, AHEAD + NSTRIP * b + u + 1)
            self.ph.hold(pool, self.rounded, AHEAD + NSTRIP * b + u + 1)
            g.tensor_tensor(self.parts["own", "low"][u % SLOTS][:, :, :], rows,
                            self.parts["own", "high"][u % SLOTS][:, :, :], ALU.subtract).then_inc(self.rest, 1)

    def wait_conved(self, eng, b, g):
        eng.wait_ge(self.conved, self.lead + self.per * NSTRIP * b + g + 1)

    def wait_high(self, pe, b, u):
        pe.wait_ge(self.next_high[u % SLOTS], 32 * (NSTRIP // SLOTS) * b + 32 * (u // SLOTS) + 32)

    def wait_low(self, pe, b, u):
        pe.wait_ge(self.next_low[u % SLOTS], 32 * (NSTRIP // SLOTS) * b + 32 * (u // SLOTS) + 32)

    def wait_strip(self, pe, b, u):
        self.wait_high(pe, b, u)
        self.wait_low(pe, b, u)

    def passes(self, u, w_high, w_low):
        for q, w in (("high", w_high), ("high", w_low), ("low", w_high)):
            for ab, n in enumerate(("own", "next")):
                yield self.parts[n, q][u % SLOTS], w, ab


AHEAD = 3


def tap_of(ab, dh, pi, po):
    if ab == 0:
        return 3 * dh + 1 + pi - po
    return {(0, 1): 3 * dh + 2, (1, 0): 3 * dh}.get((pi, po))


TILES6 = [(ab, dh, po) for ab in range(2) for dh in range(3) for po in range(2)]


def kernels_phase(nc, p, names):
    rows = {"qk": ("qkv_w", "dw_w", 0), "v": ("qkv_w", "dw_w", 2 * C), "x1": ("w_in", "w_dw", 0), "x2": ("w_in", "w_dw", HID)}
    with_v = names == ("qk",)
    with Phase(nc, "kn") as ph:
        every = names + ("v",) * with_v
        size = {n: C if n == "v" else HID for n in every}
        w1 = {n: ph.sb(f"w1_{n}", [size[n], C2]) for n in every}
        dw = {n: ph.sb(f"dw_{n}", [size[n], 9]) for n in every}
        scaled = {n: p["v_taps"] if n == "v" else ph.sb(f"scaled_{n}", [HID, len(TILES6), C2]) for n in every}
        width = 4 * C2 if "x1" in names else QK_COLS
        rows3 = ph.sb("rows3", [C2, 2, 3, width])
        rows4 = ph.sb("rows4", [C2, 2, 4, width])
        half = ph.sb("half", [C2, 2, width])
        high, low = p["w_hid" if "x1" in names else "w_qk"]
        combined, padded = ph.sem("combined"), ph.sem("padded")
        sums = [ph.ps(f"sum{k}") for k in range(4)]
        loaded, made, multiplied, copied = ph.sem("loaded"), ph.sem("made"), ph.sem("multiplied"), ph.sem("copied")
        block = ph.block()

        @block.sync
        def _(sp):
            for n in every:
                w, d, at = rows[n]
                for pi in range(2):
                    sp.dma_start(w1[n][:, pi * C:(pi + 1) * C], p[w][at:at + size[n]]).then_inc(loaded, 16)
                sp.dma_start(dw[n][:, :], p[d][at:at + size[n]]).then_inc(loaded, 16)

        @block.vector
        def _(dve):
            if not "x1" in names:
                nc.vector.memset(rows3[:, :, :, 2 * HID:], 0.0).then_inc(padded, 1)
                dve.wait_ge(padded, 1)
            dve.wait_ge(loaded, 3 * len(every) * 16)
            for n in every:
                for j, (ab, dh, po) in enumerate(TILES6):
                    for pi in range(2):
                        t = tap_of(ab, dh, pi, po)
                        o = scaled[n][:, j, pi * C:(pi + 1) * C]
                        if t is None:
                            ins = nc.vector.memset(o, 0.0)
                        else:
                            ins = nc.vector.tensor_scalar(o, w1[n][:, pi * C:(pi + 1) * C], dw[n][:, t:t + 1], None, ALU.mult)
                ins.then_inc(made, 1)
            i = 0
            for n in names:
                for ab, dh, po in TILES6:
                    dve.wait_ge(multiplied, i + 1)
                    s = sums[i % 4][0:C2, 0:HID]
                    if n == "qk":
                        ins = nc.vector.tensor_copy(rows3[:, ab, dh, po * HID:(po + 1) * HID], s)
                    else:
                        w3, x = rows3[:, ab, dh], int(n == "x2")
                        if po == 0:
                            ins = nc.vector.tensor_copy(w3[:, 128 * x:128 * x + HID], s)
                        else:
                            nc.vector.tensor_copy(w3[:, 128 * x + HID:128 * x + 128], s[:, 0:32])
                            ins = nc.vector.tensor_copy(w3[:, 256 + 64 * x:256 + 64 * x + 64], s[:, 32:HID])
                    ins.then_inc(copied, 1)
                    i += 1
            dve.wait_ge(copied, i)
            g0, g1, g2 = (rows3[:, :, dh, :] for dh in range(3))
            v = nc.vector
            v.tensor_copy(rows4[:, :, 0, :], g0)
            v.tensor_copy(rows4[:, :, 3, :], g2)
            v.tensor_tensor(half[:, :, :], g0, g2, ALU.add).then_inc(combined, 1)
            dve.wait_ge(combined, 1)
            v.tensor_tensor(rows4[:, :, 1, :], half[:, :, :], g1, ALU.add)
            v.tensor_tensor(rows4[:, :, 2, :], half[:, :, :], g1, ALU.subtract).then_inc(combined, 1)
            dve.wait_ge(combined, 2)
            v.tensor_scalar(rows4[:, :, 1:3, :], rows4[:, :, 1:3, :], 0.5, None, ALU.mult).then_inc(combined, 1)
            dve.wait_ge(combined, 3)
            v.tensor_copy(high[:, :, :, :], rows4[:, :, :, :]).then_inc(combined, 1)
            dve.wait_ge(combined, 4)
            v.tensor_tensor(low[:, :, :, :], rows4[:, :, :, :], high[:, :, :, :], ALU.subtract).then_inc(combined, 1)

        @block.tensor
        def _(pe):
            i = 0
            for j, n in enumerate(names):
                pe.wait_ge(made, j + 1)
                for t in range(len(TILES6)):
                    if i >= 4:
                        pe.wait_ge(copied, i - 3)
                    nc.tensor.matmul(sums[i % 4][0:C2, 0:HID], scaled[n][:, t, :], p["ident"][:, :],
                                     start=True, stop=True).then_inc(multiplied, 1)
                    i += 1


def gram_phase(nc, src, scale, shift, weights, gram):
    with Phase(nc, "qk") as ph:
        NP = STRIP // 2
        rs = RowStream(nc, ph, src, scale, shift, NP)
        W2 = 2 * HID
        four = [[ph.ps(f"four{k}{j}") for j in range(2)] for k in range(3)]
        gsum = ph.ps("gsum")
        rows = [ph.sb(f"rows{k}", [128, 2, W2]) for k in range(3)]
        second = ph.sb("second", [128, 2, W2])
        both = ph.sb("both", [128, 2, W2])
        evacuated, used, folded, mid = (ph.sem(n) for n in ("evacuated", "used", "folded", "mid"))
        block = ph.block()
        NPB = H // 2
        BODY = NPB // 4

        @block.sync
        def _(sp):
            rs.sync(sp, lambda b, hb: rs.wait_normed(sp, b, hb))

        @block.scalar
        def _(act):
            act.wait_ge(rs.cleared, 1)
            with act.Fori(0, B) as b:
                for u in range(NSTRIP):
                    rs.prepare(act, b, u)

        @block.gpsimd
        def _(pool):
            rs.pool_clear(pool)
            with pool.Fori(0, B) as b:
                rs.pool_batch(pool, b)

        @block.tensor
        def _(pe):
            def grams(b, n):
                pe.wait_ge(evacuated, 3 + NPB * b + n + 1)
                if n % BODY == 0:
                    pe.wait_ge(folded, 1 + 4 * b + n // BODY)
                for j in range(4):
                    q = rows[n % 3][:, j // 2, (j % 2) * HID:(j % 2 + 1) * HID]
                    mm = nc.tensor.matmul(gsum[0:HID, 0:HID], q, q, start=(n % BODY == 0 and j == 0),
                                          stop=(n % BODY == BODY - 1 and j == 3))
                mm.then_inc(used, 1)

            with pe.Fori(0, B) as b:
                for n in range(NPB):
                    u, pr = n // NP, n % NP
                    if pr == 0:
                        rs.wait_strip(pe, b, u)
                    pe.wait_ge(evacuated, NPB * b + n + 1)
                    for t in range(4):
                        for j, (px, w, ab) in enumerate(rs.passes(u, *weights)):
                            mm = nc.tensor.matmul(four[n % 3][t // 2][:, (t % 2) * QK_COLS:(t % 2 + 1) * QK_COLS],
                                                  px[:, 4 * t + pr, 1:1 + PAIRS], w[:, ab, t, :],
                                                  start=(j == 0), stop=(j == 5))
                    mm.then_inc(rs.conved, 1)
                    if n >= 1:
                        grams(b, n - 1)
                grams(b, NPB - 1)

        @block.vector
        def _(dve):
            dve.sem_inc(evacuated, 3)
            dve.sem_inc(folded, 1)
            dve.sem_inc(used, 3)
            with dve.Fori(0, B) as b:
                def fold(part):
                    dve.wait_ge(used, 3 + NPB * b + BODY * (part + 1))
                    g = gram[:, bass.ds(b, 1), :].rearrange("p b n -> p (b n)")
                    if part == 0:
                        nc.vector.tensor_copy(g, gsum[0:HID, 0:HID]).then_inc(folded, 1)
                    else:
                        dve.wait_ge(folded, 1 + 4 * b + part)
                        nc.vector.tensor_tensor(g, gsum[0:HID, 0:HID], g, ALU.add).then_inc(folded, 1)

                for n in range(NPB):
                    rs.wait_conved(dve, b, n)
                    m = [four[n % 3][t // 2][:, (t % 2) * QK_COLS:(t % 2) * QK_COLS + W2] for t in range(4)]
                    dve.wait_ge(evacuated, 3 + NPB * b + n)
                    nc.vector.tensor_copy(second[:, 0, :], m[2]).then_inc(mid, 1)
                    dve.wait_ge(mid, 2 * NPB * b + 2 * n + 1)
                    nc.vector.tensor_tensor(both[:, 0, :], m[1], second[:, 0, :], ALU.add)
                    nc.vector.tensor_tensor(both[:, 1, :], m[1], second[:, 0, :], ALU.subtract).then_inc(mid, 1)
                    dve.wait_ge(mid, 2 * NPB * b + 2 * n + 2)
                    dve.wait_ge(used, NPB * b + n + 1)
                    nc.vector.tensor_tensor(rows[n % 3][:, 0, :], both[:, 0, :], m[0], ALU.add)
                    nc.vector.tensor_tensor(rows[n % 3][:, 1, :], both[:, 1, :], m[3], ALU.subtract).then_inc(evacuated, 1)
                    if n % BODY == 1 and n > BODY:
                        fold(n // BODY - 1)
                fold(3)


def attention_phase(nc, p, gram, w_v):
    with Phase(nc, "at") as ph:
        sq, diag, norm, rn = (ph.sb(n, [HID, HID]) if n == "sq" else ph.sb(n, [HID, 1]) for n in ("sq", "diag", "norm", "rn"))
        dk = ph.sb("dk", [HID, C])
        temp = ph.sb("temp", [C, 1])
        logit, prob, attn = (ph.sb(n, [C, C]) for n in ("logit", "prob", "attn"))
        top, total, inv = (ph.sb(n, [C, 1]) for n in ("top", "total", "inv"))
        proj_t, mixed = ph.sb("proj_t", [C, C]), ph.sb("mixed", [C, C])
        pl, pm = ph.ps("pl"), ph.ps("pm")
        pk = [ph.ps(f"pk{k}") for k in range(3)]
        loaded, vec, root, prod, expd = (ph.sem(n) for n in ("loaded", "vec", "root", "prod", "expd"))
        block = ph.block()
        NV = 13
        TILES = len(TILES6)

        @block.sync
        def _(sp):
            sp.dma_start(temp[:, :], p["temperature"].to_broadcast([C, 1])).then_inc(loaded, 16)
            sp.dma_start(proj_t[:, :], p["proj_t"]).then_inc(loaded, 16)

        @block.vector
        def _(dve):
            dve.wait_ge(loaded, 32)
            for b in range(B):
                v = NV * b
                nc.vector.tensor_tensor(sq[:, :], gram[:, b, :], p["ident"][:, :], ALU.mult).then_inc(vec, 1)
                dve.wait_ge(vec, v + 1)
                nc.vector.reduce_sum(diag[:, :], sq[:, :], AX_X).then_inc(vec, 1)
                dve.wait_ge(root, b + 1)
                nc.vector.tensor_scalar(sq[:, 0:1], norm[:, :], L2_EPS, None, ALU.max).then_inc(vec, 1)
                dve.wait_ge(vec, v + 3)
                nc.vector.reciprocal(rn[:, :], sq[:, 0:1]).then_inc(vec, 1)
                dve.wait_ge(vec, v + 4)
                nc.vector.tensor_scalar(dk[:, :], p["ident"][:, C:C2], rn[:, :], None, ALU.mult).then_inc(vec, 1)
                dve.wait_ge(prod, 3 * b + 1)
                nc.vector.tensor_scalar(logit[:, :], pl[0:C, 0:C], rn[0:C, :], temp[:, :], ALU.mult, ALU.mult)\
                  .then_inc(vec, 1)
                dve.wait_ge(vec, v + 6)
                nc.vector.reduce_max(top[:, :], logit[:, :], AX_X).then_inc(vec, 1)
                dve.wait_ge(vec, v + 7)
                nc.vector.tensor_scalar(logit[:, :], logit[:, :], top[:, :], None, ALU.subtract).then_inc(vec, 1)
                dve.wait_ge(expd, b + 1)
                nc.vector.reduce_sum(total[:, :], prob[:, :], AX_X).then_inc(vec, 1)
                dve.wait_ge(vec, v + 9)
                nc.vector.reciprocal(inv[:, :], total[:, :]).then_inc(vec, 1)
                dve.wait_ge(vec, v + 10)
                nc.vector.tensor_scalar(attn[:, :], prob[:, :], inv[:, :], None, ALU.mult).then_inc(vec, 1)
                dve.wait_ge(prod, 3 * b + 2)
                nc.vector.tensor_copy(mixed[:, :], pm[0:C, 0:C]).then_inc(vec, 1)
                dve.wait_ge(prod, 3 * b + 3)
                for j in range(3):
                    ins = nc.vector.tensor_copy(
                        w_v[:, b, 4 * j:4 * j + 4, :], pk[j][0:C2, 0:4 * C].rearrange("p (t n) -> p t n", t=4))
                ins.then_inc(vec, 1)

        @block.scalar
        def _(act):
            for b in range(B):
                act.wait_ge(vec, NV * b + 2)
                nc.scalar.activation(norm[:, :], diag[:, :], ACT.Sqrt).then_inc(root, 1)
                act.wait_ge(vec, NV * b + 8)
                nc.scalar.activation(prob[:, :], logit[:, :], ACT.Exp).then_inc(expd, 1)

        @block.tensor
        def _(pe):
            for b in range(B):
                pe.wait_ge(vec, NV * b + 5)
                nc.tensor.matmul(pl[0:C, 0:C], gram[:, b, 0:C], dk[:, :], start=True, stop=True).then_inc(prod, 1)
                pe.wait_ge(vec, NV * b + 11)
                nc.tensor.matmul(pm[0:C, 0:C], attn[:, :], proj_t[:, :], start=True, stop=True).then_inc(prod, 1)
                pe.wait_ge(vec, NV * b + 12)
                for t in range(TILES):
                    mm = nc.tensor.matmul(pk[t // 4][0:C2, (t % 4) * C:(t % 4 + 1) * C], p["v_taps"][:, t, :],
                                          mixed[:, :], start=True, stop=True)
                mm.then_inc(prod, 1)


def value_phase(nc, src, scale, shift, w_v, dst, stats):
    with Phase(nc, "va") as ph:
        NG = 2
        NGB = NG * NSTRIP
        rs = RowStream(nc, ph, src, scale, shift, NG, plain=True, raws=4)
        w_high, w_low = ph.sb("w_high", [C2, 12, C], F32R), ph.sb("w_low", [C2, 12, C], F32R)
        sums = [ph.ps(f"sum{k}") for k in range(4)]
        stored = [ph.sem(f"stored{k}") for k in range(4)]
        w_set, w_split, measured = ph.sem("w_set"), ph.sem("w_split"), ph.sem("measured")
        added = ph.sem("added")
        block = ph.block()

        @block.sync
        def _(sp):
            def store(b, hb):
                ph.hold(sp, added, 4 + NGB * b + 4 * (hb + 1))
                d = dst[hb][:, :, :, :, bass.ds(b, 1)].rearrange("wb hp wp c b s -> (wp c) (wb hp) (b s)")
                sp.dma_start(d, rs.raw[hb % 4][:, :].rearrange("p (k s) -> p k s", s=SUB)).then_inc(stored[hb % 4], 16)

            def before_load(b, hb):
                if hb >= 2:
                    ph.hold(sp, stored[(hb - 2) % 4], 16 + 64 * b + 16 * ((hb - 2) // 4) + 16)
                    ph.hold(sp, measured, NB + NB * b + hb - 1)
                else:
                    ph.hold(sp, stored[hb + 2], 16 + 64 * b)
                    ph.hold(sp, measured, NB + NB * b + hb - 1)

            def store_before(b, hb):
                if hb >= 1:
                    store(b, hb - 1)

            rs.sync(sp, before_load, lambda b: store(b, NB - 1), store_before)
            for k in range(4):
                sp.wait_ge(stored[k], 16 + 64 * B)

        @block.scalar
        def _(act):
            act.wait_ge(rs.cleared, 1)
            with act.Fori(0, B) as b:
                for u in range(NSTRIP):
                    rs.prepare(act, b, u)

        @block.gpsimd
        def _(pool):
            rs.pool_clear(pool)
            with pool.Fori(0, B) as b:
                rs.pool_batch(pool, b)

        @block.tensor
        def _(pe):
            with pe.Fori(0, B) as b:
                pe.wait_ge(w_set, b + 1)
                for g in range(NGB):
                    u, hp = g // NG, g % NG
                    if hp == 0:
                        rs.wait_high(pe, b, u)
                    pe.wait_ge(added, NGB * b + g + 1)
                    n = 0
                    for i, (px, w, ab) in enumerate(rs.passes(u, w_high, w_low)):
                        if hp == 0 and i == 4:
                            rs.wait_low(pe, b, u)
                        for dh in range(3):
                            mm = nc.tensor.matmul(sums[g % 4][0:C2, :],
                                                  w[:, ab * 6 + dh * 2:ab * 6 + dh * 2 + 2, :].rearrange("p t n -> p (t n)"),
                                                  px[:, dh + hp:dh + hp + STRIP - 1:2, 1:1 + PAIRS],
                                                  start=(n == 0), stop=(n == 17))
                            n += 1
                    mm.then_inc(rs.conved, 1)

        @block.vector
        def _(dve):
            dve.sem_inc(added, 4)
            dve.sem_inc(measured, NB)
            for k in range(4):
                dve.sem_inc(stored[k], 16)
            with dve.Fori(0, B) as b:
                w = w_v[:, bass.ds(b, 1), :, :].rearrange("p b t n -> p (b t) n")
                nc.vector.tensor_copy(w_high[:, :, :], w).then_inc(w_split, 1)
                dve.wait_ge(w_split, b + 1)
                nc.vector.tensor_tensor(w_low[:, :, :], w, w_high[:, :, :], ALU.subtract).then_inc(w_set, 1)
                for hb in range(NB):
                    raw = rs.raw[hb % 4][:, :].rearrange("p (k q i j) -> p k q i j", k=NB, q=2, i=HALF)
                    dve.wait_ge(rs.normed, NB * b + hb + 1)
                    for e in range(2):
                        for hp in range(2):
                            g = 4 * hb + 2 * e + hp
                            rs.wait_conved(dve, b, g)
                            v = raw[:, :, hp, 4 * e:4 * e + 4].rearrange("p k i j -> p i k j")
                            nc.vector.tensor_tensor(v, sums[g % 4][0:C2, :].rearrange("p (i k j) -> p i k j", i=4, j=HALF),
                                                    v, ALU.add).then_inc(added, 1)
                    dve.wait_ge(added, 4 + NGB * b + 4 * (hb + 1))
                    for part in range(4):
                        last = nc.vector.bn_stats(
                            stats[:, bass.ds(b, 1), hb * 4 + part, :].rearrange("p b s -> p (b s)"),
                            rs.raw[hb % 4][:, part * 512:(part + 1) * 512])
                    last.then_inc(measured, 1)


def gated_phase(nc, p, src, scale, shift, mixed):
    with Phase(nc, "gf") as ph:
        NH = 2 * NSTRIP
        NC = 2 * C
        G = W // 32
        TILES = (2, 0, 1)
        HN = 2 * PAIRS
        rs = RowStream(nc, ph, src, scale, shift, 2 * len(TILES))
        four = [[ph.ps(f"four{t}{j}") for j in range(2)] for t in range(3)]
        px_sum = [ph.ps(f"px_sum{j}") for j in range(2)]
        second = ph.sb("second", [128, HN])
        both = ph.sb("both", [128, 2, HN])
        x_a = [ph.sb(f"x_a{k}", [128, 2, HN]) for k in range(2)]
        x_b = ph.sb("x_b", [128, 2, HN])
        x_c = [ph.sb(f"x_c{k}", [128, 2, HN]) for k in range(2)]
        gelu_c = [ph.sb(f"gelu_c{k}", [128, 2, HN]) for k in range(2)]
        hid_a = [ph.sb(f"hid_a{k}", [128, G, 128]) for k in range(2)]
        hid_c = [ph.sb(f"hid_c{k}", [128, G, 128]) for k in range(2)]
        w_out = ph.sb("w_out", [128, 2, NC])
        stage = [ph.sb(f"stage{k}", [128, NC, G * QS]) for k in range(2)]
        taken, gelued, gated, mid = ph.sem("taken"), ph.sem("gelued"), ph.sem("gated"), ph.sem("mid")
        projected, moved = ph.sem("projected"), ph.sem("moved")
        w_in, zeroed = ph.sem("w_in"), ph.sem("zeroed")
        stored = [ph.sem(f"stored{k}") for k in range(2)]
        block = ph.block()

        @block.sync
        def _(sp):
            sp.dma_start(w_out[:, :, :], p["w_out"]).then_inc(w_in, 16)
            def store(b, q):
                ph.hold(sp, moved, 2 + 2 * NSTRIP * b + 2 * QS * (q + 1))
                sp.dma_start(mixed[:, :, bass.ds(QB * b + q, 1), :].rearrange("p m q n -> p m (q n)"),
                             stage[q % 2][:, :, :]).then_inc(stored[q % 2], 16)

            def before_load(b, hb):
                rs.wait_normed(sp, b, hb)
                if hb >= 4 and hb % 2 == 0:
                    store(b, hb // 2 - 2)

            def last_stores(b):
                store(b, QB - 2)
                store(b, QB - 1)

            rs.sync(sp, before_load, last_stores)
            for k in range(2):
                sp.wait_ge(stored[k], 16 + 16 * QB * B // 2)

        @block.gpsimd
        def _(pool):
            rs.pool_clear(pool)
            with pool.Fori(0, B) as b:
                rs.pool_batch(pool, b)

        @block.tensor
        def _(pe):
            def project(b, s):
                pe.wait_ge(gated, 2 + NH * b + 2 * s + 2)
                for j in range(2):
                    pe.wait_ge(moved, 2 * NSTRIP * b + 2 * s + j + 1)
                    for g in range(4):
                        o = px_sum[j][:, g * NC:(g + 1) * NC]
                        nc.tensor.matmul(o, hid_a[s % 2][:, 4 * j + g, :], w_out[:, 0, :], start=True, stop=False)
                        mm = nc.tensor.matmul(o, hid_c[s % 2][:, 4 * j + g, :], w_out[:, 1, :], start=False, stop=True)
                    mm.then_inc(projected, 1)

            pe.wait_ge(w_in, 16)
            pe.wait_ge(zeroed, 2)
            with pe.Fori(0, B) as b:
                for h in range(NH):
                    u, j = h // 2, h % 2
                    if j == 0:
                        rs.wait_strip(pe, b, u)
                    for n, tile in enumerate(TILES):
                        pe.wait_ge(taken, 3 * NH * b + 3 * h + n + 1)
                        for t in range(4):
                            for i, (px, w, ab) in enumerate(rs.passes(u, *p["w_hid"])):
                                mm = nc.tensor.matmul(four[tile][t // 2][:, (t % 2) * HN:(t % 2 + 1) * HN],
                                                      w[:, ab, t, 128 * tile:128 * tile + 128],
                                                      px[:, 4 * t + 2 * j:4 * t + 2 * j + 2, 1:1 + PAIRS],
                                                      start=(i == 0), stop=(i == 5))
                        mm.then_inc(rs.conved, 1)
                    if j == 0 and u:
                        project(b, u - 1)
                project(b, NSTRIP - 1)

        @block.scalar
        def _(act):
            act.wait_ge(rs.cleared, 1)
            def batch(b, last):
                for h in range(NH):
                    act.wait_ge(taken, 3 + 3 * NH * b + 3 * h + 1)
                    nc.scalar.activation(gelu_c[h % 2][64:128, :, :], x_c[h % 2][0:64, :, :], ACT.Gelu).then_inc(gelued, 1)
                    act.wait_ge(taken, 3 + 3 * NH * b + 3 * h + 2)
                    nc.scalar.activation(x_a[h % 2][:, :, :], x_a[h % 2][:, :, :], ACT.Gelu).then_inc(gelued, 1)
                    if h % 2 == 1:
                        u = h // 2 + SLOTS
                        if u < NSTRIP:
                            rs.prepare(act, b, u)
                        elif not last:
                            rs.prepare(act, b + 1, u - NSTRIP)

            for u in range(SLOTS):
                rs.prepare(act, 0, u)
            with act.Fori(0, B - 1) as b:
                batch(b, False)
            batch(B - 1, True)

        @block.vector
        def _(dve):
            def move(b, s):
                q, sq = s // QS, s % QS
                if sq == 0:
                    dve.wait_ge(stored[q % 2], 16 * (QB // 2 * b + q // 2 + 1))
                out = stage[q % 2][:, :, :].rearrange("p m (g s) -> p g m s", s=QS)
                for j in range(2):
                    dve.wait_ge(projected, 4 + 2 * NSTRIP * b + 2 * s + j + 1)
                    nc.vector.tensor_copy(out[:, 4 * j:4 * j + 4, :, sq],
                                          px_sum[j][:, 0:4 * NC].rearrange("p (g m) -> p g m", g=4)).then_inc(moved, 1)

            for k in range(2):
                nc.vector.memset(hid_c[k][0:64, :, :], 0.0).then_inc(zeroed, 1)
            dve.sem_inc(taken, 3)
            dve.sem_inc(gated, 2)
            dve.sem_inc(projected, 4)
            dve.sem_inc(moved, 2)
            for k in range(2):
                dve.sem_inc(stored[k], 16)
            with dve.Fori(0, B) as b:
                for h in range(NH):
                    k, u, j = h % 2, h // 2, h % 2
                    for n, tile in enumerate(TILES):
                        out = {0: x_a[k], 1: x_b, 2: x_c[k]}[tile]
                        v = 3 * NH * b + 3 * h + n
                        m = [four[tile][t // 2][:, (t % 2) * HN:(t % 2 + 1) * HN] for t in range(4)]
                        rs.wait_conved(dve, b, 3 * h + n)
                        dve.wait_ge(taken, 3 + v)
                        nc.vector.tensor_copy(second[:, :], m[2]).then_inc(mid, 1)
                        dve.wait_ge(mid, 2 * v + 1)
                        nc.vector.tensor_tensor(both[:, 0, :], m[1], second[:, :], ALU.add)
                        nc.vector.tensor_tensor(both[:, 1, :], m[1], second[:, :], ALU.subtract).then_inc(mid, 1)
                        dve.wait_ge(mid, 2 * v + 2)
                        dve.wait_ge(gated, NH * b + h + (2 if tile == 1 else 1))
                        nc.vector.tensor_tensor(out[:, 0, :], both[:, 0, :], m[0], ALU.add)
                        nc.vector.tensor_tensor(out[:, 1, :], both[:, 1, :], m[3], ALU.subtract).then_inc(taken, 1)
                    dve.wait_ge(projected, 2 * NSTRIP * b + 2 * u + 2)

                    def hid(t, lo, hp):
                        w = t[u % 2][lo:128, :, :].rearrange("p g (w h x) -> p (g w) h x", w=2, h=2)[:, :, hp]
                        return w.rearrange("p a (i j) -> p i a j", j=HALF)[:, 2 * j:2 * j + 2]

                    def px(t, lo, hp):
                        return t[lo:128, hp, :].rearrange("p (i a j) -> p i a j", i=2, j=HALF)

                    dve.wait_ge(gelued, 2 * NH * b + 2 * h + 2)
                    dve.wait_ge(taken, 3 + 3 * NH * b + 3 * h + 3)
                    for hp in range(2):
                        nc.vector.tensor_tensor(hid(hid_c, 64, hp), px(gelu_c[k], 64, hp), px(x_c[k], 64, hp), ALU.mult)
                        last = nc.vector.tensor_tensor(hid(hid_a, 0, hp), px(x_a[k], 0, hp), px(x_b, 0, hp), ALU.mult)
                    last.then_inc(gated, 1)
                    if j == 0 and u:
                        move(b, u - 1)
                move(b, NSTRIP - 1)


QS = 4
QB = NSTRIP // QS



FREQ = 8 * 5


def filter_phase(nc, p, mixed, patches, out):
    with Phase(nc, "fi") as ph:
        N = B * H // 8 * W // 32
        y = [ph.sb(f"y{k}", [128, 2, N]) for k in range(2)]
        res = [ph.sb(f"res{k}", [128, 2, N]) for k in range(2)]
        o = [ph.sb(f"o{k}", [128, 2, N]) for k in range(2)]
        wave_in = ph.sb("wave_in", [2 * FREQ, 256])
        wave_out = ph.sb("wave_out", [2 * FREQ, 256])
        same = ph.sb("same", [128, 512])
        fw = ph.sb("fw", [2 * FREQ, C])
        scaled = [ph.sb(f"scaled{k}", [2 * FREQ, 256]) for k in range(2)]
        mat = [ph.sb(f"mat{k}", [128, 512]) for k in range(2)]
        pmat = [ph.ps(f"pmat{k}") for k in range(2)]
        sums = [ph.ps(f"sum{k}") for k in range(4)]
        consts = ph.sem("consts")
        y_in = [ph.sem(f"y_in{k}") for k in range(2)]
        res_in = [ph.sem(f"res_in{k}") for k in range(2)]
        weighted, built, masked = ph.sem("weighted"), ph.sem("built"), ph.sem("masked")
        filtered, added = ph.sem("filtered"), ph.sem("added")
        stored = [ph.sem(f"stored{k}") for k in range(2)]
        block = ph.block()
        QN = 4

        @block.sync
        def _(sp):
            def load(c, k):
                src = mixed.rearrange("p (q c) n s -> p q c (n s)", q=2)
                sp.dma_start(y[k][:, :, :], src[:, :, bass.ds(c, 1), :].rearrange("p q c n -> p (q c) n")).then_inc(y_in[k], 16)
                r = patches[bass.ds(c, 1)].rearrange("c w h x q g n -> (c w h x) q (g n)")
                sp.dma_start(res[k][:, :, :], r).then_inc(res_in[k], 16)

            def store(c, k):
                ph.hold(sp, added, 4 + QN * (c + 1))
                sp.dma_start(out[bass.ds(c, 1)].rearrange("c p q n -> (c p) q n"), o[k][:, :, :]).then_inc(stored[k], 16)

            for d, s in ((wave_in[:, :], p["wave_in"]), (wave_out[:, :], p["wave_out"]), (same[:, :], p["same_patch"]),
                         (fw[0:FREQ, :], p["fft_w"]), (fw[FREQ:2 * FREQ, :], p["fft_w"])):
                sp.dma_start(d, s).then_inc(consts, 16)
            load(0, 0)
            load(1, 1)
            with sp.Fori(0, C // 2 - 1) as i:
                for k in range(2):
                    store(2 * i + k, k)
                    load(2 * i + k + 2, k)
            store(C - 2, 0)
            store(C - 1, 1)
            for k in range(2):
                sp.wait_ge(stored[k], 16 + 16 * (C // 2))

        @block.scalar
        def _(act):
            act.wait_ge(consts, 80)
            act.sem_inc(built, 2)
            with act.Fori(0, C // 2) as i:
                for k in range(2):
                    c = 2 * i + k
                    act.wait_ge(built, c + 1)
                    nc.scalar.activation(scaled[k][:, :], wave_in[:, :], ACT.Copy, scale=fw[:, bass.ds(c, 1)])\
                      .then_inc(weighted, 1)

        @block.tensor
        def _(pe):
            def build(c, k):
                pe.wait_ge(weighted, c + 1)
                pe.wait_ge(masked, c + 1)
                for po in range(2):
                    mm = nc.tensor.matmul(pmat[k][:, po * 256:(po + 1) * 256], scaled[k][:, po * 128:(po + 1) * 128],
                                          wave_out[:, :], start=True, stop=True)
                mm.then_inc(built, 1)

            def filt(i, k):
                c = 2 * i + k
                pe.wait_ge(masked, 2 + c + 1)
                pe.wait_ge(y_in[k], 16 * i + 16)
                for n in range(QN):
                    po_out, half = n // 2, n % 2
                    pe.wait_ge(added, QN * c + n + 1)
                    for po in range(2):
                        lhs = mat[k][:, po * 256 + po_out * 128:po * 256 + po_out * 128 + 128]
                        mm = nc.tensor.matmul(sums[n][:, :], lhs, y[k][:, po, half * 512:half * 512 + 512],
                                              start=(po == 0), stop=(po == 1))
                    mm.then_inc(filtered, 1)

            pe.wait_ge(consts, 80)
            build(0, 0)
            with pe.Fori(0, C // 2 - 1) as i:
                build(2 * i + 1, 1)
                filt(i, 0)
                build(2 * i + 2, 0)
                filt(i, 1)
            build(C - 1, 1)
            filt(C // 2 - 1, 0)
            filt(C // 2 - 1, 1)

        @block.vector
        def _(dve):
            def mask(c, k):
                dve.wait_ge(built, 2 + c + 1)
                dve.wait_ge(filtered, QN * c + QN)
                nc.vector.tensor_tensor(mat[k][:, :], pmat[k][:, :], same[:, :], ALU.mult).then_inc(masked, 1)

            def add(i, k):
                c = 2 * i + k
                dve.wait_ge(res_in[k], 16 * i + 16)
                dve.wait_ge(stored[k], 16 * i + 16)
                for n in range(QN):
                    po, half = n // 2, n % 2
                    dve.wait_ge(filtered, 2 * QN + QN * c + n + 1)
                    for bb in range(2):
                        b = 2 * half + bb
                        r = res[k][:, po, :].rearrange("p (g b q s) -> p b q g s", g=W // 32, b=B, q=QB)[:, b]
                        z = sums[n][:, bb * 256:bb * 256 + 256].rearrange("p (q g s) -> p q g s", q=QB, g=W // 32)
                        d = o[k][:, po, b * 256:b * 256 + 256].rearrange("p (q g s) -> p q g s", q=QB, g=W // 32)
                        ins = nc.vector.tensor_tensor(d, z, r, ALU.add)
                    ins.then_inc(added, 1)

            dve.sem_inc(masked, 2)
            dve.sem_inc(filtered, 2 * QN)
            dve.sem_inc(added, 4)
            for k in range(2):
                dve.sem_inc(stored[k], 16)
            dve.wait_ge(consts, 80)
            mask(0, 0)
            with dve.Fori(0, C // 2 - 1) as i:
                mask(2 * i + 1, 1)
                add(i, 0)
                mask(2 * i + 2, 0)
                add(i, 1)
            mask(C - 1, 1)
            add(C // 2 - 1, 0)
            add(C // 2 - 1, 1)




def build(nc, p, out):
    dram = {n: nc.dram_tensor(n, [NB, NB, 2, 2, C, B, SUB], F32).ap() for n in ("x1", "x2", "up", "x3")}
    down = nc.dram_tensor("down", [C2, H + 2, B, PAIRS], F32).ap()
    right = nc.dram_tensor("right", [C2, W, B, PAIRS], F32).ap()
    mixed = nc.dram_tensor("mixed", [128, C2, QB * B, W // 32 * QS], F32).ap()
    patches = nc.dram_tensor("patches", [C, 2, 2, 32, 2, W // 32, B * H // 8], F32).ap()
    with Phase(nc, "all") as ph:
        ident, group_avg = ph.sb("ident", [HID, HID]), ph.sb("group_avg", [C2, C2])
        stats = ph.sb("stats", [C2, B, NSTAT, 6])
        scale, shift = ph.sb("scale", [C2, B]), ph.sb("shift", [C2, B])
        p["ident_dram"], p["ident"] = p["ident"], ident
        consts_phase(nc, ((ident, p["ident_dram"]), (group_avg, p["group_avg"])))

        with Phase(nc, "l0") as l0:
            p["w_qk"] = [l0.sb(f"w_qk_{q}", [C2, 2, 4, QK_COLS], F32R) for q in ("high", "low")]
            p["v_taps"] = l0.sb("v_taps", [C, len(TILES6), C2])
            gram = l0.sb("gram", [HID, B, HID])
            w_v = l0.sb("w_v", [C2, B, len(TILES6), C])
            kernels_phase(nc, p, ("qk",))
            stats_phase(nc, p["x"], stats)
            norm_phase(nc, stats, group_avg, scale, shift)
            gram_phase(nc, p["x"], scale, shift, p["w_qk"], gram)
            attention_phase(nc, p, gram, w_v)
            value_phase(nc, p["x"], scale, shift, w_v, dram["x1"], stats)

        for layer, src, dst in ((1, dram["x1"], dram["x2"]), (2, dram["x2"], dram["x3"])):
            norm_phase(nc, stats, group_avg, scale, shift)
            t = {n: p[f"{n}_taps{layer}"] for n in ("down", "right", "left")}
            forward_sweep(nc, "dn", src, "h", t["down"], down, norm=(scale, shift))
            backward_sweep(nc, "up", down, "h", t["down"], dram["up"])
            forward_sweep(nc, "rt", dram["up"], "w", t["right"], right)
            backward_sweep(nc, "lt", right, "w", t["left"], dst, residual=src, stats=stats,
                           patches=patches if layer == 2 else None)

        norm_phase(nc, stats, group_avg, scale, shift)
        with Phase(nc, "l3") as l3:
            p["w_hid"] = [l3.sb(f"w_hid_{q}", [C2, 2, 4, 4 * C2], F32R) for q in ("high", "low")]
            kernels_phase(nc, p, ("x1", "x2"))
            gated_phase(nc, p, dram["x3"], scale, shift, mixed)
        filter_phase(nc, p, mixed, patches, out)


def consts_phase(nc, pairs):
    with Phase(nc, "cs") as ph:
        loaded = ph.sem("loaded")
        block = ph.block()

        @block.sync
        def _(sp):
            for d, s in pairs:
                sp.dma_start(d[:, :], s).then_inc(loaded, 16)
            sp.wait_ge(loaded, 16 * len(pairs))




def sweep_taps(w, bias):
    t = np.zeros((C2 + 1, 3, C2), np.float32)
    for s in range(3):
        for pi in range(2):
            for po in range(2):
                k = 2 * (s - 1) + pi - po + 2
                if 0 <= k < 5:
                    t[pi * C:(pi + 1) * C, s, po * C:(po + 1) * C] = w[:, :, k].T
    for po in range(2):
        t[C2, 1, po * C:(po + 1) * C] = bias
    return t


def waves():
    m = np.arange(128)
    hp, hi, wi = m // 32 % 2, m // 8 % 4, m % 8
    row, patch = 2 * hi + hp, (m // 64) * 2 + wi // 4
    win, wout = np.zeros((2 * FREQ, 256)), np.zeros((2 * FREQ, 256))
    for po in range(2):
        col = 2 * (wi % 4) + po
        for f in range(FREQ):
            ky, kx = f // 5, f % 5
            coef = (1 if kx in (0, 4) else 2) / 64
            phase = 2 * np.pi * ((ky * row + kx * col) % 8) / 8
            s = slice(po * 128, po * 128 + 128)
            win[f, s], win[FREQ + f, s] = coef * np.cos(phase), coef * np.sin(phase)
            wout[f, s], wout[FREQ + f, s] = np.cos(phase), np.sin(phase)
    same = (patch[:, None] == patch[None, :]).astype(np.float32)
    return win.astype(np.float32), wout.astype(np.float32), np.tile(same, (1, 4))


def kernel(**inputs):
    import concourse.bacc as bacc
    from concourse.bass_utils import run_bass_kernel_spmd

    g = {k: np.asarray(v) for k, v in inputs.items()}
    a = {}
    x = g["x"].reshape(B, C, NB, HALF, 2, NB, HALF, 2)
    a["x"] = x.transpose(2, 5, 4, 7, 1, 0, 3, 6).reshape(NB, NB, 2, 2, C, B, SUB)
    a["qkv_w"] = g["L0_conv_qkv_w"].reshape(3 * C, C)
    a["dw_w"] = g["L0_conv_dw_w"].reshape(3 * C, 9)
    a["proj_t"] = g["L0_conv_proj_w"].reshape(C, C).T
    a["temperature"] = g["L0_conv_temperature"].reshape(1, 1)
    for layer in (1, 2):
        for n in ("down", "right", "left"):
            a[f"{n}_taps{layer}"] = sweep_taps(g[f"L{layer}_conv_{n}_w"], g[f"L{layer}_conv_{n}_b"])
    a["w_in"] = g["L3_conv_w_in"]
    a["w_dw"] = g["L3_conv_w_dw"].reshape(2 * HID, 9)
    w = np.zeros((2 * HID, 2 * C), np.float32)
    for po in range(2):
        w[po * HID:(po + 1) * HID, po * C:(po + 1) * C] = g["L3_conv_w_out"].T
    w_out = np.zeros((128, 2, 2 * C), np.float32)
    w_out[:, 0] = w[0:128]
    w_out[64:128, 1] = w[128:192]
    a["w_out"] = w_out
    a["fft_w"] = g["L3_conv_fft_w"].reshape(C, FREQ).T
    a["wave_in"], a["wave_out"], a["same_patch"] = waves()
    a["ident"] = np.eye(HID, dtype=np.float32)
    group = np.arange(C2) % C // (C // GROUPS)
    a["group_avg"] = ((group[:, None] == group[None, :]) / (2 * C // GROUPS)).astype(np.float32)
    a = {k: np.ascontiguousarray(v) for k, v in a.items()}

    nc = bacc.Bacc("TRN2", target_bir_lowering=False, num_devices=1)
    nc.disable_value_cache = True
    p = {k: nc.dram_tensor(f"in_{k}", v.shape, F32, kind="ExternalInput").ap() for k, v in a.items()}
    out = nc.dram_tensor("out", (C, 128, 2, B * H // 8 * W // 32), F32, kind="ExternalOutput").ap()
    build(nc, p, out)
    r = run_bass_kernel_spmd(nc, [{f"in_{k}": v for k, v in a.items()}], core_ids=[0])
    y = r.results[0]["out"].reshape(C, 2, 2, 4, 2, 4, 2, B, QB, W // 32, QS)
    return y.transpose(7, 0, 8, 10, 3, 2, 9, 1, 4, 5, 6).reshape(B, C, H, W)
```
